# Optimizing a Trainium2 kernel written in Bass

```python
import numpy as np
import jax
import jax.numpy as jnp

def _softmax(x, axis=-1):
    return jax.nn.softmax(x, axis=axis)

def _gelu(x):
    return jax.nn.gelu(x, approximate=True)

def _silu(x):
    return jax.nn.silu(x)

def _sigmoid(x):
    return jax.nn.sigmoid(x)

def _layernorm(x, axis=-1, eps=1e-05):
    m = jnp.mean(x, axis=axis, keepdims=True)
    v = jnp.var(x, axis=axis, keepdims=True)
    return (x - m) / jnp.sqrt(v + eps)

def _scatter_add(tgt, idx, src, axis=0):
    return tgt.at[idx].add(src)

def _segment_sum(src, seg, n):
    return jax.ops.segment_sum(src, seg, n)
kernel_name = 'mk_lm_tower_d2_tok_ids1024_r4_61df0d'

def setup_inputs(seed: int=0):
    np.random.seed(seed)
    _w = jnp.asarray

    def _rec_inputs():
        import jax
        import jax.numpy as jnp
        _rk = jax.random.key(seed)
        x = jax.random.randint(jax.random.fold_in(_rk, 1), (8, 512), 0, 31993, jnp.int32)
        return x
    x = _rec_inputs()

    def _L0_tok_setup():
        import jax, jax.numpy as jnp
        import numpy as np
        VOCAB, D, H = (8000, 256, 16)
        DH = D // H
        DFF = 4 * D
        EPS = 1e-05

        def layer_norm(x, g, b):
            mu = jnp.mean(x, axis=-1, keepdims=True)
            var = jnp.var(x, axis=-1, keepdims=True)
            return (x - mu) * jax.lax.rsqrt(var + EPS) * g + b

        def pos_enc(seq_len, d_model):
            pos = jnp.arange(seq_len, dtype=jnp.float32)[:, None]
            i_even = jnp.arange(0, d_model, 2, dtype=jnp.float32)[None, :]
            angle = pos / jnp.power(10000.0, 2.0 * i_even / d_model)
            pe = jnp.zeros((seq_len, d_model), dtype=jnp.float32)
            pe = pe.at[:, 0::2].set(jnp.sin(angle))
            pe = pe.at[:, 1::2].set(jnp.cos(angle))
            return pe
        key = jax.random.key(seed)
        ks = jax.random.split(key, 16)
        s = 0.02
        return {'tokens': jax.random.randint(ks[0], (4, 512), 0, VOCAB), 'emb': jax.random.normal(ks[1], (VOCAB, D), jnp.float32) * s, 'in_proj_w': jax.random.normal(ks[2], (3 * D, D), jnp.float32) * s, 'in_proj_b': jnp.zeros((3 * D,), jnp.float32), 'out_proj_w': jax.random.normal(ks[3], (D, D), jnp.float32) * s, 'out_proj_b': jnp.zeros((D,), jnp.float32), 'w1': jax.random.normal(ks[4], (DFF, D), jnp.float32) * s, 'b1': jnp.zeros((DFF,), jnp.float32), 'w2': jax.random.normal(ks[5], (D, DFF), jnp.float32) * s, 'b2': jnp.zeros((D,), jnp.float32), 'g1': jnp.ones((D,), jnp.float32), 'beta1': jnp.zeros((D,), jnp.float32), 'g2': jnp.ones((D,), jnp.float32), 'beta2': jnp.zeros((D,), jnp.float32)}
    _L0_tok_all = _L0_tok_setup()
    _L0_tok_in = {k: v for k, v in _L0_tok_all.items() if k in ('emb', 'in_proj_w', 'in_proj_b', 'out_proj_w', 'out_proj_b', 'w1', 'b1', 'w2', 'b2', 'g1', 'beta1', 'g2', 'beta2')}
    del _L0_tok_all

    def _L0_attn_setup():
        import jax, jax.numpy as jnp
        import numpy as np
        import math
        D_MODEL = 256
        LAYER_ID = 6
        NUM_LAYERS = 12
        B = 8
        T = 512

        def _wkv(w, u, k, v):
            wn = -jnp.exp(w)

            def step(carry, kv):
                aa, bb, pp = carry
                kt, vt = kv
                ww = u + kt
                p = jnp.maximum(pp, ww)
                e1 = jnp.exp(pp - p)
                e2 = jnp.exp(ww - p)
                y = (e1 * aa + e2 * vt) / (e1 * bb + e2)
                ww2 = pp + wn
                p2 = jnp.maximum(ww2, kt)
                e1b = jnp.exp(ww2 - p2)
                e2b = jnp.exp(kt - p2)
                return ((e1b * aa + e2b * vt, e1b * bb + e2b, p2), y)
            Bd, Td, Cd = k.shape
            init = (jnp.zeros((Bd, Cd), k.dtype), jnp.zeros((Bd, Cd), k.dtype), jnp.full((Bd, Cd), -1e+38, k.dtype))
            kT = jnp.swapaxes(k, 0, 1)
            vT = jnp.swapaxes(v, 0, 1)
            _, ys = jax.lax.scan(step, init, (kT, vT))
            return jnp.swapaxes(ys, 0, 1)
        key = jax.random.key(seed)
        ks = jax.random.split(key, 5)
        r01 = LAYER_ID / (NUM_LAYERS - 1)
        r1a0 = 1.0 - LAYER_ID / NUM_LAYERS
        h = np.arange(D_MODEL, dtype=np.float32)
        w = (-5.0 + 8.0 * (h / (D_MODEL - 1)) ** (0.7 + 1.3 * r01)).astype(np.float32)
        zigzag = np.array([(i + 1) % 3 - 1 for i in range(D_MODEL)], np.float32) * 0.5
        u = (np.ones(D_MODEL, np.float32) * math.log(0.3) + zigzag).astype(np.float32)
        xinit = (h / D_MODEL).astype(np.float32)
        tmk = (xinit ** r1a0).reshape(1, 1, D_MODEL).astype(np.float32)
        tmv = (tmk + 0.3 * r01).astype(np.float32)
        tmr = (xinit ** (0.5 * r1a0)).reshape(1, 1, D_MODEL).astype(np.float32)
        s = 1.0 / math.sqrt(D_MODEL)
        Wk = jax.random.normal(ks[0], (D_MODEL, D_MODEL), jnp.float32) * s
        Wv = jax.random.normal(ks[1], (D_MODEL, D_MODEL), jnp.float32) * s
        Wr = jax.random.normal(ks[2], (D_MODEL, D_MODEL), jnp.float32) * s
        Wo = jax.random.normal(ks[3], (D_MODEL, D_MODEL), jnp.float32) * s
        x = jax.random.normal(ks[4], (B, T, D_MODEL), jnp.float32)
        return dict(x=x, w=jnp.asarray(w), u=jnp.asarray(u), time_mix_k=jnp.asarray(tmk), time_mix_v=jnpp if False else jnp.asarray(tmv), time_mix_r=jnp.asarray(tmr), Wk=Wk, Wv=Wv, Wr=Wr, Wo=Wo)
    _L0_attn_all = _L0_attn_setup()
    _L0_attn_in = {k: v for k, v in _L0_attn_all.items() if k in ('w', 'u', 'time_mix_k', 'time_mix_v', 'time_mix_r', 'Wk', 'Wv', 'Wr', 'Wo')}
    del _L0_attn_all

    def _L0_ffn_setup():
        import jax, jax.numpy as jnp
        import numpy as np
        B, S, H = (1, 512, 256)
        E, K = (16, 4)
        G, TG = (4, 2)
        I_MOE = 128
        N_SH = 2
        SCALE = 2.5

        def _mlp(x, gw, uw, dw):
            return jax.nn.silu(x @ gw.T) * (x @ uw.T) @ dw.T

        def _route(x2d, router_weight, e_bias):
            T = x2d.shape[0]
            scores = jax.nn.sigmoid(x2d @ router_weight.T)
            sc = scores + e_bias[None, :]
            group_scores = jnp.sum(jax.lax.top_k(sc.reshape(T, G, E // G), 2)[0], axis=-1)
            _, gidx = jax.lax.top_k(group_scores, TG)
            gmask = jnp.zeros((T, G), sc.dtype).at[jnp.arange(T)[:, None], gidx].set(1.0)
            smask = jnp.repeat(gmask, E // G, axis=1)
            masked = jnp.where(smask > 0, sc, 0.0)
            _, tidx = jax.lax.top_k(masked, K)
            tw = jnp.take_along_axis(scores, tidx, axis=1)
            tw = tw / (jnp.sum(tw, axis=-1, keepdims=True) + 1e-20)
            tw = tw * SCALE
            return (tidx, tw)

        def _moe_forward(hidden_states, router_weight, e_bias, gate_w, up_w, down_w, sh_gate_w, sh_up_w, sh_down_w):
            orig_shape = hidden_states.shape
            x = hidden_states.reshape(-1, H)
            T = x.shape[0]
            tidx, tw = _route(x, router_weight, e_bias)
            g = jnp.einsum('th,eih->tei', x, gate_w)
            u = jnp.einsum('th,eih->tei', x, up_w)
            h = jax.nn.silu(g) * u
            yo = jnp.einsum('tei,ehi->teh', h, down_w)
            combine = jnp.zeros((T, E), tw.dtype).at[jnp.arange(T)[:, None], tidx].add(tw)
            routed = jnp.einsum('te,teh->th', combine, yo)
            shared = _mlp(hidden_states.reshape(-1, H), sh_gate_w, sh_up_w, sh_down_w)
            return (routed + shared).reshape(orig_shape)
        key = jax.random.key(seed)
        ks = jax.random.split(key, 9)
        s = 0.02
        return {'hidden_states': jax.random.normal(ks[0], (B, S, H), jnp.float32), 'router_weight': jax.random.normal(ks[1], (E, H), jnp.float32) * s, 'e_bias': jnp.zeros((E,), jnp.float32), 'gate_w': jax.random.normal(ks[2], (E, I_MOE, H), jnp.float32) * s, 'up_w': jax.random.normal(ks[3], (E, I_MOE, H), jnp.float32) * s, 'down_w': jax.random.normal(ks[4], (E, H, I_MOE), jnp.float32) * s, 'sh_gate_w': jax.random.normal(ks[5], (N_SH * I_MOE, H), jnp.float32) * s, 'sh_up_w': jax.random.normal(ks[6], (N_SH * I_MOE, H), jnp.float32) * s, 'sh_down_w': jax.random.normal(ks[7], (H, N_SH * I_MOE), jnp.float32) * s}
    _L0_ffn_all = _L0_ffn_setup()
    _L0_ffn_in = {k: v for k, v in _L0_ffn_all.items() if k in ('router_weight', 'e_bias', 'gate_w', 'up_w', 'down_w', 'sh_gate_w', 'sh_up_w', 'sh_down_w')}
    del _L0_ffn_all

    def _L1_attn_setup():
        import jax, jax.numpy as jnp
        import numpy as np
        DIM = 256
        HEADS = 16
        DHEAD = DIM // HEADS
        EPS_NORM = 1e-06
        EPS_DEN = 1e-06

        def rmsnorm(x, w):
            xf = x.astype(jnp.float32)
            return (w * xf * jax.lax.rsqrt(jnp.mean(xf * xf, axis=-1, keepdims=True) + EPS_NORM)).astype(x.dtype)
        key = jax.random.key(seed)
        ks = jax.random.split(key, 6)
        b, n = (4, 1024)
        x = jax.random.normal(ks[0], (b, n, DIM), dtype=jnp.float32)
        W_qkv = jax.random.normal(ks[1], (DIM, 3 * DIM), dtype=jnp.float32) * DIM ** (-0.5)
        qn_w = jnp.ones((DIM,), dtype=jnp.float32)
        kn_w = jnp.ones((DIM,), dtype=jnp.float32)
        W_out = jax.random.normal(ks[2], (DIM, DIM), dtype=jnp.float32) * DIM ** (-0.5)
        b_out = jnp.zeros((DIM,), dtype=jnp.float32)
        return {'x': x, 'W_qkv': W_qkv, 'qn_w': qn_w, 'kn_w': kn_w, 'W_out': W_out, 'b_out': b_out}
    _L1_attn_all = _L1_attn_setup()
    _L1_attn_in = {k: v for k, v in _L1_attn_all.items() if k in ('W_qkv', 'qn_w', 'kn_w', 'W_out', 'b_out')}
    del _L1_attn_all

    def _L1_ffn_setup():
        import jax, jax.numpy as jnp
        import numpy as np
        B, K, D = (128, 32, 256)
        E = 32
        H = int(D * 0.25)

        def _rsqrt_uniform(key, shape, d):
            bound = d ** (-0.5)
            return jax.random.uniform(key, shape, jnp.float32, -bound, bound)
        key = jax.random.key(seed)
        ks = jax.random.split(key, 7)
        return {'x': jax.random.normal(ks[0], (B, K, D), jnp.float32), 'router_w': _rsqrt_uniform(ks[1], (E, D), D), 'router_b': _rsqrt_uniform(ks[2], (E,), D), 'weights1': _rsqrt_uniform(ks[3], (E, D, H), H), 'bias1': _rsqrt_uniform(ks[4], (E, H), H), 'weights2': _rsqrt_uniform(ks[5], (E, H, D), D), 'bias2': _rsqrt_uniform(ks[6], (E, D), D)}
    _L1_ffn_all = _L1_ffn_setup()
    _L1_ffn_in = {k: v for k, v in _L1_ffn_all.items() if k in ('router_w', 'router_b', 'weights1', 'bias1', 'weights2', 'bias2')}
    del _L1_ffn_all
    return {'x': x, 'L0_tok_emb': _L0_tok_in['emb'], 'L0_tok_in_proj_w': _L0_tok_in['in_proj_w'], 'L0_tok_in_proj_b': _L0_tok_in['in_proj_b'], 'L0_tok_out_proj_w': _L0_tok_in['out_proj_w'], 'L0_tok_out_proj_b': _L0_tok_in['out_proj_b'], 'L0_tok_w1': _L0_tok_in['w1'], 'L0_tok_b1': _L0_tok_in['b1'], 'L0_tok_w2': _L0_tok_in['w2'], 'L0_tok_b2': _L0_tok_in['b2'], 'L0_tok_g1': _L0_tok_in['g1'], 'L0_tok_beta1': _L0_tok_in['beta1'], 'L0_tok_g2': _L0_tok_in['g2'], 'L0_tok_beta2': _L0_tok_in['beta2'], 'L0_attn_w': _L0_attn_in['w'], 'L0_attn_u': _L0_attn_in['u'], 'L0_attn_time_mix_k': _L0_attn_in['time_mix_k'], 'L0_attn_time_mix_v': _L0_attn_in['time_mix_v'], 'L0_attn_time_mix_r': _L0_attn_in['time_mix_r'], 'L0_attn_Wk': _L0_attn_in['Wk'], 'L0_attn_Wv': _L0_attn_in['Wv'], 'L0_attn_Wr': _L0_attn_in['Wr'], 'L0_attn_Wo': _L0_attn_in['Wo'], 'L0_ffn_router_weight': _L0_ffn_in['router_weight'], 'L0_ffn_e_bias': _L0_ffn_in['e_bias'], 'L0_ffn_gate_w': _L0_ffn_in['gate_w'], 'L0_ffn_up_w': _L0_ffn_in['up_w'], 'L0_ffn_down_w': _L0_ffn_in['down_w'], 'L0_ffn_sh_gate_w': _L0_ffn_in['sh_gate_w'], 'L0_ffn_sh_up_w': _L0_ffn_in['sh_up_w'], 'L0_ffn_sh_down_w': _L0_ffn_in['sh_down_w'], 'L1_attn_W_qkv': _L1_attn_in['W_qkv'], 'L1_attn_qn_w': _L1_attn_in['qn_w'], 'L1_attn_kn_w': _L1_attn_in['kn_w'], 'L1_attn_W_out': _L1_attn_in['W_out'], 'L1_attn_b_out': _L1_attn_in['b_out'], 'L1_ffn_router_w': _L1_ffn_in['router_w'], 'L1_ffn_router_b': _L1_ffn_in['router_b'], 'L1_ffn_weights1': _L1_ffn_in['weights1'], 'L1_ffn_bias1': _L1_ffn_in['bias1'], 'L1_ffn_weights2': _L1_ffn_in['weights2'], 'L1_ffn_bias2': _L1_ffn_in['bias2']}

def reference(x, L0_tok_emb, L0_tok_in_proj_w, L0_tok_in_proj_b, L0_tok_out_proj_w, L0_tok_out_proj_b, L0_tok_w1, L0_tok_b1, L0_tok_w2, L0_tok_b2, L0_tok_g1, L0_tok_beta1, L0_tok_g2, L0_tok_beta2, L0_attn_w, L0_attn_u, L0_attn_time_mix_k, L0_attn_time_mix_v, L0_attn_time_mix_r, L0_attn_Wk, L0_attn_Wv, L0_attn_Wr, L0_attn_Wo, L0_ffn_router_weight, L0_ffn_e_bias, L0_ffn_gate_w, L0_ffn_up_w, L0_ffn_down_w, L0_ffn_sh_gate_w, L0_ffn_sh_up_w, L0_ffn_sh_down_w, L1_attn_W_qkv, L1_attn_qn_w, L1_attn_kn_w, L1_attn_W_out, L1_attn_b_out, L1_ffn_router_w, L1_ffn_router_b, L1_ffn_weights1, L1_ffn_bias1, L1_ffn_weights2, L1_ffn_bias2):
    import jax
    import jax.numpy as jnp

    def _L0_tok_ref(tokens, emb, in_proj_w, in_proj_b, out_proj_w, out_proj_b, w1, b1, w2, b2, g1, beta1, g2, beta2):
        import jax, jax.numpy as jnp
        import numpy as np
        VOCAB, D, H = (8000, 256, 16)
        DH = D // H
        DFF = 4 * D
        EPS = 1e-05

        def layer_norm(x, g, b):
            mu = jnp.mean(x, axis=-1, keepdims=True)
            var = jnp.var(x, axis=-1, keepdims=True)
            return (x - mu) * jax.lax.rsqrt(var + EPS) * g + b

        def pos_enc(seq_len, d_model):
            pos = jnp.arange(seq_len, dtype=jnp.float32)[:, None]
            i_even = jnp.arange(0, d_model, 2, dtype=jnp.float32)[None, :]
            angle = pos / jnp.power(10000.0, 2.0 * i_even / d_model)
            pe = jnp.zeros((seq_len, d_model), dtype=jnp.float32)
            pe = pe.at[:, 0::2].set(jnp.sin(angle))
            pe = pe.at[:, 1::2].set(jnp.cos(angle))
            return pe
        B, S = tokens.shape
        x = emb[tokens] + pos_enc(S, D)[None, :, :]
        qkv = x @ in_proj_w.T + in_proj_b
        q, k, v = jnp.split(qkv, 3, axis=-1)
        q = q.reshape(B, S, H, DH)
        k = k.reshape(B, S, H, DH)
        v = v.reshape(B, S, H, DH)
        scores = jnp.einsum('bqhd,bkhd->bhqk', q, k) / jnp.sqrt(jnp.float32(DH))
        attn = jax.nn.softmax(scores, axis=-1)
        ctx = jnp.einsum('bhqk,bkhd->bqhd', attn, v).reshape(B, S, D)
        attn_out = ctx @ out_proj_w.T + out_proj_b
        h = layer_norm(x + attn_out, g1, beta1)
        ff = jax.nn.relu(h @ w1.T + b1) @ w2.T + b2
        return layer_norm(h + ff, g2, beta2)

    def _L0_attn_ref(x, w, u, time_mix_k, time_mix_v, time_mix_r, Wk, Wv, Wr, Wo):
        import jax, jax.numpy as jnp
        import numpy as np
        import math
        D_MODEL = 256
        LAYER_ID = 6
        NUM_LAYERS = 12
        B = 8
        T = 512

        def _wkv(w, u, k, v):
            wn = -jnp.exp(w)

            def step(carry, kv):
                aa, bb, pp = carry
                kt, vt = kv
                ww = u + kt
                p = jnp.maximum(pp, ww)
                e1 = jnp.exp(pp - p)
                e2 = jnp.exp(ww - p)
                y = (e1 * aa + e2 * vt) / (e1 * bb + e2)
                ww2 = pp + wn
                p2 = jnp.maximum(ww2, kt)
                e1b = jnp.exp(ww2 - p2)
                e2b = jnp.exp(kt - p2)
                return ((e1b * aa + e2b * vt, e1b * bb + e2b, p2), y)
            Bd, Td, Cd = k.shape
            init = (jnp.zeros((Bd, Cd), k.dtype), jnp.zeros((Bd, Cd), k.dtype), jnp.full((Bd, Cd), -1e+38, k.dtype))
            kT = jnp.swapaxes(k, 0, 1)
            vT = jnp.swapaxes(v, 0, 1)
            _, ys = jax.lax.scan(step, init, (kT, vT))
            return jnp.swapaxes(ys, 0, 1)
        xs = jnp.pad(x, ((0, 0), (1, 0), (0, 0)))[:, :-1]
        xk = x * time_mix_k + xs * (1.0 - time_mix_k)
        xv = x * time_mix_v + xs * (1.0 - time_mix_v)
        xr = x * time_mix_r + xs * (1.0 - time_mix_r)
        k = jnp.einsum('btc,dc->btd', xk, Wk)
        v = jnp.einsum('btc,dc->btd', xv, Wv)
        r = jnp.einsum('btc,dc->btd', xr, Wr)
        wkv = _wkv(w, u, k, v)
        rwkv = jax.nn.sigmoid(r) * wkv
        return jnp.einsum('btc,dc->btd', rwkv, Wo)

    def _L0_ffn_ref(hidden_states, router_weight, e_bias, gate_w, up_w, down_w, sh_gate_w, sh_up_w, sh_down_w):
        import jax, jax.numpy as jnp
        import numpy as np
        B, S, H = (1, 512, 256)
        E, K = (16, 4)
        G, TG = (4, 2)
        I_MOE = 128
        N_SH = 2
        SCALE = 2.5

        def _mlp(x, gw, uw, dw):
            return jax.nn.silu(x @ gw.T) * (x @ uw.T) @ dw.T

        def _route(x2d, router_weight, e_bias):
            T = x2d.shape[0]
            scores = jax.nn.sigmoid(x2d @ router_weight.T)
            sc = scores + e_bias[None, :]
            group_scores = jnp.sum(jax.lax.top_k(sc.reshape(T, G, E // G), 2)[0], axis=-1)
            _, gidx = jax.lax.top_k(group_scores, TG)
            gmask = jnp.zeros((T, G), sc.dtype).at[jnp.arange(T)[:, None], gidx].set(1.0)
            smask = jnp.repeat(gmask, E // G, axis=1)
            masked = jnp.where(smask > 0, sc, 0.0)
            _, tidx = jax.lax.top_k(masked, K)
            tw = jnp.take_along_axis(scores, tidx, axis=1)
            tw = tw / (jnp.sum(tw, axis=-1, keepdims=True) + 1e-20)
            tw = tw * SCALE
            return (tidx, tw)

        def _moe_forward(hidden_states, router_weight, e_bias, gate_w, up_w, down_w, sh_gate_w, sh_up_w, sh_down_w):
            orig_shape = hidden_states.shape
            x = hidden_states.reshape(-1, H)
            T = x.shape[0]
            tidx, tw = _route(x, router_weight, e_bias)
            g = jnp.einsum('th,eih->tei', x, gate_w)
            u = jnp.einsum('th,eih->tei', x, up_w)
            h = jax.nn.silu(g) * u
            yo = jnp.einsum('tei,ehi->teh', h, down_w)
            combine = jnp.zeros((T, E), tw.dtype).at[jnp.arange(T)[:, None], tidx].add(tw)
            routed = jnp.einsum('te,teh->th', combine, yo)
            shared = _mlp(hidden_states.reshape(-1, H), sh_gate_w, sh_up_w, sh_down_w)
            return (routed + shared).reshape(orig_shape)
        return _moe_forward(hidden_states, router_weight, e_bias, gate_w, up_w, down_w, sh_gate_w, sh_up_w, sh_down_w)

    def _L1_attn_ref(x, W_qkv, qn_w, kn_w, W_out, b_out):
        import jax, jax.numpy as jnp
        import numpy as np
        DIM = 256
        HEADS = 16
        DHEAD = DIM // HEADS
        EPS_NORM = 1e-06
        EPS_DEN = 1e-06

        def rmsnorm(x, w):
            xf = x.astype(jnp.float32)
            return (w * xf * jax.lax.rsqrt(jnp.mean(xf * xf, axis=-1, keepdims=True) + EPS_NORM)).astype(x.dtype)
        b, n, _ = x.shape
        qkv = x @ W_qkv
        q, k, v = jnp.split(qkv, 3, axis=-1)
        q = rmsnorm(q, qn_w)
        k = rmsnorm(k, kn_w)

        def split_heads(t):
            return t.reshape(b, n, HEADS, DHEAD).transpose(0, 2, 1, 3)
        q, k, v = map(split_heads, (q, k, v))
        q = jax.nn.relu(q).astype(jnp.float32)
        k = jax.nn.relu(k).astype(jnp.float32)
        v = v.astype(jnp.float32)
        kv = jnp.einsum('bhnd,bhne->bhde', k, v)
        out = jnp.einsum('bhnd,bhde->bhne', q, kv)
        k_sum = k.sum(axis=2)
        normalizer = jnp.einsum('bhnd,bhd->bhn', q, k_sum) + EPS_DEN
        out = out / normalizer[..., None]
        out = out.transpose(0, 2, 1, 3).reshape(b, n, DIM)
        return out @ W_out + b_out

    def _L1_ffn_ref(x, router_w, router_b, weights1, bias1, weights2, bias2):
        import jax, jax.numpy as jnp
        import numpy as np
        B, K, D = (128, 32, 256)
        E = 32
        H = int(D * 0.25)

        def _rsqrt_uniform(key, shape, d):
            bound = d ** (-0.5)
            return jax.random.uniform(key, shape, jnp.float32, -bound, bound)
        b, k, d = x.shape
        x_flat = x.reshape(-1, d)
        n = x_flat.shape[0]
        logits = x_flat @ router_w.T + router_b
        routed_idx = jnp.argmax(logits, axis=-1)

        def expert_mlp(w1, b1, w2, b2):
            h = jax.nn.relu(x_flat @ w1 + b1)
            return jax.nn.relu(h @ w2 + b2)
        y_all = jax.vmap(expert_mlp)(weights1, bias1, weights2, bias2)
        out_flat = y_all[routed_idx, jnp.arange(n)]
        return out_flat.reshape(b, k, d)
    h = _L0_tok_ref(x, L0_tok_emb, L0_tok_in_proj_w, L0_tok_in_proj_b, L0_tok_out_proj_w, L0_tok_out_proj_b, L0_tok_w1, L0_tok_b1, L0_tok_w2, L0_tok_b2, L0_tok_g1, L0_tok_beta1, L0_tok_g2, L0_tok_beta2)
    h = h + _L0_attn_ref(_layernorm(h, axis=-1), L0_attn_w, L0_attn_u, L0_attn_time_mix_k, L0_attn_time_mix_v, L0_attn_time_mix_r, L0_attn_Wk, L0_attn_Wv, L0_attn_Wr, L0_attn_Wo)
    h = h + _L0_ffn_ref(_layernorm(h, axis=-1), L0_ffn_router_weight, L0_ffn_e_bias, L0_ffn_gate_w, L0_ffn_up_w, L0_ffn_down_w, L0_ffn_sh_gate_w, L0_ffn_sh_up_w, L0_ffn_sh_down_w)
    h = h + _L1_attn_ref(_layernorm(h, axis=-1), L1_attn_W_qkv, L1_attn_qn_w, L1_attn_kn_w, L1_attn_W_out, L1_attn_b_out)
    h = h + _L1_ffn_ref(_layernorm(h, axis=-1), L1_ffn_router_w, L1_ffn_router_b, L1_ffn_weights1, L1_ffn_bias1, L1_ffn_weights2, L1_ffn_bias2)
    return h

_drawn_inputs = setup_inputs


def setup_inputs(seed=0):
    import zlib

    import numpy as np

    out = dict(_drawn_inputs(seed))
    spreads = {'L0_tok_in_proj_b': (0.0, 0.1),
     'L0_tok_out_proj_b': (0.0, 0.1),
     'L0_tok_b1': (0.0, 0.1),
     'L0_tok_b2': (0.0, 0.1),
     'L0_tok_g1': (1.0, 0.2),
     'L0_tok_beta1': (0.0, 0.1),
     'L0_tok_g2': (1.0, 0.2),
     'L0_tok_beta2': (0.0, 0.1),
     'L0_ffn_e_bias': (0.0, 0.521),
     'L1_attn_qn_w': (1.0, 0.6),
     'L1_attn_kn_w': (1.0, 0.6),
     'L1_attn_b_out': (0.0, 0.1)}
    factors = {'L0_attn_u': 64.0,
     'L0_attn_time_mix_k': 8.0,
     'L0_attn_time_mix_r': 3.713,
     'L0_ffn_router_weight': 6.691,
     'L0_ffn_gate_w': 4.318,
     'L0_ffn_up_w': 3.911,
     'L0_ffn_down_w': 4.272,
     'L0_ffn_sh_gate_w': 3.73,
     'L0_ffn_sh_up_w': 3.62,
     'L0_ffn_sh_down_w': 3.766,
     'L1_ffn_bias1': 8.0,
     'L1_ffn_bias2': 3.072}
    for name, (base, spread) in spreads.items():
        noise = np.random.default_rng([zlib.crc32(name.encode()), seed]).standard_normal(out[name].shape)
        drawn = base * np.exp(spread * noise) if base else spread * noise
        out[name] = jnp.asarray(drawn.astype(out[name].dtype))
    for name, factor in factors.items():
        out[name] = (out[name] * factor).astype(out[name].dtype)
    return out
```

```python
from contextlib import ExitStack

import numpy as np
import concourse.bass as bass
from concourse import mybir

F32 = mybir.dt.float32
BF16 = mybir.dt.bfloat16
I32 = mybir.dt.int32
U32 = mybir.dt.uint32
ALU = mybir.AluOpType
ACT = mybir.ActivationFunctionType
AX = mybir.AxisListType

P = 128
B, S, D = 8, 512, 256
TT = S // P
NT = B * TT
KC = D // P
HD = 16
NH = D // HD
G4 = 4
NG = NH // G4
VOCAB = 8000
DFF = 4 * D
AWORDS = 52736
LN_EPS = 1e-5

QPART = (0, 0, 1, 1, 0, 2)
KPART = (0, 1, 0, 1, 2, 0)
NPARTS = len(QPART)
SROWS = NPARTS * HD


def build(nc, a, out, stop=99):
    ctx = ExitStack()
    with ctx:
        held = []

        def sem(name):
            held.append(nc.alloc_semaphore(name=name))
            return held[-1]

        arena = ctx.enter_context(nc.sbuf_tensor("arena", [P, AWORDS], F32))
        ps = ctx.enter_context(nc.psum_tensor("ps", [P, 8, 512], F32))
        free = [0]

        def take(n, dt=F32, at=None):
            words = n if dt != BF16 else (n + 1) // 2
            start = free[0] if at is None else at
            if at is None:
                free[0] += words
                assert free[0] <= AWORDS, free[0]
            v = arena[:, start:start + words]
            return v if dt == F32 else v.bitcast(dt)

        def mark():
            return free[0]

        H = take(NT * D).rearrange("p (t d) -> p t d", d=D)
        ident = take(P)
        identb = take(P, BF16)
        mhalf = take(TT)

        ENGINES = 5

        def run(stages):
            bar = sem(f"stage_ends{len(stages)}")

            def program(e, which):
                for n, stage in enumerate(stages):
                    stage[which](e)
                    e.drain().then_inc(bar, 1)
                    e.wait_ge(bar, ENGINES * (n + 1))

            with nc.Block() as block:
                @block.sync
                def _(sp):
                    program(sp, 0)

                @block.gpsimd
                def _(pool):
                    program(pool, 1)

                @block.scalar
                def _(act):
                    program(act, 2)

                @block.vector
                def _(dve):
                    program(dve, 3)

                @block.tensor
                def _(pe):
                    program(pe, 4)
            nc.clear_and_free_semaphores(held)
            held.clear()
            nc.all_engine_barrier()

        def alone(e):
            e.sem_inc(passed[0], 1)

        PERSIST = mark()
        passed = [sem("passed")]

        V = take(NT * D).rearrange("p (t d) -> p t d", d=D)
        STAGE1 = mark()
        idx = take(NT, I32)
        W_QK = take(KC * 2 * D).rearrange("p (k m) -> p k m", k=KC)
        W_V = take(KC * D).rearrange("p (k m) -> p k m", k=KC)
        b_qk = take(4)
        pos = take(TT * D).rearrange("p (t d) -> p t d", d=D)
        b_v = take(D)
        b_o = take(D)
        tokf = take(NT)
        negf = take(NT)
        idxs = take(2 * TT, I32).rearrange("p (s t) -> p s t", s=2)
        xg = take(2 * TT * D).rearrange("p (s t d) -> p s t d", s=2, d=D)
        xT = take(2 * KC * S).rearrange("p (s k t) -> p s k t", s=2, k=KC)
        qf = take(2 * S).rearrange("p (s t) -> p s t", s=2)
        qr = take(2 * S).rearrange("p (s t) -> p s t", s=2)
        parts = take(2 * 4 * 3 * S, BF16).rearrange("p (s m c t) -> p s m c t", s=2, m=4, c=3)
        split_dram = nc.dram_tensor("split_dram", (B, 4, P, 3, S), BF16, kind="Internal").ap()

        const_in = sem("const_in")
        tok_in = sem("tok_in")
        idx_steps = sem("idx_steps")
        ident_ready = sem("ident_ready")
        identb_ready = sem("identb_ready")
        idx_slot = sem("idx_slot")
        gathered = [sem(f"gathered{t}") for t in range(2 * TT)]
        x_ready = sem("x_ready")
        x_kept = sem("x_kept")
        x_turned = sem("x_turned")
        xT_ready = sem("xT_ready")
        qk_done = sem("qk_done")
        v_done = sem("v_done")
        qk_read = sem("qk_read")
        v_read = sem("v_read")
        part0 = sem("part0")
        rest0 = sem("rest0")
        part1 = sem("part1")
        part2 = sem("part2")
        parts_out = [sem(f"parts_out{s}") for s in range(2)]
        CONSTS = 8

        def sp_embed(sp):
            sp.dma_start(idx, a["x"]).then_inc(tok_in, 16)
            for dst, name in ((W_QK, "w_qk"), (W_V, "w_v"), (b_qk, "b_qk"), (pos, "pos"), (ident, "ident")):
                sp.dma_start(dst, a[name]).then_inc(const_in, 16)
            sp.dma_start(b_v, a["b_v"].to_broadcast((P, D))).then_inc(const_in, 16)
            sp.dma_start(b_o, a["b_o"].to_broadcast((P, D))).then_inc(const_in, 16)
            with sp.Fori(0, B // 2) as pair:
                for s in range(2):
                    sp.wait_ge(part0, (pair * 2 + s) * 4 + 4)
                    sp.wait_ge(part1, (pair * 2 + s) * 4 + 4)
                    sp.wait_ge(part2, (pair * 2 + s) * 4 + 4)
                    sp.dma_start(split_dram[pair * 2 + s].rearrange("m p c t -> p m c t"), parts[:, s]).then_inc(parts_out[s], 16)
            for s in range(2):
                sp.wait_ge(parts_out[s], 16 * (B // 2))

        def pool_embed(pool):
            pool.wait_ge(idx_steps, 5)
            pool.sem_inc(x_kept, 1)
            with pool.Fori(0, B // 2) as pair:
                for s in range(2):
                    pool.wait_ge(x_turned, pair * 2 + s)
                    pool.wait_ge(x_kept, pair * 2 + s)
                    pool.tensor_copy(idxs[:, s, :], idx[:, bass.ds((pair * 2 + s) * TT, TT)]).then_inc(idx_slot, 1)
                    pool.wait_ge(idx_slot, pair * 2 + s + 1)
                    alone(pool)
                    for t in range(TT):
                        pool.indirect_dma_start(
                            out=xg[:, s, t, :], out_offset=None, in_=a["emb"],
                            in_offset=bass.IndirectOffsetOnAxis(ap=idxs[:, s, t:t + 1].bitcast(U32), axis=0)
                        ).then_inc(gathered[s * TT + t], 16)
                    pool.wait_ge(x_ready, pair * 2 + s + 1)
                    pool.tensor_tensor(H[:, bass.ds((pair * 2 + s) * TT, TT), :], xg[:, s],
                                       b_o.unsqueeze(1).to_broadcast((P, TT, D)), ALU.add).then_inc(x_kept, 1)

        def dve_embed(dve):
            dve.wait_ge(tok_in, 16)
            dve.tensor_copy(tokf, idx).then_inc(idx_steps, 1)
            dve.wait_ge(idx_steps, 1)
            dve.tensor_scalar(negf, tokf, 0.0, float(VOCAB), ALU.is_lt, ALU.mult).then_inc(idx_steps, 1)
            dve.wait_ge(idx_steps, 2)
            dve.tensor_tensor(tokf, tokf, negf, ALU.add).then_inc(idx_steps, 1)
            dve.wait_ge(idx_steps, 3)
            dve.tensor_scalar(negf, tokf, 0.0, float(VOCAB - 1), ALU.max, ALU.min).then_inc(idx_steps, 1)
            dve.wait_ge(idx_steps, 4)
            dve.tensor_copy(idx, negf).then_inc(idx_steps, 1)
            dve.wait_ge(const_in, 16 * 7)
            dve.tensor_copy(identb, ident).then_inc(identb_ready, 1)
            dve.tensor_scalar(b_qk[:, 0:2], b_qk[:, 0:2], HD ** -0.5, None, ALU.mult).then_inc(identb_ready, 1)
            dve.sem_inc(x_turned, 1)
            with dve.Fori(0, B // 2) as pair:
                for s in range(2):
                    b = pair * 2 + s
                    for t in range(TT):
                        dve.wait_ge(gathered[s * TT + t], pair * 16 + 16)
                    dve.tensor_tensor(xg[:, s], xg[:, s], pos, ALU.add).then_inc(x_ready, 1)
                    for m in range(4):
                        dve.wait_ge(part0, b * 4 + m + 1)
                        dve.tensor_tensor(qr[:, m % 2], qf[:, m % 2], parts[:, s, m, 0, :], ALU.subtract).then_inc(rest0, 1)
                        dve.wait_ge(part1, b * 4 + m + 1)
                        dve.tensor_tensor(parts[:, s, m, 2, :], qr[:, m % 2], parts[:, s, m, 1, :], ALU.subtract).then_inc(part2, 1)
                    for h in range(2):
                        dve.wait_ge(v_done, b * 2 + h + 1)
                        dve.tensor_tensor(V[:, bass.ds(b * TT + 2 * h, 2), :], ps[:, 6 + h, :].rearrange("p (t d) -> p t d", d=D),
                                          b_v.unsqueeze(1).to_broadcast((P, 2, D)), ALU.add).then_inc(v_read, 1)

        def act_embed(act):
            act.wait_ge(identb_ready, 2)
            with act.Fori(0, B // 2) as pair:
                for s in range(2):
                    b = pair * 2 + s
                    act.wait_ge(x_turned, b + 2)
                    act.activation(xT[:, s], ps[:, 0:2, :], ACT.Copy).then_inc(xT_ready, 1)
                    act.wait_ge(parts_out[s], pair * 16)
                    for m in range(4):
                        scale = HD ** -0.5 if m < 2 else 1.0
                        act.wait_ge(qk_done, b * 4 + m + 1)
                        act.activation(qf[:, m % 2], ps[:, 2 + m, :], ACT.Identity, bias=b_qk[:, m:m + 1], scale=scale).then_inc(qk_read, 1)
                        act.activation(parts[:, s, m, 0, :], ps[:, 2 + m, :], ACT.Identity, bias=b_qk[:, m:m + 1], scale=scale).then_inc(part0, 1)
                        act.wait_ge(rest0, b * 4 + m + 1)
                        act.activation(parts[:, s, m, 1, :], qr[:, m % 2], ACT.Copy).then_inc(part1, 1)

        def pe_embed(pe):
            pe.wait_ge(const_in, 16 * 7)
            with pe.Fori(0, B // 2) as pair:
                for s in range(2):
                    b = pair * 2 + s
                    pe.wait_ge(x_ready, b + 1)
                    pe.wait_ge(xT_ready, b)
                    for t in range(TT):
                        for k in range(KC):
                            mm = pe.transpose(ps[:, k, t * P:(t + 1) * P], xg[:, s, t, k * P:(k + 1) * P], ident)
                    mm.then_inc(x_turned, 1)
                    pe.wait_ge(xT_ready, b + 1)
                    for m in range(4):
                        pe.wait_ge(part0, b * 4)
                        for k in range(KC):
                            mm = pe.matmul(ps[:, 2 + m, :], W_QK[:, k, m * P:(m + 1) * P], xT[:, s, k, :],
                                           start=(k == 0), stop=(k == KC - 1))
                        mm.then_inc(qk_done, 1)
                    pe.wait_ge(v_read, b * 2)
                    for t in range(TT):
                        for k in range(KC):
                            mm = pe.matmul(ps[:, 6 + t // 2, (t % 2) * D:(t % 2 + 1) * D], xT[:, s, k, t * P:(t + 1) * P], W_V[:, k, :],
                                           start=(k == 0), stop=(k == KC - 1))
                        if t % 2:
                            mm.then_inc(v_done, 1)

        free[0] = STAGE1
        W_O = take(NG * D).rearrange("p (j d) -> p j d", j=NG)
        RING = 4
        AHEAD = 2
        q6 = take(RING * G4 * S, BF16).rearrange("p (r h t) -> p r h t", r=RING, h=G4)
        k6 = take(RING * G4 * S, BF16).rearrange("p (r h t) -> p r h t", r=RING, h=G4)
        vaug = take(2 * TT * NH * 32).rearrange("p (s t h e) -> p s t h e", s=2, t=TT, h=NH)
        pT = take(2 * G4 * S).rearrange("p (r h t) -> p r h t", r=2, h=G4)
        cT = take(NG * S).rearrange("p (j t) -> p j t", j=NG)
        sums = take(S)
        rsum = take(S)
        nmax = take(16).rearrange("p (t h) -> p t h", h=G4)
        nrest = take(16).rearrange("p (t h) -> p t h", h=G4)
        msplit = take(2 * TT * G4 * 3, BF16).rearrange("p (s t h c) -> p s t h c", s=2, t=TT, h=G4)
        mt = take(2 * S, BF16).rearrange("p (s t) -> p s t", s=2)
        MROWS = 3 * G4
        QROWS = SROWS + 3

        wo_in = sem("wo_in")
        ones_ready = sem("ones_ready")
        qk_in = [sem(f"qk_in{r}") for r in range(RING)]
        m_in = [sem(f"m_in{r}") for r in range(RING)]
        vaug_ready = sem("vaug_ready")
        s1_done = sem("s1_done")
        max_done = sem("max_done")
        max_steps = sem("max_steps")
        mt_done = sem("mt_done")
        mt_ready = sem("mt_ready")
        s2_done = sem("s2_done")
        exp_done = sem("exp_done")
        pv_done = sem("pv_done")
        ctx_steps = sem("ctx_steps")
        ctx_ready = sem("ctx_ready")
        o_done = sem("o_done")
        o_read = sem("o_read")
        GROUPS = B * NG
        PAIR = 2 * NG

        def sp_attn(sp):
            sp.dma_start(W_O, a["w_o"]).then_inc(wo_in, 16)
            with sp.Fori(0, B // 2) as pair:
                for u in range(PAIR):
                    b, j, r = pair * 2 + u // NG, u % NG, u % RING
                    sp.wait_ge(s2_done, (pair * PAIR + u + 1) * 8)
                    for dst, first, which in ((q6, 0, QPART), (k6, 2, KPART)):
                        for n, c in enumerate(which):
                            src = split_dram[b, first + j // 2, (j % 2) * 64:(j % 2 + 1) * 64, c, :]
                            sp.dma_start(dst[n * HD:(n + 1) * HD, r], src.rearrange("(h d) t -> d h t", d=HD)).then_inc(qk_in[r], 16)

        def pool_attn(pool):
            pool.memset(vaug, 1.0).then_inc(ones_ready, 1)
            pool.wait_ge(ones_ready, 1)
            pool.memset(k6[SROWS:QROWS], 1.0).then_inc(ones_ready, 1)
            pool.wait_ge(ones_ready, 2)
            with pool.Fori(0, B // 2) as pair:
                for s in range(2):
                    b = pair * 2 + s
                    pool.wait_ge(pv_done, b * 16)
                    pool.tensor_copy(vaug[:, s, :, :, 0:HD], V[:, bass.ds(b * TT, TT), :].rearrange("p t (h d) -> p t h d", d=HD)).then_inc(vaug_ready, 1)

        def pe_attn(pe):
            def maxima(g, u, qt):
                r = u % RING
                if qt == 0:
                    pe.wait_ge(qk_in[r], (g_uses(g, u)) * 12 * 16)
                pe.wait_ge(max_done, g * 4 + qt)
                for h in range(G4):
                    mm = pe.matmul(ps[:, h, :], q6[0:SROWS, r, h, qt * P:(qt + 1) * P], k6[0:SROWS, r, h, :], start=True, stop=True)
                mm.then_inc(s1_done, 1)

            def g_uses(g, u):
                return uses[0] + u // RING + 1

            def turn_maxima(g, u, g_rows=None):
                pe.wait_ge(max_steps, g * 6 + 6)
                pe.wait_ge(mt_ready, g)
                if g_rows is not None:
                    pe.wait_ge(o_read, g_rows)
                out7 = ps[:, 7, 0:256].bitcast(BF16)
                for qt in range(TT):
                    mm = pe.transpose(out7[0:MROWS, qt * P:(qt + 1) * P], msplit[:, u % 2, qt].rearrange("p h c -> p (h c)"), identb)
                mm.then_inc(mt_done, 1)

            def scores(g, u, c):
                r, kt, hp = u % RING, c // 2, c % 2
                if c == 0:
                    pe.wait_ge(m_in[r], g_uses(g, u) * 4 * 16)
                pe.wait_ge(exp_done, g * 8 + c)
                for i in range(2):
                    h = 2 * hp + i
                    mm = pe.matmul(ps[:, 4 + i, :], k6[0:QROWS, r, h, kt * P:(kt + 1) * P], q6[0:QROWS, r, h, :], start=True, stop=True)
                mm.then_inc(s2_done, 1)

            def values(g, u, kt):
                s, j = u // NG, u % NG
                if kt == 0:
                    pe.wait_ge(ctx_ready, g)
                    pe.wait_ge(vaug_ready, uses[0] + s + 1)
                pe.wait_ge(exp_done, g * 8 + 2 * kt + 2)
                for h in range(G4):
                    mm = pe.matmul(ps[32 * h:32 * h + 32, 6, :], vaug[:, s, kt, G4 * j + h, :], pT[:, kt % 2, h, :],
                                   start=(kt == 0), stop=(kt == TT - 1))
                mm.then_inc(pv_done, 1)

            def out_proj(b, t, turned):
                pe.wait_ge(mt_ready, turned)
                pe.wait_ge(ctx_ready, (b + 1) * NG)
                pe.wait_ge(o_read, b * TT + t)
                for j in range(NG):
                    mm = pe.matmul(ps[:, 7, 256:512], cT[:, j, t * P:(t + 1) * P], W_O[:, j, :], start=(j == 0), stop=(j == NG - 1))
                mm.then_inc(o_done, 1)

            uses = [0]
            pe.sem_inc(s2_done, RING * 8)
            pe.sem_inc(pv_done, 16)
            pe.wait_ge(wo_in, 16)
            pe.wait_ge(ones_ready, 2)
            for g in range(AHEAD):
                for qt in range(TT):
                    maxima(g, g, qt)
                turn_maxima(g, g)

            def step(pair, last):
                for u in range(PAIR):
                    g = pair * PAIR + u
                    ahead = not last or u + AHEAD < PAIR

                    def look(qt):
                        if ahead:
                            v = u + AHEAD
                            uses[0] = pair * 2
                            maxima(g + AHEAD, v, qt)
                    uses[0] = pair * 2
                    scores(g, u, 0)
                    look(0)
                    scores(g, u, 1)
                    scores(g, u, 2)
                    values(g, u, 0)
                    look(1)
                    scores(g, u, 3)
                    if u == NG:
                        out_proj(pair * 2, 0, g + AHEAD)
                        out_proj(pair * 2, 1, g + AHEAD)
                    scores(g, u, 4)
                    values(g, u, 1)
                    look(2)
                    scores(g, u, 5)
                    if u == NG:
                        out_proj(pair * 2, 2, g + AHEAD)
                        out_proj(pair * 2, 3, g + AHEAD)
                    scores(g, u, 6)
                    values(g, u, 2)
                    look(3)
                    scores(g, u, 7)
                    if ahead:
                        turn_maxima(g + AHEAD, u, pair * 2 * TT + (TT if u >= NG else 0))
                    values(g, u, 3)
                for t in range(TT):
                    out_proj(pair * 2 + 1, t, pair * PAIR + PAIR + (0 if last else AHEAD))

            with pe.Fori(0, B // 2 - 1) as pair:
                step(pair, False)
            step(B // 2 - 1, True)

        def act_attn(act):
            def spread_maxima(g, u, uses):
                act.wait_ge(m_in[(u - 2) % RING], (uses + (u - 2) // RING + 1) * 64)
                act.wait_ge(mt_done, g + 1)
                act.activation(mt[0:MROWS, u % 2, :], ps[0:MROWS, 7, 0:256].bitcast(BF16), ACT.Copy).then_inc(mt_ready, 1)
                act.wait_ge(mt_ready, g + 1)
                for h in range(G4):
                    act.dma_start(q6[SROWS:QROWS, u % RING, h, :], mt[3 * h:3 * h + 3, u % 2, :]).then_inc(m_in[u % RING], 16)

            def exps(g, u, c):
                kt, hp = c // 2, c % 2
                act.wait_ge(s2_done, g * 8 + c + 1 + RING * 8)
                if hp == 0:
                    act.wait_ge(pv_done, g * TT + kt + 15)
                act.activation(pT[:, kt % 2, 2 * hp:2 * hp + 2, :], ps[:, 4:6, :], ACT.Exp).then_inc(exp_done, 1)

            for g in range(AHEAD):
                act.wait_ge(mt_done, g + 1)
                act.activation(mt[0:MROWS, g % 2, :], ps[0:MROWS, 7, 0:256].bitcast(BF16), ACT.Copy).then_inc(mt_ready, 1)
                act.wait_ge(mt_ready, g + 1)
                for h in range(G4):
                    act.dma_start(q6[SROWS:QROWS, g % RING, h, :], mt[3 * h:3 * h + 3, g % 2, :]).then_inc(m_in[g % RING], 16)

            def step(pair, last):
                for u in range(PAIR):
                    g = pair * PAIR + u
                    for c in range(8):
                        exps(g, u, c)
                    if not last or u + AHEAD < PAIR:
                        spread_maxima(g + AHEAD, u + AHEAD, pair * 2)

            with act.Fori(0, B // 2 - 1) as pair:
                step(pair, False)
            step(B // 2 - 1, True)

        def dve_attn(dve):
            def maxima(g, u, residual_of=None):
                for qt in range(TT):
                    if residual_of is not None and qt == 2:
                        residual(residual_of, 0)
                        residual(residual_of, 1)
                    if residual_of is not None and qt == 3:
                        residual(residual_of, 2)
                        residual(residual_of, 3)
                    dve.wait_ge(s1_done, g * 4 + qt + 1)
                    dve.tensor_reduce(nmax[:, qt, :], ps[:, 0:4, :], AX.X, ALU.max, negate=True).then_inc(max_done, 1)
                m = msplit[:, u % 2]
                dve.wait_ge(max_done, g * 4 + 4)
                dve.wait_ge(mt_ready, g)
                dve.tensor_copy(m[:, :, :, 0], nmax).then_inc(max_steps, 1)
                dve.wait_ge(max_steps, g * 6 + 1)
                dve.tensor_tensor(nrest, nmax, m[:, :, :, 0], ALU.subtract).then_inc(max_steps, 1)
                dve.wait_ge(max_steps, g * 6 + 2)
                dve.tensor_copy(m[:, :, :, 1], nrest).then_inc(max_steps, 1)
                dve.wait_ge(max_steps, g * 6 + 3)
                dve.tensor_tensor(m[:, :, :, 2], nrest, m[:, :, :, 1], ALU.subtract).then_inc(max_steps, 3)

            def normed(g, u):
                dve.wait_ge(pv_done, g * TT + TT + 16)
                alone(dve)
                dve.stream_shuffle(sums, ps[:, 6, :], [16 + i % 16 for i in range(32)]).then_inc(ctx_steps, 1)
                dve.wait_ge(ctx_steps, g * 2 + 1)
                dve.reciprocal(rsum, sums).then_inc(ctx_steps, 1)
                dve.wait_ge(ctx_steps, g * 2 + 2)
                dve.tensor_tensor(cT[:, u % NG, :], ps[:, 6, :], rsum, ALU.mult).then_inc(ctx_ready, 1)

            def residual(b, t):
                dve.wait_ge(o_done, b * TT + t + 1)
                h = H[:, bass.ds(b * TT + t, 1), :] if not isinstance(b, int) else H[:, b * TT + t:b * TT + t + 1, :]
                dve.tensor_tensor(h, ps[:, 7:8, 256:512], h, ALU.add).then_inc(o_read, 1)

            for g in range(AHEAD):
                maxima(g, g)

            def step(pair, last):
                for u in range(PAIR):
                    g = pair * PAIR + u
                    if not last or u + AHEAD < PAIR:
                        maxima(g + AHEAD, u, pair * 2 if u == NG else None)
                    normed(g, u)
                for t in range(TT):
                    residual(pair * 2 + 1, t)

            with dve.Fori(0, B // 2 - 1) as pair:
                step(pair, False)
            step(B // 2 - 1, True)

        class Front:

            def __init__(self, name, affine=None, pad=0):
                self.affine = affine
                self.z = take(2 * TT * D).rearrange("p (s t d) -> p s t d", s=2, d=D)
                self.pad = pad
                self.zT = take(2 * KC * (S + pad)).rearrange("p (s k t) -> p s k t", s=2, k=KC)
                self.stats = take(2 * TT * 6).rearrange("p (s t x) -> p s t x", s=2, t=TT)
                self.mv = take(2 * TT * 2).rearrange("p (s t x) -> p s t x", s=2, t=TT)
                self.rstd = take(2 * TT).rearrange("p (s t) -> p s t", s=2)
                self.stat_steps = sem(name + "_stat_steps")
                self.rstd_steps = sem(name + "_rstd_steps")
                self.z_ready = sem(name + "_z_ready")
                self.scaled = sem(name + "_scaled")
                self.turned = sem(name + "_turned")
                self.zT_ready = sem(name + "_zT_ready")

            def dve(self, dve, b, s, wait_slot):
                for t in range(TT):
                    h = H[:, bass.ds(b * TT + t, 1), :].rearrange("p a d -> p (a d)")
                    last = dve.bn_stats(self.stats[:, s, t, :], h)
                last.then_inc(self.stat_steps, 1)
                dve.wait_ge(self.stat_steps, b * 2 + 1)
                alone(dve)
                for t in range(TT):
                    last = dve.bn_aggr(self.mv[:, s, t, :], self.stats[:, s, t, :])
                last.then_inc(self.stat_steps, 1)
                wait_slot()
                dve.wait_ge(self.rstd_steps, b * 2 + 2)
                for t in range(TT):
                    h = H[:, bass.ds(b * TT + t, 1), :].rearrange("p a d -> p (a d)")
                    last = dve.tensor_scalar(self.z[:, s, t, :], h, self.mv[:, s, t, 0:1], self.rstd[:, s, t:t + 1], ALU.subtract, ALU.mult)
                last.then_inc(self.z_ready, 1)

            def pool(self, pool, b, s):
                root_of_variance(pool, self.rstd[:, s], self.mv[:, s, :, 1], self.stat_steps, b * 2 + 2, self.rstd_steps, b * 2)
                if self.affine:
                    gain, shift = self.affine
                    pool.wait_ge(self.z_ready, b + 1)
                    pool.tensor_tensor(self.z[:, s], self.z[:, s], gain.unsqueeze(1).to_broadcast((P, TT, D)), ALU.mult).then_inc(self.scaled, 1)
                    pool.wait_ge(self.scaled, b * 2 + 1)
                    pool.tensor_tensor(self.z[:, s], self.z[:, s], shift.unsqueeze(1).to_broadcast((P, TT, D)), ALU.add).then_inc(self.scaled, 1)

            def pe(self, pe, b, s):
                if self.affine:
                    pe.wait_ge(self.scaled, b * 2 + 2)
                else:
                    pe.wait_ge(self.z_ready, b + 1)
                pe.wait_ge(self.zT_ready, b)
                for t in range(TT):
                    for k in range(KC):
                        mm = pe.transpose(ps[:, k, t * P:(t + 1) * P], self.z[:, s, t, k * P:(k + 1) * P], ident)
                mm.then_inc(self.turned, 1)

            def act(self, act, b, s, wait_slot):
                act.wait_ge(self.turned, b + 1)
                wait_slot()
                act.activation(self.zT[:, s, :, self.pad:], ps[:, 0:KC, :], ACT.Copy).then_inc(self.zT_ready, 1)

        def root_of_variance(pool, rstd, var, ready, count, steps, done):
            pool.wait_ge(ready, count)
            alone(pool)
            pool.tensor_scalar(rstd, var, LN_EPS, None, ALU.add).then_inc(steps, 1)
            pool.wait_ge(steps, done + 1)
            pool.tensor_tensor(rstd, rstd, mhalf, ALU.pow).then_inc(steps, 1)

        def batches(e, first, step):
            first(0, 0)
            with e.Fori(0, B // 2 - 1) as pair:
                step(pair * 2, 0, False)
                step(pair * 2 + 1, 1, False)
            step(B - 2, 0, False)
            step(B - 1, 1, True)

        free[0] = PERSIST
        MF = DFF // P
        W_1 = take(KC * DFF).rearrange("p (k m) -> p k m", k=KC)
        W_2 = take(MF * D).rearrange("p (k d) -> p k d", k=MF)
        b_1 = take(MF)
        norms = take(5 * D).rearrange("p (n d) -> p n d", n=5)
        g_1, beta_1, b_2, g_2, beta_2 = (norms[:, n] for n in range(5))
        f3 = Front("ff", affine=(g_1, beta_1))
        fT = take(2 * MF * S).rearrange("p (s m t) -> p s m t", s=2, m=MF)
        y2 = take(2 * TT * D).rearrange("p (s t d) -> p s t d", s=2, d=D)
        stats2 = take(2 * TT * 6).rearrange("p (s t x) -> p s t x", s=2, t=TT)
        mv2 = take(2 * TT * 2).rearrange("p (s t x) -> p s t x", s=2, t=TT)
        rstd2 = take(2 * TT).rearrange("p (s t) -> p s t", s=2)
        w3_in = sem("w3_in")
        mhalf_ready = sem("mhalf_ready")
        up_done = sem("up_done")
        relu_done = sem("relu_done")
        down_done = sem("down_done")
        y2_sums = sem("y2_sums")
        y2_steps = sem("y2_steps")
        rstd2_steps = sem("rstd2_steps")
        h0_steps = sem("h0_steps")

        def sp_ff(sp):
            for dst, name in ((W_1, "w_1"), (W_2, "w_2"), (b_1, "b_1")):
                sp.dma_start(dst, a[name]).then_inc(w3_in, 16)
            sp.dma_start(norms.rearrange("p n d -> p (n d)"), a["norms"].to_broadcast((P, 5 * D))).then_inc(w3_in, 16)

        def pool_ff(pool):
            pool.memset(mhalf, -0.5).then_inc(mhalf_ready, 1)
            pool.wait_ge(mhalf_ready, 1)
            pool.wait_ge(w3_in, 64)

            def step(b, s, last):
                if not last:
                    f3.pool(pool, b + 1, 1 - s)
                root_of_variance(pool, rstd2[:, s], mv2[:, s, :, 1], y2_steps, b * 3 + 2, rstd2_steps, b * 2)
                pool.wait_ge(y2_steps, b * 3 + 3)
                pool.tensor_tensor(y2[:, s], y2[:, s], g_2.unsqueeze(1).to_broadcast((P, TT, D)), ALU.mult).then_inc(h0_steps, 1)
                pool.wait_ge(h0_steps, b * 2 + 1)
                pool.tensor_tensor(H[:, bass.ds(b * TT, TT), :], y2[:, s], beta_2.unsqueeze(1).to_broadcast((P, TT, D)), ALU.add).then_inc(h0_steps, 1)
            batches(pool, lambda b, s: f3.pool(pool, b, s), step)

        def pe_ff(pe):
            pe.wait_ge(w3_in, 64)

            def step(b, s, last):
                pe.wait_ge(f3.zT_ready, b + 1)
                for m in range(MF):
                    pe.wait_ge(relu_done, b * MF + m - 3 if m >= 4 else b * MF)
                    for k in range(KC):
                        mm = pe.matmul(ps[:, 2 + m % 4, :], W_1[:, k, m * P:(m + 1) * P], f3.zT[:, s, k, :], start=(k == 0), stop=(k == KC - 1))
                    mm.then_inc(up_done, 1)
                if not last:
                    f3.pe(pe, b + 1, 1 - s)
                pe.wait_ge(relu_done, b * MF + MF)
                pe.wait_ge(y2_sums, b * 2)
                for t in range(TT):
                    for m in range(MF):
                        mm = pe.matmul(ps[:, 6 + t // 2, (t % 2) * D:(t % 2 + 1) * D], fT[:, s, m, t * P:(t + 1) * P], W_2[:, m, :],
                                       start=(m == 0), stop=(m == MF - 1))
                    if t % 2:
                        mm.then_inc(down_done, 1)
            batches(pe, lambda b, s: f3.pe(pe, b, s), step)

        def act_ff(act):
            act.wait_ge(w3_in, 64)
            free_slot = lambda b: (lambda: act.wait_ge(up_done, b * MF))

            def step(b, s, last):
                for m in range(MF):
                    act.wait_ge(up_done, b * MF + m + 1)
                    if m == 0:
                        act.wait_ge(down_done, b * 2)
                    act.activation(fT[:, s, m, :], ps[:, 2 + m % 4, :], ACT.Relu, bias=b_1[:, m:m + 1]).then_inc(relu_done, 1)
                if not last:
                    f3.act(act, b + 1, 1 - s, free_slot(b))
            act.sem_inc(down_done, 2)
            batches(act, lambda b, s: f3.act(act, b, s, lambda: None), step)

        def dve_ff(dve):
            dve.wait_ge(w3_in, 64)

            def step(b, s, last):
                if not last:
                    f3.dve(dve, b + 1, 1 - s, lambda: dve.wait_ge(y2_sums, b * 2))
                dve.wait_ge(h0_steps, b * 2)
                for h in range(2):
                    dve.wait_ge(down_done, b * 2 + h + 1 + 2)
                    dve.tensor_tensor(y2[:, s, 2 * h:2 * h + 2, :], ps[:, 6 + h, :].rearrange("p (t d) -> p t d", d=D),
                                      f3.z[:, s, 2 * h:2 * h + 2, :], ALU.add).then_inc(y2_sums, 1)
                dve.wait_ge(y2_sums, b * 2 + 2)
                dve.tensor_tensor(y2[:, s], y2[:, s], b_2.unsqueeze(1).to_broadcast((P, TT, D)), ALU.add).then_inc(y2_added, 1)
                dve.wait_ge(y2_added, b + 1)
                for t in range(TT):
                    ins = dve.bn_stats(stats2[:, s, t, :], y2[:, s, t, :])
                ins.then_inc(y2_steps, 1)
                dve.wait_ge(y2_steps, b * 3 + 1)
                alone(dve)
                for t in range(TT):
                    ins = dve.bn_aggr(mv2[:, s, t, :], stats2[:, s, t, :])
                ins.then_inc(y2_steps, 1)
                dve.wait_ge(rstd2_steps, b * 2 + 2)
                for t in range(TT):
                    ins = dve.tensor_scalar(y2[:, s, t, :], y2[:, s, t, :], mv2[:, s, t, 0:1], rstd2[:, s, t:t + 1], ALU.subtract, ALU.mult)
                ins.then_inc(y2_steps, 1)
            batches(dve, lambda b, s: f3.dve(dve, b, s, lambda: None), step)
        y2_added = sem("y2_added")

        free[0] = PERSIST
        W_NOW, W_PAST = (take(3 * KC * D).rearrange("p (n k m) -> p n k m", n=3, k=KC) for _ in range(2))
        past = take(3 * KC).rearrange("p (n k) -> p n k", n=3)
        W_WO = take(KC * D).rearrange("p (k d) -> p k d", k=KC)
        vecs = take(5 * KC).rearrange("p (n k) -> p n k", n=5)
        wn = take(KC)
        decay = take(KC * S).rearrange("p (k t) -> p k t", k=KC)
        f4 = Front("wkv", pad=1)

        def rows4(n=S, slots=0):
            if slots:
                return take(slots * KC * n).rearrange("p (s k t) -> p s k t", s=slots, k=KC)
            return take(KC * n).rearrange("p (k t) -> p k t", k=KC)
        k_s, v_s, er_s = rows4(slots=2), rows4(slots=2), rows4(slots=2)
        PPm, AA, BB = rows4(S + 1), rows4(S + 1), rows4(S + 1)
        gap, gap0, gap1, e1b, e2b, e2v = (rows4() for _ in range(6))
        dif, dif0, dif1, e1, e2 = (rows4() for _ in range(5))
        num, nv, den, rden = (rows4() for _ in range(4))
        rT = rows4(slots=2)
        w4_in = sem("w4_in")
        w4_steps = sem("w4_steps")
        edges = sem("edges")
        firsts = sem("firsts")
        mixture = sem("mixture")
        kvr_done = sem("kvr_done")
        kvr_kept = sem("kvr_kept")
        scan_p = sem("scan_p")
        gaps = sem("gaps")
        decays = sem("decays")
        ev_ready = sem("ev_ready")
        scan_ab = sem("scan_ab")
        weights = sem("weights")
        nv_ready = sem("nv_ready")
        ratio = sem("ratio")
        r_ready = sem("r_ready")
        wo_done = sem("wo_done")
        wo_read = sem("wo_read")

        def sp_wkv(sp):
            for dst, name in ((W_NOW, "w_kvr"), (W_WO, "w_wo"), (vecs, "vecs")):
                sp.dma_start(dst, a[name]).then_inc(w4_in, 16)

        def pool_wkv(pool):
            for s in range(2):
                pool.memset(f4.zT[:, s, :, 0:1], 0.0).then_inc(edges, 1)

            def step(b, s, last):
                pool.wait_ge(decays, b * 2 + 2)
                pool.tensor_tensor(e2v, e2b, v_s[:, s], ALU.mult).then_inc(ev_ready, 1)
                if not last:
                    f4.pool(pool, b + 1, 1 - s)
                pool.wait_ge(weights, b * 2 + 2)
                pool.tensor_tensor(nv, e2, v_s[:, s], ALU.mult).then_inc(nv_ready, 1)
            pool.wait_ge(edges, 2)
            batches(pool, lambda b, s: f4.pool(pool, b, s), step)

        def pe_wkv(pe):
            pe.wait_ge(mixture, 7)
            pe.wait_ge(edges, 2)
            pe.sem_inc(kvr_done, 6)

            def kvr(b, s):
                pe.wait_ge(f4.zT_ready, b + 1)
                for n in range(3):
                    for m in range(KC):
                        pe.wait_ge(kvr_kept, b * 6 if n < 2 else b * 6 + m + 1)
                        for k in range(KC):
                            pe.matmul(ps[:, 2 + (2 * n + m) % 4, :], W_PAST[:, n, k, m * P:(m + 1) * P], f4.zT[:, s, k, 0:S],
                                      start=(k == 0), stop=False)
                            mm = pe.matmul(ps[:, 2 + (2 * n + m) % 4, :], W_NOW[:, n, k, m * P:(m + 1) * P], f4.zT[:, s, k, 1:],
                                           start=False, stop=(k == KC - 1))
                        mm.then_inc(kvr_done, 1)

            def out(b, s):
                pe.wait_ge(r_ready, b + 1)
                pe.wait_ge(wo_read, b * 2)
                for t in range(TT):
                    for k in range(KC):
                        mm = pe.matmul(ps[:, 6 + t // 2, (t % 2) * D:(t % 2 + 1) * D], rT[:, s, k, t * P:(t + 1) * P], W_WO[:, k, :],
                                       start=(k == 0), stop=(k == KC - 1))
                    if t % 2:
                        mm.then_inc(wo_done, 1)

            def step(b, s, last):
                if not last:
                    f4.pe(pe, b + 1, 1 - s)
                    kvr(b + 1, 1 - s)
                out(b, s)

            def first(b, s):
                f4.pe(pe, b, s)
                kvr(b, s)
            batches(pe, first, step)

        def act_wkv(act):
            act.wait_ge(w4_in, 48)
            act.activation(wn, vecs[:, 3], ACT.Exp).then_inc(w4_steps, 1)

            def keep(b, s):
                for n, (dst, f, scale) in enumerate(((k_s, ACT.Copy, 1.0), (v_s, ACT.Copy, 1.0), (er_s, ACT.Exp, -1.0))):
                    if n == 0:
                        if not (isinstance(b, int) and b == 0):
                            act.wait_ge(r_ready, b - 1)
                    for m in range(KC):
                        act.wait_ge(kvr_done, b * 6 + 2 * n + m + 1 + 6)
                        act.activation(dst[:, s, m, :], ps[:, 2 + (2 * n + m) % 4, :], f, scale=scale).then_inc(kvr_kept, 1)

            def step(b, s, last):
                act.wait_ge(gaps, b * 3 + 3)
                act.wait_ge(ratio, b * 5)
                act.activation(e1b, gap0, ACT.Exp).then_inc(decays, 1)
                act.activation(e2b, gap1, ACT.Exp, scale=-1.0).then_inc(decays, 1)
                act.wait_ge(scan_p, b * 5 + 5)
                act.activation(e1, dif0, ACT.Exp).then_inc(weights, 1)
                act.activation(e2, dif1, ACT.Exp, scale=-1.0).then_inc(weights, 1)
                if not last:
                    f4.act(act, b + 1, 1 - s, lambda: act.wait_ge(kvr_done, b * 6))
                    keep(b + 1, 1 - s)

            def first(b, s):
                f4.act(act, b, s, lambda: None)
                keep(b, s)
            batches(act, first, step)

        def dve_wkv(dve):
            dve.wait_ge(w4_in, 48)
            dve.tensor_scalar(past, vecs[:, 0:3], -1.0, 1.0, ALU.mult, ALU.add).then_inc(mixture, 1)
            dve.wait_ge(mixture, 1)
            for n in range(3):
                for k in range(KC):
                    dve.tensor_scalar(W_PAST[:, n, k], W_NOW[:, n, k], past[:, n, k:k + 1], None, ALU.mult)
                    dve.drain()
                    dve.tensor_scalar(W_NOW[:, n, k], W_NOW[:, n, k], vecs[:, n, k:k + 1], None, ALU.mult).then_inc(mixture, 1)
            for t, x in ((PPm, -1e38), (AA, 0.0), (BB, 0.0)):
                dve.memset(t[:, :, 0:1], x).then_inc(firsts, 1)
            dve.wait_ge(w4_steps, 1)
            dve.tensor_scalar(wn, wn, -1.0, None, ALU.mult).then_inc(w4_steps, 1)
            dve.memset(decay, 0.0).then_inc(w4_steps, 1)
            dve.wait_ge(w4_steps, 3)
            for k in range(KC):
                dve.tensor_scalar(decay[:, k], decay[:, k], wn[:, k:k + 1], None, ALU.add).then_inc(w4_steps, 1)
            dve.wait_ge(w4_steps, 5)
            dve.wait_ge(firsts, 3)
            u_ = vecs[:, 4]

            def step(b, s, last):
                dve.wait_ge(kvr_kept, b * 6 + 6)
                for k in range(KC):
                    dve.tensor_tensor_scan(PPm[:, k, 1:], decay[:, k], k_s[:, s, k], -1e38, ALU.add, ALU.max).then_inc(scan_p, 1)
                dve.wait_ge(scan_p, b * 5 + 2)
                for k in range(KC):
                    ins = dve.scalar_tensor_tensor(out=gap[:, k], in0=PPm[:, k, 0:S], scalar=wn[:, k:k + 1], in1=k_s[:, s, k], op0=ALU.add, op1=ALU.subtract)
                ins.then_inc(gaps, 1)
                for k in range(KC):
                    ins = dve.scalar_tensor_tensor(out=dif[:, k], in0=PPm[:, k, 0:S], scalar=u_[:, k:k + 1], in1=k_s[:, s, k], op0=ALU.subtract, op1=ALU.subtract)
                ins.then_inc(scan_p, 1)
                dve.wait_ge(gaps, b * 3 + 1)
                dve.wait_ge(decays, b * 2)
                dve.tensor_scalar(gap0, gap, 0.0, None, ALU.min).then_inc(gaps, 1)
                dve.tensor_scalar(gap1, gap, 0.0, None, ALU.max).then_inc(gaps, 1)
                dve.wait_ge(scan_p, b * 5 + 3)
                dve.wait_ge(weights, b * 2)
                dve.tensor_scalar(dif0, dif, 0.0, None, ALU.min).then_inc(scan_p, 1)
                dve.tensor_scalar(dif1, dif, 0.0, None, ALU.max).then_inc(scan_p, 1)
                if not last:
                    f4.dve(dve, b + 1, 1 - s, lambda: None)
                dve.wait_ge(decays, b * 2 + 2)
                for k in range(KC):
                    dve.tensor_tensor_scan(BB[:, k, 1:], e1b[:, k], e2b[:, k], 0.0, ALU.mult, ALU.add).then_inc(scan_ab, 1)
                dve.wait_ge(weights, b * 2 + 2)
                dve.wait_ge(scan_ab, b * 4 + 2)
                dve.tensor_tensor(den, e1, BB[:, :, 0:S], ALU.mult).then_inc(ratio, 1)
                dve.wait_ge(ev_ready, b + 1)
                for k in range(KC):
                    dve.tensor_tensor_scan(AA[:, k, 1:], e1b[:, k], e2v[:, k], 0.0, ALU.mult, ALU.add).then_inc(scan_ab, 1)
                dve.wait_ge(ratio, b * 5 + 1)
                dve.tensor_tensor(den, den, e2, ALU.add).then_inc(ratio, 1)
                dve.wait_ge(scan_ab, b * 4 + 4)
                dve.tensor_tensor(num, e1, AA[:, :, 0:S], ALU.mult).then_inc(ratio, 1)
                dve.wait_ge(ratio, b * 5 + 3)
                for k in range(KC):
                    ins = dve.scalar_tensor_tensor(out=den[:, k], in0=er_s[:, s, k], scalar=1.0, in1=den[:, k], op0=ALU.add, op1=ALU.mult)
                ins.then_inc(ratio, 1)
                dve.wait_ge(nv_ready, b + 1)
                dve.tensor_tensor(num, num, nv, ALU.add).then_inc(ratio, 1)
                dve.wait_ge(ratio, b * 5 + 5)
                dve.reciprocal(rden, den).then_inc(gated, 1)
                dve.wait_ge(gated, b + 1)
                dve.wait_ge(wo_done, b * 2)
                dve.tensor_tensor(rT[:, s], num, rden, ALU.mult).then_inc(r_ready, 1)
                for h in range(2):
                    dve.wait_ge(wo_done, b * 2 + h + 1 + 2)
                    hh = H[:, bass.ds(b * TT + 2 * h, 2), :]
                    dve.tensor_tensor(hh, ps[:, 6 + h, :].rearrange("p (t d) -> p t d", d=D), hh, ALU.add).then_inc(wo_read, 1)
            dve.sem_inc(wo_done, 2)
            batches(dve, lambda b, s: f4.dve(dve, b, s, lambda: None), step)
        gated = sem("gated")

        class Dispatch:

            def __init__(self, name, experts, picks):
                self.E, self.K = experts, picks
                blocks = B * S * picks // P + experts - 1
                self.N = -(-blocks // 4) * 4
                E, K, N = self.E, self.K, self.N
                te = lambda: take(NT * E).rearrange("p (t e) -> p t e", e=E)
                self.logits = te()
                self.rank = te()
                self.chosen = te()
                self.place = te()
                self.total = take(NT * E).rearrange("p (e t) -> p e t", e=E)
                self.run = take(NT * E).rearrange("p (e t) -> p e t", e=E)
                self.nblk = take(E)
                self.start = take(E)
                self.slot = take(NT * K).rearrange("p (t k) -> p t k", k=K)
                self.sloti = take(NT * K, I32).rearrange("p (t k) -> p t k", k=K)
                self.hi = take(NT * K).rearrange("p (t k) -> p t k", k=K)
                self.hii = take(NT * K, I32).rearrange("p (t k) -> p t k", k=K)
                self.lo = take(NT * K).rearrange("p (t k) -> p t k", k=K)
                self.expert = take(N)
                self.experti = take(N, I32)
                self.tokens = take(N, I32)
                self.tokf = take(N)
                self.steps = sem(name + "_steps")
                self.counted = sem(name + "_counted")
                self.hot_ready = sem(name + "_hot_ready")
                self.hot_scaled = sem(name + "_hot_scaled")
                self.listed = sem(name + "_listed")
                self.table = sem(name + "_table")
                self.n = 0

            def temps(self):
                E, K, N = self.E, self.K, self.N
                self.wide = take(max(N * E, NT * E * (E if K > 1 else 1)))
                self.hot_lo = take(2 * K * P, BF16).rearrange("p (s k n) -> p s k n", s=2, k=K)
                self.hot_hi = take(2 * K * N, BF16).rearrange("p (s k n) -> p s k n", s=2, k=K)
                self.hot_t = take(2 * 2 * K * N, BF16).rearrange("p (s k c n) -> p s k c n", s=2, k=K, c=2)

            def link(self, dve, ins):
                self.n += 1
                ins.then_inc(self.steps, 1)
                dve.wait_ge(self.steps, self.n)

            def dve(self, dve):
                E, K, N = self.E, self.K, self.N
                link = lambda ins: self.link(dve, ins)
                dve.wait_ge(self.counted, 1)
                link(dve.tensor_copy(self.total, ps[:, 1, 0:NT * E].rearrange("p (t e) -> p e t", e=E) if NT * E <= 512 else
                                     ps[:, 2:4, :].rearrange("p a (t e) -> p e (a t)", e=E)))
                link(dve.tensor_tensor_scan(self.run.rearrange("p e t -> p (e t)"), later[:, 0:NT * E],
                                            self.total.rearrange("p e t -> p (e t)"), 0.0, ALU.mult, ALU.add))
                wide = self.wide[:, 0:E * NT].rearrange("p (e t) -> p e t", e=E)
                link(dve.tensor_tensor(wide, self.run[:, :, NT - 1:NT].to_broadcast((P, E, NT)),
                                       tiles128.unsqueeze(1).to_broadcast((P, E, NT)), ALU.is_gt))
                link(dve.tensor_reduce(self.nblk, wide, AX.X, ALU.add))
                link(dve.tensor_tensor_scan(self.start, onesr[:, 0:E], self.nblk, 0.0, ALU.mult, ALU.add))
                link(dve.tensor_tensor(self.start, self.start, self.nblk, ALU.subtract))
                wide = self.wide[:, 0:N * E].rearrange("p (n e) -> p n e", e=E)
                link(dve.tensor_tensor(wide, self.start.unsqueeze(1).to_broadcast((P, N, E)),
                                       count[:, 0:N].unsqueeze(2).to_broadcast((P, N, E)), ALU.is_le))
                link(dve.tensor_reduce(self.expert, wide, AX.X, ALU.add))
                link(dve.tensor_scalar(self.expert, self.expert, -1.0, None, ALU.add))
                link(dve.tensor_copy(self.experti, self.expert))
                link(dve.tensor_tensor(self.run, self.run, self.total, ALU.subtract))
                link(dve.tensor_scalar(self.start, self.start, float(P), None, ALU.mult))
                link(dve.tensor_tensor(self.run, self.run, self.start.unsqueeze(2).to_broadcast((P, E, NT)), ALU.add))
                within = ps[:, 0, 0:NT * E].rearrange("p (t e) -> p t e", e=E) if NT * E <= 512 else None
                if within is not None:
                    link(dve.tensor_tensor(self.place, within, self.run.rearrange("p e t -> p t e"), ALU.add))
                else:
                    for h in range(2):
                        link(dve.tensor_tensor(self.place[:, h * NT // 2:(h + 1) * NT // 2, :], ps[:, h, :].rearrange("p (t e) -> p t e", e=E),
                                               self.run.rearrange("p e t -> p t e")[:, h * NT // 2:(h + 1) * NT // 2, :], ALU.add))
                wide = self.wide[:, 0:NT * E].rearrange("p (t e) -> p t e", e=E)
                for k in range(K):
                    if K > 1:
                        link(dve.scalar_tensor_tensor(out=wide, in0=self.rank, scalar=float(k), in1=self.place, op0=ALU.is_equal, op1=ALU.mult))
                    else:
                        link(dve.tensor_tensor(wide, self.chosen, self.place, ALU.mult))
                    link(dve.tensor_reduce(self.slot[:, :, k], wide, AX.X, ALU.add))
                link(dve.tensor_copy(self.sloti, self.slot))
                link(dve.tensor_scalar(self.hii, self.sloti, 7, None, ALU.arith_shift_right))
                link(dve.tensor_copy(self.hi, self.hii))
                link(dve.scalar_tensor_tensor(out=self.lo, in0=self.hi, scalar=-float(P), in1=self.slot, op0=ALU.mult, op1=ALU.add))
                with dve.Fori(0, NT // 2) as pair:
                    for s in range(2):
                        t = pair * 2 + s
                        dve.wait_ge(self.listed, t)
                        dve.tensor_tensor(self.hot_lo[:, s], countb[:, 0:P].unsqueeze(1).to_broadcast((P, K, P)),
                                          self.lo[:, bass.ds(t, 1), :].rearrange("p a k -> p (a k)").unsqueeze(2).to_broadcast((P, K, P)),
                                          ALU.is_equal)
                        dve.tensor_tensor(self.hot_hi[:, s], countb[:, 0:N].unsqueeze(1).to_broadcast((P, K, N)),
                                          self.hi[:, bass.ds(t, 1), :].rearrange("p a k -> p (a k)").unsqueeze(2).to_broadcast((P, K, N)),
                                          ALU.is_equal).then_inc(self.hot_ready, 1)
                dve.wait_ge(self.listed, NT + 1)
                c = [ps[:, 4, 0:N], ps[:, 5, 0:N]]
                link(dve.tensor_copy(self.tokf, c[1]))
                link(dve.scalar_tensor_tensor(out=self.tokf, in0=self.tokf, scalar=float(P), in1=c[0], op0=ALU.mult, op1=ALU.add))
                dve.tensor_copy(self.tokens, self.tokf).then_inc(self.table, 1)

            def act(self, act):
                with act.Fori(0, NT // 2) as pair:
                    for s in range(2):
                        t = pair * 2 + s
                        act.wait_ge(self.hot_ready, t + 1)
                        act.activation(self.hot_t[:, s, :, 0, :], self.hot_hi[:, s], ACT.Copy, scale=row_of)
                        act.activation(self.hot_t[:, s, :, 1, :], self.hot_hi[:, s], ACT.Copy, scale=tile_of[:, bass.ds(t, 1)]).then_inc(self.hot_scaled, 1)

            def pe(self, pe, ready, n):
                E, K, N = self.E, self.K, self.N
                pe.wait_ge(ready, n)
                flat = self.chosen.rearrange("p t e -> p (t e)")
                parts = NT * E // 512
                for h in range(parts):
                    pe.matmul(ps[:, h, :], before, flat[:, h * 512:(h + 1) * 512], start=True, stop=True)
                for h in range(parts):
                    mm = pe.matmul(ps[:, (1 if parts == 1 else 2 + h), :], ones, flat[:, h * 512:(h + 1) * 512], start=True, stop=True)
                mm.then_inc(self.counted, 1)
                for c in range(2):
                    pe.matmul(ps[:, 4 + c, 0:N], zerob, identb_wide[:, 0:N], start=True, stop=False, skip_group_check=True)
                pe.sem_inc(self.listed, 1)
                with pe.Fori(0, NT // 2) as pair:
                    for s in range(2):
                        t = pair * 2 + s
                        pe.wait_ge(self.hot_scaled, t + 1)
                        for k in range(K):
                            for c in range(2):
                                mm = pe.matmul(ps[:, 4 + c, 0:N], self.hot_lo[:, s, k, :], self.hot_t[:, s, k, c, :], start=False, stop=False,
                                               skip_group_check=True)
                        mm.then_inc(self.listed, 1)


        def blocks(e, n, step):
            for i in range(4):
                step(i, i, lambda m: m >= 0)
            with e.Fori(1, n // 4) as quad:
                for s in range(4):
                    step(quad * 4 + s, s, lambda m: True)
            for i in range(n, n + 3):
                step(i, i % 4, lambda m: m < n)

        class Gather:

            def __init__(self, name, d, source):
                self.d, self.source = d, source
                self.x = take(4 * D).rearrange("p (s d) -> p s d", s=4)
                self.at = take(4, I32)
                self.xT = take(4 * KC * P).rearrange("p (s k t) -> p s k t", s=4, k=KC)
                self.at_ready = sem(name + "_at_ready")
                self.x_in = [sem(f"{name}_x_in{s}") for s in range(4)]
                self.turned = sem(name + "_x_turned")
                self.ready = sem(name + "_xT_ready")

            def pool(self, pool):
                pool.wait_ge(self.d.table, 1)
                with pool.Fori(0, self.d.N // 4) as quad:
                    for s in range(4):
                        pool.wait_ge(self.x_in[s], quad * 16)
                        pool.tensor_copy(self.at[:, s:s + 1], self.d.tokens[:, bass.ds(quad * 4 + s, 1)]).then_inc(self.at_ready, 1)
                        pool.wait_ge(self.at_ready, quad * 4 + s + 1)
                        pool.wait_ge(self.turned, quad * 4 + s + 1)
                        alone(pool)
                        pool.indirect_dma_start(out=self.x[:, s, :], out_offset=None, in_=self.source,
                                                in_offset=bass.IndirectOffsetOnAxis(ap=self.at[:, s:s + 1].bitcast(U32), axis=0)
                                                ).then_inc(self.x_in[s], 16)

            def pe(self, pe, i, s):
                pe.wait_ge(self.x_in[s], (i - s) * 4 + 16)
                pe.wait_ge(self.ready, i + 1)
                for k in range(KC):
                    mm = pe.transpose(ps[:, s % 2, k * P:(k + 1) * P], self.x[:, s, k * P:(k + 1) * P], ident)
                mm.then_inc(self.turned, 1)

            def act(self, act, i, s, used, n):
                act.wait_ge(self.turned, i + 1 + 4)
                act.wait_ge(used, n)
                act.activation(self.xT[:, s].rearrange("p k t -> p (k t)"), ps[:, s % 2, 0:KC * P], ACT.Copy).then_inc(self.ready, 1)

        free[0] = PERSIST
        E5, K5, INTER = 16, 4, 128
        GROUPS5, PER5 = 4, 4
        W_GU = take(KC * E5 * 2 * INTER).rearrange("p (k e m) -> p k e m", k=KC, e=E5)
        W_D = take(E5 * D).rearrange("p (e d) -> p e d", e=E5)
        consts = take(1280)
        later, tiles128, onesr, count, tile_of = (consts[:, x:y] for x, y in ((0, 1024), (1024, 1056), (1056, 1088), (1088, 1248), (1248, 1280)))
        before = take(P)
        ones = take(P)
        row_of = take(1)
        countb = take(160, BF16)
        zerob = take(P, BF16)
        identb_wide = countb
        CONST_END = mark()
        d5 = Dispatch("moe", E5, K5)
        weight = take(NT * K5).rearrange("p (t k) -> p t k", k=K5)
        e_bias = take(E5)
        STAGE5 = mark()
        W_R = take(KC * E5).rearrange("p (k e) -> p k e", k=KC)
        W_SG, W_SU, W_SD = (take(KC * D).rearrange("p (k d) -> p k d", k=KC) for _ in range(3))
        f5 = Front("moe")
        z_dram = nc.dram_tensor("z_dram", (B * S, D), F32, kind="Internal").ap()
        sg = take(2 * S).rearrange("p (m t) -> p m t", m=2)
        shT = take(2 * KC * S).rearrange("p (s m t) -> p s m t", s=2, m=KC)
        w5_in = sem("w5_in")
        wx5_in = sem("wx5_in")
        z_out = [sem(f"z_out{s}") for s in range(2)]
        lg_done = sem("lg_done")
        lg_read = sem("lg_read")
        gate_done = sem("gate_done")
        up5_done = sem("up5_done")
        silu_done = sem("silu_done")
        sh_ready = sem("sh_ready")
        sd_done = sem("sd_done")
        sd_read = sem("sd_read")

        def sp_shared(sp):
            for dst, name in ((W_R, "w_r"), (W_SG, "w_sg"), (W_SU, "w_su"), (W_SD, "w_sd"), (before, "before"), (row_of, "row_of")):
                sp.dma_start(dst, a[name]).then_inc(w5_in, 16)
            sp.dma_start(consts, a["consts"].to_broadcast((P, 1280))).then_inc(w5_in, 16)
            sp.dma_start(e_bias, a["e_bias"].to_broadcast((P, E5))).then_inc(w5_in, 16)
            for dst, name in ((W_GU, "w_gu"), (W_D, "w_d")):
                sp.dma_start(dst, a[name]).then_inc(wx5_in, 16)
            with sp.Fori(0, B // 2) as pair:
                for s in range(2):
                    b = pair * 2 + s
                    sp.wait_ge(f5.z_ready, b + 1)
                    sp.dma_start(z_dram[bass.ds(b * S, S), :].rearrange("(t p) d -> p t d", p=P), f5.z[:, s]).then_inc(z_out[s], 16)
            for s in range(2):
                sp.wait_ge(z_out[s], 16 * (B // 2))

        def pool_shared(pool):
            pool.memset(ones, 1.0)

            def step(b, s, last):
                if not last:
                    f5.pool(pool, b + 1, 1 - s)
            batches(pool, lambda b, s: f5.pool(pool, b, s), step)

        def pe_shared(pe):
            pe.wait_ge(w5_in, 16 * 8)
            pe.sem_inc(sd_done, 2)

            def step(b, s, last):
                zT = f5.zT
                pe.wait_ge(f5.zT_ready, b + 1)
                pe.wait_ge(lg_read, b)
                for t in range(TT):
                    for k in range(KC):
                        mm = pe.matmul(ps[:, 5, t * E5:(t + 1) * E5], zT[:, s, k, t * P:(t + 1) * P], W_R[:, k, :], start=(k == 0), stop=(k == KC - 1))
                mm.then_inc(lg_done, 1)
                for m in range(KC):
                    pe.wait_ge(silu_done, b * 2)
                    for k in range(KC):
                        mm = pe.matmul(ps[:, 2 + 2 * m, :], W_SG[:, k, m * P:(m + 1) * P], zT[:, s, k, :], start=(k == 0), stop=(k == KC - 1))
                    mm.then_inc(gate_done, 1)
                    pe.wait_ge(sh_ready, b * 2 + m)
                    for k in range(KC):
                        mm = pe.matmul(ps[:, 3, :], W_SU[:, k, m * P:(m + 1) * P], zT[:, s, k, :], start=(k == 0), stop=(k == KC - 1))
                    mm.then_inc(up5_done, 1)
                if not last:
                    f5.pe(pe, b + 1, 1 - s)
                pe.wait_ge(sh_ready, b * 2 + 2)
                pe.wait_ge(sd_read, b * 2)
                for t in range(TT):
                    for k in range(KC):
                        mm = pe.matmul(ps[:, 6 + t // 2, (t % 2) * D:(t % 2 + 1) * D], shT[:, s, k, t * P:(t + 1) * P], W_SD[:, k, :],
                                       start=(k == 0), stop=(k == KC - 1))
                    if t % 2:
                        mm.then_inc(sd_done, 1)
            batches(pe, lambda b, s: f5.pe(pe, b, s), step)

        def act_shared(act):
            def step(b, s, last):
                for m in range(KC):
                    act.wait_ge(gate_done, b * 2 + m + 1)
                    act.wait_ge(sh_ready, b * 2)
                    act.activation(sg[:, m, :], ps[:, 2 + 2 * m, :], ACT.Silu).then_inc(silu_done, 1)
                if not last:
                    f5.act(act, b + 1, 1 - s, lambda: act.wait_ge(up5_done, b * 2))
            batches(act, lambda b, s: f5.act(act, b, s, lambda: None), step)

        def dve_shared(dve):
            dve.memset(zerob, 0.0)
            dve.wait_ge(w5_in, 16 * 8)
            dve.tensor_copy(countb, count)

            def step(b, s, last):
                if not last:
                    def slot_free():
                        dve.wait_ge(f5.turned, b)
                        dve.wait_ge(z_out[1 - s], b * 8 if s == 0 else (b - 1) * 8 + 16)
                    f5.dve(dve, b + 1, 1 - s, slot_free)
                dve.wait_ge(lg_done, b + 1)
                dve.tensor_copy(d5.logits[:, bass.ds(b * TT, TT), :], ps[:, 5, 0:TT * E5].rearrange("p (t e) -> p t e", e=E5)).then_inc(lg_read, 1)
                for m in range(KC):
                    dve.wait_ge(up5_done, b * 2 + m + 1)
                    dve.wait_ge(silu_done, b * 2 + m + 1)
                    dve.wait_ge(sd_done, b * 2)
                    dve.tensor_tensor(shT[:, s, m, :], sg[:, m, :], ps[:, 3, :], ALU.mult).then_inc(sh_ready, 1)
                for h in range(2):
                    dve.wait_ge(sd_done, b * 2 + h + 1 + 2)
                    hh = H[:, bass.ds(b * TT + 2 * h, 2), :]
                    dve.tensor_tensor(hh, ps[:, 6 + h, :].rearrange("p (t d) -> p t d", d=D), hh, ALU.add).then_inc(sd_read, 1)
            batches(dve, lambda b, s: f5.dve(dve, b, s, lambda: None), step)

        free[0] = STAGE5
        d5.temps()
        sc = take(NT * E5).rearrange("p (t e) -> p t e", e=E5)
        pairs = take(NT * GROUPS5 * 6).rearrange("p (t g n) -> p t g n", g=GROUPS5, n=6)
        gsum = take(NT * GROUPS5).rearrange("p (t g) -> p t g", g=GROUPS5)
        gcmp = take(NT * GROUPS5 * GROUPS5).rearrange("p (t g n) -> p t g n", g=GROUPS5, n=GROUPS5)
        grank = take(NT * GROUPS5).rearrange("p (t g) -> p t g", g=GROUPS5)
        wsum = take(NT)
        scores_ready = sem("scores_ready")
        chosen5 = sem("chosen5")

        def sp_route5(sp):
            sp.wait_ge(wx5_in, 32)

        def pool_route5(pool):
            pass

        def act_route5(act):
            act.activation(d5.logits.rearrange("p t e -> p (t e)"), d5.logits.rearrange("p t e -> p (t e)"), ACT.Sigmoid).then_inc(scores_ready, 1)
            d5.act(act)

        def pe_route5(pe):
            d5.pe(pe, chosen5, 1)

        def ranks(link, dve, values, compared, rank, n):
            for j in range(n):
                v = values[:, :, j:j + 1]
                dve.tensor_tensor(compared[:, :, 0:j + 1, j], v.to_broadcast((P, NT, j + 1)), values[:, :, 0:j + 1], ALU.is_gt)
                if j < n - 1:
                    dve.tensor_tensor(compared[:, :, j + 1:n, j], v.to_broadcast((P, NT, n - 1 - j)), values[:, :, j + 1:n], ALU.is_ge)
            link(dve.drain())
            link(dve.tensor_reduce(rank, compared, AX.X, ALU.add))

        def dve_route5(dve):
            link = lambda ins: d5.link(dve, ins)
            dve.wait_ge(scores_ready, 1)
            link(dve.tensor_tensor(sc, d5.logits, e_bias.unsqueeze(1).to_broadcast((P, NT, E5)), ALU.add))
            g4 = sc.rearrange("p t (g i) -> p (t g) i", i=PER5)
            flat = pairs.rearrange("p t g n -> p (t g) n")
            n = 0
            for i in range(PER5):
                for j in range(i + 1, PER5):
                    ins = dve.tensor_tensor(flat[:, :, n], g4[:, :, i], g4[:, :, j], ALU.add)
                    n += 1
            link(dve.drain())
            link(dve.tensor_reduce(gsum, pairs, AX.X, ALU.max))
            ranks(link, dve, gsum, gcmp, grank, GROUPS5)
            link(dve.tensor_scalar(grank, grank, 2.0, None, ALU.is_lt))
            link(dve.tensor_tensor(sc.rearrange("p t (g i) -> p (t g) i", i=PER5), sc.rearrange("p t (g i) -> p (t g) i", i=PER5),
                                   grank.rearrange("p t g -> p (t g)").unsqueeze(2).to_broadcast((P, NT * GROUPS5, PER5)), ALU.mult))
            ranks(link, dve, sc, d5.wide.rearrange("p (t g n) -> p t g n", g=E5, n=E5), d5.rank, E5)
            dve.tensor_scalar(d5.chosen, d5.rank, float(K5), None, ALU.is_lt).then_inc(chosen5, 1)
            dve.wait_ge(chosen5, 1)
            link(dve.tensor_tensor(sc, d5.logits, d5.chosen, ALU.mult))
            link(dve.tensor_reduce(wsum, sc, AX.X, ALU.add))
            link(dve.tensor_scalar(wsum, wsum, 1e-20, None, ALU.add))
            link(dve.reciprocal(wsum, wsum))
            link(dve.tensor_tensor(sc, sc, wsum.unsqueeze(2).to_broadcast((P, NT, E5)), ALU.mult))
            link(dve.tensor_scalar(sc, sc, 2.5, None, ALU.mult))
            wide = d5.wide[:, 0:NT * E5].rearrange("p (t e) -> p t e", e=E5)
            for k in range(K5):
                link(dve.scalar_tensor_tensor(out=wide, in0=d5.rank, scalar=float(k), in1=sc, op0=ALU.is_equal, op1=ALU.mult))
                link(dve.tensor_reduce(weight[:, :, k], wide, AX.X, ALU.add))
            d5.dve(dve)

        free[0] = STAGE5
        g7 = Gather("moe", d5, z_dram)
        sg7 = take(4 * INTER).rearrange("p (s i) -> p s i", s=4)
        h7 = take(4 * INTER).rearrange("p (s i) -> p s i", s=4)
        hT7 = take(4 * P).rearrange("p (s t) -> p s t", s=4)
        y7 = take(4 * D).rearrange("p (s d) -> p s d", s=4)
        y_dram = nc.dram_tensor("y_dram", (d5.N * P, D), F32, kind="Internal").ap()
        gu_done = sem("gu_done")
        silu7 = sem("silu7")
        h7_ready = sem("h7_ready")
        h7_turned = sem("h7_turned")
        hT7_ready = sem("hT7_ready")
        dn_done = sem("dn_done")
        y7_ready = sem("y7_ready")
        y7_out = [sem(f"y7_out{s}") for s in range(4)]
        NB7 = d5.N

        def sp_experts(sp):
            with sp.Fori(0, NB7 // 4) as quad:
                for s in range(4):
                    sp.wait_ge(y7_ready, quad * 4 + s + 1 + 2)
                    sp.dma_start(y_dram[bass.ds((quad * 4 + s) * P, P), :], y7[:, s, :]).then_inc(y7_out[s], 16)
            for s in range(4):
                sp.wait_ge(y7_out[s], 16 * (NB7 // 4))

        def pool_experts(pool):
            g7.pool(pool)

        def pe_experts(pe):
            pe.sem_inc(g7.turned, 4)
            pe.sem_inc(gu_done, 4)

            def expert(n):
                return pe.value_load(d5.experti[0:1, bass.ds(n, 1)], min_val=0, max_val=E5 - 1)

            def step(i, s, there):
                if there(i):
                    g7.pe(pe, i, s)
                if there(i - 1):
                    c = (s - 1) % 4
                    e = expert(i - 1)
                    pe.wait_ge(g7.ready, i + 2)
                    pe.wait_ge(h7_ready, i)
                    for k in range(KC):
                        mm = pe.matmul(ps[:, 2 + c % 2, 0:2 * INTER], g7.xT[:, c, k, :], W_GU[:, k, bass.ds(e, 1), :].rearrange("p a m -> p (a m)"),
                                       start=(k == 0), stop=(k == KC - 1))
                    mm.then_inc(gu_done, 1)
                if there(i - 2):
                    c = (s - 2) % 4
                    pe.wait_ge(h7_ready, i - 1 + 2)
                    pe.wait_ge(hT7_ready, i - 1)
                    pe.transpose(ps[:, 4 + c % 2, 0:P], h7[:, c, :], ident).then_inc(h7_turned, 1)
                if there(i - 3):
                    c = (s - 3) % 4
                    e = expert(i - 3)
                    pe.wait_ge(hT7_ready, i - 2 + 2)
                    pe.wait_ge(y7_ready, i - 2)
                    pe.matmul(ps[:, 6 + c % 2, 0:D], hT7[:, c, :], W_D[:, bass.ds(e, 1), :].rearrange("p a d -> p (a d)"),
                              start=True, stop=True).then_inc(dn_done, 1)
            blocks(pe, NB7, step)

        def act_experts(act):
            act.sem_inc(g7.ready, 2)

            def step(i, s, there):
                if there(i):
                    g7.act(act, i, s, gu_done, i + 1)
                if there(i - 1):
                    c = (s - 1) % 4
                    act.wait_ge(gu_done, i + 4)
                    act.wait_ge(h7_ready, i - 2 if not isinstance(i, int) or i >= 2 else 0)
                    act.activation(sg7[:, c, :], ps[:, 2 + c % 2, 0:INTER], ACT.Silu).then_inc(silu7, 1)
            blocks(act, NB7, step)

        def dve_experts(dve):
            for x in (h7_ready, hT7_ready, y7_ready):
                dve.sem_inc(x, 2)
            dve.sem_inc(h7_turned, 4)

            def step(i, s, there):
                if there(i - 1):
                    c = (s - 1) % 4
                    dve.wait_ge(silu7, i)
                    dve.wait_ge(h7_turned, i)
                    dve.tensor_tensor(h7[:, c, :], sg7[:, c, :], ps[:, 2 + c % 2, INTER:2 * INTER], ALU.mult).then_inc(h7_ready, 1)
                if there(i - 2):
                    c = (s - 2) % 4
                    dve.wait_ge(h7_turned, i - 1 + 4)
                    dve.tensor_copy(hT7[:, c, :], ps[:, 4 + c % 2, 0:P]).then_inc(hT7_ready, 1)
                if there(i - 3):
                    c = (s - 3) % 4
                    dve.wait_ge(dn_done, i - 2)
                    dve.wait_ge(y7_out[c], (i - 3 - c) * 4)
                    dve.tensor_copy(y7[:, c, :], ps[:, 6 + c % 2, 0:D]).then_inc(y7_ready, 1)
            blocks(dve, NB7, step)

        back = take(2 * K5 * D).rearrange("p (s k d) -> p s k d", s=2, k=K5)
        at8 = take(2 * K5, I32).rearrange("p (s k) -> p s k", s=2)
        at8_ready = sem("at8_ready")
        back_in = [[sem(f"back_in{s}{k}") for k in range(K5)] for s in range(2)]
        added = sem("added")

        def sp_combine(sp):
            pass

        def pool_combine(pool):
            with pool.Fori(0, NT // 2) as pair:
                for s in range(2):
                    t = pair * 2 + s
                    pool.wait_ge(added, t * K5)
                    pool.tensor_copy(at8[:, s, :], d5.sloti[:, bass.ds(t, 1), :].rearrange("p a k -> p (a k)")).then_inc(at8_ready, 1)
                    pool.wait_ge(at8_ready, t + 1)
                    alone(pool)
                    for k in range(K5):
                        pool.indirect_dma_start(out=back[:, s, k, :], out_offset=None, in_=y_dram,
                                                in_offset=bass.IndirectOffsetOnAxis(ap=at8[:, s, k:k + 1].bitcast(U32), axis=0)
                                                ).then_inc(back_in[s][k], 16)

        def dve_combine(dve):
            dve.sem_inc(added, K5)
            with dve.Fori(0, NT // 2) as pair:
                for s in range(2):
                    t = pair * 2 + s
                    h = H[:, bass.ds(t, 1), :].rearrange("p a d -> p (a d)")
                    for k in range(K5):
                        dve.wait_ge(back_in[s][k], pair * 16 + 16)
                        dve.wait_ge(added, t * K5 + k + K5)
                        dve.scalar_tensor_tensor(out=h, in0=back[:, s, k, :], scalar=weight[:, bass.ds(t, 1), k:k + 1].rearrange("p a k -> p (a k)"),
                                                 in1=h, op0=ALU.mult, op1=ALU.add).then_inc(added, 1)

        def nothing(e):
            pass

        run([(sp_embed, pool_embed, act_embed, dve_embed, pe_embed),
             (sp_attn, pool_attn, act_attn, dve_attn, pe_attn),
             (sp_ff, pool_ff, act_ff, dve_ff, pe_ff),
             (sp_wkv, pool_wkv, act_wkv, dve_wkv, pe_wkv),
             (sp_shared, pool_shared, act_shared, dve_shared, pe_shared),
             (sp_route5, pool_route5, act_route5, dve_route5, pe_route5),
             (sp_experts, pool_experts, act_experts, dve_experts, pe_experts),
             (nothing, pool_combine, nothing, dve_combine, nothing)][:stop])

        passed[0] = sem("passed2")

        free[0] = CONST_END
        HH = NH // KC
        NORM = P + HH
        W_QKV = take(KC * 3 * D).rearrange("p (k m) -> p k m", k=KC)
        W_OUT = take(KC * D).rearrange("p (k d) -> p k d", k=KC)
        qk_gain = take(2 * D)
        b_out = take(D)
        same_head = take(P)
        head_of = take(HH)
        mhalf8 = take(2 * TT).rearrange("p (t n) -> p t n", n=2)
        f9 = Front("lin")
        qk9 = take(2 * TT * 2 * D).rearrange("p (s t m) -> p s t m", s=2, t=TT)
        v9 = take(2 * TT * KC * (P + 2)).rearrange("p (s t c m) -> p s t c m", s=2, t=TT, c=KC)
        squares = take(2 * D).rearrange("p (n d) -> p n d", n=2)
        ssq = take(2 * TT * 2).rearrange("p (s t n) -> p s t n", s=2, t=TT)
        kv9 = take(2 * KC * NORM).rearrange("p (s c m) -> p s c m", s=2, c=KC)
        qT9 = take(KC * S).rearrange("p (c t) -> p c t", c=KC)
        att9 = take(TT * D).rearrange("p (t d) -> p t d", d=D)
        attT9 = take(KC * S).rearrange("p (c t) -> p c t", c=KC)
        norm9 = take(2 * NH).rearrange("p (s c h) -> p s c h", s=2, c=KC)
        w9_in = sem("w9_in")
        ones9 = sem("ones9")
        qkv_done = sem("qkv_done")
        qkv_kept = sem("qkv_kept")
        squared = sem("squared")
        rms_steps = sem("rms_steps")
        scaled9 = sem("scaled9")
        relu9 = sem("relu9")
        kv_done = sem("kv_done")
        kv_ready = sem("kv_ready")
        q_turned = sem("q_turned")
        qT_ready = sem("qT_ready")
        att_done = sem("att_done")
        norm_steps = sem("norm_steps")
        att_ready = sem("att_ready")
        att_turned = sem("att_turned")
        attT_ready = sem("attT_ready")
        proj_done = sem("proj_done")
        proj_read = sem("proj_read")
        biased9 = sem("biased9")

        def sp_linear(sp):
            for dst, name in ((W_QKV, "w_qkv"), (W_OUT, "w_out"), (same_head, "same_head"), (head_of, "head_of")):
                sp.dma_start(dst, a[name]).then_inc(w9_in, 16)
            sp.dma_start(qk_gain, a["qk_gain"].to_broadcast((P, 2 * D))).then_inc(w9_in, 16)
            sp.dma_start(b_out, a["b_out"].to_broadcast((P, D))).then_inc(w9_in, 16)

        def pool_linear(pool):
            pool.memset(mhalf8, -0.5).then_inc(ones9, 1)
            pool.wait_ge(ones9, 1)
            pool.memset(v9[:, :, :, :, P:P + 1].rearrange("p s t c m -> p (s t c) m"), 1.0).then_inc(ones9, 1)
            pool.wait_ge(w9_in, 96)

            def bias(b, s):
                pool.wait_ge(proj_read, b * 2 + 2)
                h = H[:, bass.ds(b * TT, TT), :]
                pool.tensor_tensor(h, h, b_out.unsqueeze(1).to_broadcast((P, TT, D)), ALU.add).then_inc(biased9, 1)

            def step(b, s, last):
                if not last:
                    f9.pool(pool, b + 1, 1 - s)
                pool.wait_ge(squared, b * TT * 2 + TT * 2)
                alone(pool)
                pool.tensor_scalar(ssq[:, s], ssq[:, s], 1.0 / D, 1e-6, ALU.mult, ALU.add).then_inc(rms_steps, 1)
                pool.wait_ge(rms_steps, b * 2 + 1)
                pool.tensor_tensor(ssq[:, s], ssq[:, s], mhalf8, ALU.pow).then_inc(rms_steps, 1)
                bias(b, s)
            batches(pool, lambda b, s: f9.pool(pool, b, s), step)

        def pe_linear(pe):
            pe.wait_ge(w9_in, 96)

            def step(b, s, last):
                zT = f9.zT
                pe.wait_ge(f9.zT_ready, b + 1)
                for t in range(TT):
                    n = 2 + 2 * (t % 2)
                    pe.wait_ge(qkv_kept, b * TT + t - 1 if t >= 2 else b * TT)
                    if t == 0:
                        pe.wait_ge(qT_ready, b)
                        pe.wait_ge(attT_ready, b)
                    for k in range(KC):
                        pe.matmul(ps[:, n, :], zT[:, s, k, t * P:(t + 1) * P], W_QKV[:, k, 0:2 * D], start=(k == 0), stop=(k == KC - 1))
                    for k in range(KC):
                        mm = pe.matmul(ps[:, n + 1, 0:D], zT[:, s, k, t * P:(t + 1) * P], W_QKV[:, k, 2 * D:3 * D], start=(k == 0), stop=(k == KC - 1))
                    mm.then_inc(qkv_done, 1)
                if not last:
                    f9.pe(pe, b + 1, 1 - s)
                pe.wait_ge(relu9, b + 1)
                pe.wait_ge(qkv_kept, b * TT + TT)
                for t in range(TT):
                    for c in range(KC):
                        mm = pe.transpose(ps[:, 2 + c, t * P:(t + 1) * P], qk9[:, s, t, c * P:(c + 1) * P], ident)
                mm.then_inc(q_turned, 1)
                pe.wait_ge(proj_read, b * 2)
                for c in range(KC):
                    for t in range(TT):
                        mm = pe.matmul(ps[:, 6, c * 160:c * 160 + P + 1], qk9[:, s, t, D + c * P:D + (c + 1) * P], v9[:, s, t, c, 0:P + 1],
                                       start=(t == 0), stop=(t == TT - 1))
                mm.then_inc(kv_done, 1)
                pe.wait_ge(kv_ready, b + 1)
                pe.wait_ge(qT_ready, b + 1)
                for t in range(TT):
                    if t >= 2:
                        pe.wait_ge(att_ready, b * TT + t - 1)
                    for c in range(KC):
                        mm = pe.matmul(ps[:, 7 - t % 2, c * 160:c * 160 + NORM], qT9[:, c, t * P:(t + 1) * P], kv9[:, s, c, :], start=True, stop=True)
                    mm.then_inc(att_done, 1)
                for t in range(TT):
                    pe.wait_ge(att_ready, b * TT + t + 1)
                    for c in range(KC):
                        mm = pe.transpose(ps[:, 4 + c, t * P:(t + 1) * P], att9[:, t, c * P:(c + 1) * P], ident)
                mm.then_inc(att_turned, 1)
                pe.wait_ge(attT_ready, b + 1)
                for t in range(TT):
                    for c in range(KC):
                        mm = pe.matmul(ps[:, 6 + t // 2, (t % 2) * D:(t % 2 + 1) * D], attT9[:, c, t * P:(t + 1) * P], W_OUT[:, c, :],
                                       start=(c == 0), stop=(c == KC - 1))
                    if t % 2:
                        mm.then_inc(proj_done, 1)
            batches(pe, lambda b, s: f9.pe(pe, b, s), step)

        def act_linear(act):
            def step(b, s, last):
                for t in range(TT):
                    act.wait_ge(qkv_kept, b * TT + t + 1)
                    act.wait_ge(squared, (b * TT + t) * 2)
                    if t == 0:
                        act.wait_ge(relu9, b)
                    for n in range(2):
                        act.activation(squares[:, n], qk9[:, s, t, n * D:(n + 1) * D], ACT.Square,
                                       accum_out=ssq[:, s, t, n:n + 1]).then_inc(squared, 1)
                if not last:
                    f9.act(act, b + 1, 1 - s, lambda: act.wait_ge(qkv_done, b * TT))
                act.wait_ge(q_turned, b + 1)
                act.wait_ge(proj_done, b * 2)
                act.activation(qT9, ps[:, 2:4, :], ACT.Copy).then_inc(qT_ready, 1)
                act.wait_ge(att_turned, b + 1)
                act.activation(attT9, ps[:, 4:6, :], ACT.Copy).then_inc(attT_ready, 1)
            batches(act, lambda b, s: f9.act(act, b, s, lambda: None), step)

        def dve_linear(dve):
            dve.wait_ge(w9_in, 96)
            dve.wait_ge(ones9, 2)

            def step(b, s, last):
                for t in range(TT):
                    dve.wait_ge(qkv_done, b * TT + t + 1)
                    n = 2 + 2 * (t % 2)
                    dve.tensor_copy(qk9[:, s, t, :], ps[:, n, :])
                    dve.tensor_copy(v9[:, s, t, :, 0:P], ps[:, n + 1, 0:D].rearrange("p (c m) -> p c m", c=KC)).then_inc(qkv_kept, 1)
                if not last:
                    f9.dve(dve, b + 1, 1 - s, lambda: dve.wait_ge(f9.turned, b))
                dve.wait_ge(rms_steps, b * 2 + 2)
                dve.wait_ge(qkv_kept, b * TT + TT)
                for t in range(TT):
                    for n in range(2):
                        x = qk9[:, s, t, n * D:(n + 1) * D]
                        ins = dve.scalar_tensor_tensor(out=x, in0=x, scalar=ssq[:, s, t, n:n + 1], in1=qk_gain[:, n * D:(n + 1) * D],
                                                       op0=ALU.mult, op1=ALU.mult)
                ins.then_inc(scaled9, 1)
                dve.wait_ge(scaled9, b + 1)
                dve.tensor_scalar(qk9[:, s], qk9[:, s], 0.0, None, ALU.max).then_inc(relu9, 1)
                dve.wait_ge(kv_done, b + 1)
                for c in range(KC):
                    dve.tensor_tensor(kv9[:, s, c, 0:P], ps[:, 6, c * 160:c * 160 + P], same_head, ALU.mult)
                    ins = dve.tensor_scalar(kv9[:, s, c, P:NORM], head_of, ps[:, 6, c * 160 + P:c * 160 + P + 1], None, ALU.mult)
                ins.then_inc(kv_ready, 1)
                for t in range(TT):
                    i = b * TT + t
                    x = ps[:, 7 - t % 2, 0:320].rearrange("p (c m) -> p c m", c=KC)
                    dve.wait_ge(att_done, i + 1)
                    dve.tensor_scalar(norm9[:, 0], x[:, :, P:NORM], 1e-6, None, ALU.add).then_inc(norm_steps, 1)
                    dve.wait_ge(norm_steps, i * 2 + 1)
                    dve.reciprocal(norm9[:, 1], norm9[:, 0]).then_inc(norm_steps, 1)
                    dve.wait_ge(norm_steps, i * 2 + 2)
                    dve.wait_ge(att_turned, b)
                    for c in range(KC):
                        ins = dve.tensor_tensor(att9[:, t, c * P:(c + 1) * P].rearrange("p (h d) -> p h d", d=HD),
                                                x[:, c, 0:P].rearrange("p (h d) -> p h d", d=HD),
                                                norm9[:, 1, c, :].unsqueeze(2).to_broadcast((P, HH, HD)), ALU.mult)
                    ins.then_inc(att_ready, 1)
                for h in range(2):
                    dve.wait_ge(proj_done, b * 2 + h + 1)
                    hh = H[:, bass.ds(b * TT + 2 * h, 2), :]
                    dve.tensor_tensor(hh, ps[:, 6 + h, :].rearrange("p (t d) -> p t d", d=D), hh, ALU.add).then_inc(proj_read, 1)
            batches(dve, lambda b, s: f9.dve(dve, b, s, lambda: None), step)

        free[0] = CONST_END
        E10, HID = 32, 64
        W_E1 = take(KC * E10 * HID).rearrange("p (k e m) -> p k e m", k=KC, e=E10)
        W_E2 = take(E10 * D).rearrange("p (e d) -> p e d", e=E10)
        b_e1 = take(E10 * HID).rearrange("p (e m) -> p e m", e=E10)
        d10 = Dispatch("top", E10, 1)
        STAGE10 = mark()
        W_R10 = take(KC * E10).rearrange("p (k e) -> p k e", k=KC)
        b_r10 = take(E10)
        f10 = Front("top")
        w10_in = sem("w10_in")
        wx10_in = sem("wx10_in")
        z10_out = [sem(f"z10_out{s}") for s in range(2)]
        lg10_done = sem("lg10_done")
        lg10_read = sem("lg10_read")

        def sp_router10(sp):
            sp.dma_start(W_R10, a["w_r10"]).then_inc(w10_in, 16)
            sp.dma_start(b_r10, a["b_r10"].to_broadcast((P, E10))).then_inc(w10_in, 16)
            sp.dma_start(W_E1, a["w_e1"]).then_inc(wx10_in, 16)
            sp.dma_start(W_E2[0:HID + 1], a["w_e2"]).then_inc(wx10_in, 16)
            sp.dma_start(b_e1.rearrange("p e m -> p (e m)"), a["b_e1"].to_broadcast((P, E10 * HID))).then_inc(wx10_in, 16)
            with sp.Fori(0, B // 2) as pair:
                for s in range(2):
                    b = pair * 2 + s
                    sp.wait_ge(f10.z_ready, b + 1)
                    sp.dma_start(z_dram[bass.ds(b * S, S), :].rearrange("(t p) d -> p t d", p=P), f10.z[:, s]).then_inc(z10_out[s], 16)
            for s in range(2):
                sp.wait_ge(z10_out[s], 16 * (B // 2))

        def pool_router10(pool):
            def step(b, s, last):
                if not last:
                    f10.pool(pool, b + 1, 1 - s)
            batches(pool, lambda b, s: f10.pool(pool, b, s), step)

        def pe_router10(pe):
            pe.wait_ge(w10_in, 32)

            def step(b, s, last):
                if not last:
                    f10.pe(pe, b + 1, 1 - s)
                pe.wait_ge(f10.zT_ready, b + 1)
                pe.wait_ge(lg10_read, b)
                for t in range(TT):
                    for k in range(KC):
                        mm = pe.matmul(ps[:, 5, t * E10:(t + 1) * E10], f10.zT[:, s, k, t * P:(t + 1) * P], W_R10[:, k, :],
                                       start=(k == 0), stop=(k == KC - 1))
                mm.then_inc(lg10_done, 1)
            batches(pe, lambda b, s: f10.pe(pe, b, s), step)

        def act_router10(act):
            def step(b, s, last):
                if not last:
                    f10.act(act, b + 1, 1 - s, lambda: act.wait_ge(lg10_done, b))
            batches(act, lambda b, s: f10.act(act, b, s, lambda: None), step)

        def dve_router10(dve):
            dve.wait_ge(w10_in, 32)

            def step(b, s, last):
                if not last:
                    def slot_free():
                        dve.wait_ge(f10.turned, b)
                        dve.wait_ge(z10_out[1 - s], b * 8 if s == 0 else (b - 1) * 8 + 16)
                    f10.dve(dve, b + 1, 1 - s, slot_free)
                dve.wait_ge(lg10_done, b + 1)
                dve.tensor_tensor(d10.logits[:, bass.ds(b * TT, TT), :], ps[:, 5, 0:TT * E10].rearrange("p (t e) -> p t e", e=E10),
                                  b_r10.unsqueeze(1).to_broadcast((P, TT, E10)), ALU.add).then_inc(lg10_read, 1)
            batches(dve, lambda b, s: f10.dve(dve, b, s, lambda: None), step)

        free[0] = STAGE10
        d10.temps()
        best = take(NT)
        rev = take(E10)
        chosen10 = sem("chosen10")

        def sp_route10(sp):
            sp.wait_ge(wx10_in, 48)

        def act_route10(act):
            d10.act(act)

        def pe_route10(pe):
            d10.pe(pe, chosen10, 1)

        def dve_route10(dve):
            link = lambda ins: d10.link(dve, ins)
            wide = d10.wide[:, 0:NT * E10].rearrange("p (t e) -> p t e", e=E10)
            link(dve.tensor_reduce(best, d10.logits, AX.X, ALU.max))
            link(dve.tensor_tensor(wide, d10.logits, best.unsqueeze(2).to_broadcast((P, NT, E10)), ALU.is_equal))
            link(dve.tensor_scalar(rev, count[:, 0:E10], -1.0, float(E10), ALU.mult, ALU.add))
            link(dve.tensor_tensor(wide, wide, rev.unsqueeze(1).to_broadcast((P, NT, E10)), ALU.mult))
            link(dve.tensor_reduce(best, wide, AX.X, ALU.max))
            dve.tensor_tensor(d10.chosen, rev.unsqueeze(1).to_broadcast((P, NT, E10)), best.unsqueeze(2).to_broadcast((P, NT, E10)),
                              ALU.is_equal).then_inc(chosen10, 1)
            d10.dve(dve)

        free[0] = STAGE10
        g12 = Gather("top", d10, z_dram)
        h12 = take(4 * HID).rearrange("p (s i) -> p s i", s=4)
        hT12 = take(4 * P).rearrange("p (s t) -> p s t", s=4)
        y12 = take(4 * D).rearrange("p (s d) -> p s d", s=4)
        e1_done = sem("e1_done")
        h12_ready = sem("h12_ready")
        h12_turned = sem("h12_turned")
        hT12_ready = sem("hT12_ready")
        e2_done = sem("e2_done")
        y12_ready = sem("y12_ready")
        y12_out = [sem(f"y12_out{s}") for s in range(4)]
        ones12 = sem("ones12")
        NB12 = d10.N

        def sp_experts12(sp):
            with sp.Fori(0, NB12 // 4) as quad:
                for s in range(4):
                    sp.wait_ge(y12_ready, quad * 4 + s + 1 + 2)
                    sp.dma_start(y_dram[bass.ds((quad * 4 + s) * P, P), :], y12[:, s, :]).then_inc(y12_out[s], 16)
            for s in range(4):
                sp.wait_ge(y12_out[s], 16 * (NB12 // 4))

        def pool_experts12(pool):
            pool.memset(hT12[HID:HID + 1], 1.0).then_inc(ones12, 1)
            pool.wait_ge(ones12, 1)
            g12.pool(pool)

        def pe_experts12(pe):
            pe.sem_inc(g12.turned, 4)
            pe.sem_inc(e1_done, 4)
            pe.sem_inc(e2_done, 4)
            pe.wait_ge(ones12, 1)

            def expert(n):
                return pe.value_load(d10.experti[0:1, bass.ds(n, 1)], min_val=0, max_val=E10 - 1)

            def step(i, s, there):
                if there(i):
                    g12.pe(pe, i, s)
                if there(i - 1):
                    c = (s - 1) % 4
                    e = expert(i - 1)
                    pe.wait_ge(g12.ready, i + 2)
                    pe.wait_ge(h12_ready, i)
                    for k in range(KC):
                        mm = pe.matmul(ps[:, 2 + c % 2, 0:HID], g12.xT[:, c, k, :], W_E1[:, k, bass.ds(e, 1), :].rearrange("p a m -> p (a m)"),
                                       start=(k == 0), stop=(k == KC - 1))
                    mm.then_inc(e1_done, 1)
                if there(i - 2):
                    c = (s - 2) % 4
                    pe.wait_ge(h12_ready, i - 1 + 2)
                    pe.wait_ge(hT12_ready, i - 1)
                    alone(pe)
                    pe.transpose(ps[0:HID, 4 + c % 2, 0:P], h12[:, c, :], ident).then_inc(h12_turned, 1)
                if there(i - 3):
                    c = (s - 3) % 4
                    e = expert(i - 3)
                    pe.wait_ge(hT12_ready, i - 2 + 2)
                    pe.wait_ge(y12_ready, i - 2)
                    pe.matmul(ps[:, 6 + c % 2, 0:D], hT12[0:HID + 1, c, :], W_E2[0:HID + 1, bass.ds(e, 1), :].rearrange("p a d -> p (a d)"),
                              start=True, stop=True).then_inc(e2_done, 1)
            blocks(pe, NB12, step)

        def act_experts12(act):
            act.sem_inc(g12.ready, 2)
            act.sem_inc(hT12_ready, 2)

            def step(i, s, there):
                if there(i):
                    g12.act(act, i, s, e1_done, i + 1)
                if there(i - 2):
                    c = (s - 2) % 4
                    act.wait_ge(h12_turned, i - 1 + 4)
                    act.wait_ge(e2_done, i - 1)
                    act.activation(hT12[0:HID, c, :], ps[0:HID, 4 + c % 2, 0:P], ACT.Relu).then_inc(hT12_ready, 1)
            blocks(act, NB12, step)

        def dve_experts12(dve):
            for x in (h12_ready, y12_ready):
                dve.sem_inc(x, 2)
            dve.sem_inc(h12_turned, 4)

            def step(i, s, there):
                if there(i - 1):
                    c = (s - 1) % 4
                    e = dve.value_load(d10.experti[0:1, bass.ds(i - 1, 1)], min_val=0, max_val=E10 - 1)
                    dve.wait_ge(e1_done, i + 4)
                    dve.wait_ge(h12_turned, i)
                    dve.tensor_tensor(h12[:, c, :], ps[:, 2 + c % 2, 0:HID], b_e1[:, bass.ds(e, 1), :].rearrange("p a m -> p (a m)"),
                                      ALU.add).then_inc(h12_ready, 1)
                if there(i - 3):
                    c = (s - 3) % 4
                    dve.wait_ge(e2_done, i - 2 + 4)
                    dve.wait_ge(y12_out[c], (i - 3 - c) * 4)
                    dve.tensor_scalar(y12[:, c, :], ps[:, 6 + c % 2, 0:D], 0.0, None, ALU.max).then_inc(y12_ready, 1)
            blocks(dve, NB12, step)

        back13 = take(4 * D).rearrange("p (s d) -> p s d", s=4)
        at13 = take(4, I32)
        sum13 = take(4 * D).rearrange("p (s d) -> p s d", s=4)
        at13_ready = sem("at13_ready")
        back13_in = [sem(f"back13_in{s}") for s in range(4)]
        sum13_ready = sem("sum13_ready")
        stored = [sem(f"stored{s}") for s in range(4)]

        def pool_output(pool):
            with pool.Fori(0, NT // 4) as quad:
                for s in range(4):
                    t = quad * 4 + s
                    pool.wait_ge(sum13_ready, t + 1)
                    pool.tensor_copy(at13[:, s:s + 1], d10.sloti[:, bass.ds(t, 1), :].rearrange("p a k -> p (a k)")).then_inc(at13_ready, 1)
                    pool.wait_ge(at13_ready, t + 1)
                    alone(pool)
                    pool.indirect_dma_start(out=back13[:, s, :], out_offset=None, in_=y_dram,
                                            in_offset=bass.IndirectOffsetOnAxis(ap=at13[:, s:s + 1].bitcast(U32), axis=0)
                                            ).then_inc(back13_in[s], 16)

        def dve_output(dve):
            dve.sem_inc(sum13_ready, 4)
            with dve.Fori(0, NT // 4) as quad:
                for s in range(4):
                    t = quad * 4 + s
                    dve.wait_ge(back13_in[s], quad * 16 + 16)
                    dve.wait_ge(stored[s], quad * 16)
                    dve.tensor_tensor(sum13[:, s, :], back13[:, s, :], H[:, bass.ds(t, 1), :].rearrange("p a d -> p (a d)"),
                                      ALU.add).then_inc(sum13_ready, 1)

        def sp_output(sp):
            with sp.Fori(0, NT // 4) as quad:
                for s in range(4):
                    t = quad * 4 + s
                    sp.wait_ge(sum13_ready, t + 1 + 4)
                    sp.dma_start(out[bass.ds(t * P, P), :], sum13[:, s, :]).then_inc(stored[s], 16)
            for s in range(4):
                sp.wait_ge(stored[s], 16 * (NT // 4))

        stages = [(sp_linear, pool_linear, act_linear, dve_linear, pe_linear),
                  (sp_router10, pool_router10, act_router10, dve_router10, pe_router10),
                  (sp_route10, nothing, act_route10, dve_route10, pe_route10),
                  (sp_experts12, pool_experts12, act_experts12, dve_experts12, pe_experts12),
                  (sp_output, pool_output, nothing, dve_output, nothing)][:max(0, stop - 8)]
        if a.get("dbg"):
            dbg_out = sem("dbg_out")

            def sp_dbg(sp):
                sp.dma_start(a["dbg"]["H"].rearrange("(t p) d -> p t d", p=P), H).then_inc(dbg_out, 16)
                sp.wait_ge(dbg_out, 16)
            stages.append((sp_dbg, nothing, nothing, nothing, nothing))
        run(stages)


def laid_out(x):
    f = {k: np.asarray(v) for k, v in x.items()}

    def rows(w):
        return np.ascontiguousarray(w.reshape(w.shape[0] // P, P, -1).transpose(1, 0, 2))

    def cols(v):
        return np.ascontiguousarray(v.reshape(-1, P).T)

    at = np.arange(S, dtype=np.float32)[:, None]
    even = np.arange(0, D, 2, dtype=np.float32)[None, :]
    angle = at / np.power(np.float32(10000.0), np.float32(2.0) * even / np.float32(D))
    pe = np.zeros((S, D), np.float32)
    pe[:, 0::2], pe[:, 1::2] = np.sin(angle), np.cos(angle)

    w_in, b_in = f["L0_tok_in_proj_w"], f["L0_tok_in_proj_b"]
    o = {
        "x": np.ascontiguousarray(f["x"].reshape(NT, P).T),
        "emb": f["L0_tok_emb"],
        "pos": rows(pe),
        "ident": np.eye(P, dtype=np.float32),
        "w_qk": rows(w_in[:2 * D].T),
        "w_v": rows(w_in[2 * D:].T),
        "b_qk": cols(b_in[:2 * D]),
        "b_v": b_in[None, 2 * D:],
        "b_o": f["L0_tok_out_proj_b"][None],
    }
    w_o = np.zeros((NG, G4, 32, D), np.float32)
    w_o[:, :, :HD] = f["L0_tok_out_proj_w"].T.reshape(NG, G4, HD, D)
    o["w_o"] = rows(w_o.reshape(NG * P, D))
    o["w_1"], o["w_2"], o["b_1"] = rows(f["L0_tok_w1"].T), rows(f["L0_tok_w2"].T), cols(f["L0_tok_b1"])
    o["norms"] = np.concatenate([f["L0_tok_" + n] for n in ("g1", "beta1", "b2", "g2", "beta2")])[None]
    o["w_kvr"] = np.stack([rows(f["L0_attn_W" + n].T) for n in "kvr"], 1)
    o["w_wo"] = rows(f["L0_attn_Wo"].T)
    o["vecs"] = np.stack([cols(f["L0_attn_" + n].reshape(-1)) for n in ("time_mix_k", "time_mix_v", "time_mix_r", "w", "u")], 1)
    gu = np.concatenate([f["L0_ffn_gate_w"], f["L0_ffn_up_w"]], 1)
    o["w_gu"] = np.ascontiguousarray(gu.reshape(16, 256, KC, P).transpose(3, 2, 0, 1))
    o["w_d"] = np.ascontiguousarray(f["L0_ffn_down_w"].transpose(2, 0, 1))
    o["w_r"] = rows(f["L0_ffn_router_weight"].T)
    o["e_bias"] = f["L0_ffn_e_bias"][None]
    for n, w in (("w_sg", "gate"), ("w_su", "up"), ("w_sd", "down")):
        o[n] = rows(f[f"L0_ffn_sh_{w}_w"].T)
    tile = np.arange(NT, dtype=np.float32)
    o["consts"] = np.concatenate([np.tile((tile > 0).astype(np.float32), 32), P * tile, np.ones(32, np.float32),
                                  np.arange(160, dtype=np.float32), tile])[None]
    o["before"] = np.triu(np.ones((P, P), np.float32), 1)
    o["row_of"] = np.arange(P, dtype=np.float32)[:, None]
    head = np.arange(P) // HD
    o["w_qkv"], o["w_out"] = rows(f["L1_attn_W_qkv"]), rows(f["L1_attn_W_out"])
    o["qk_gain"] = np.concatenate([f["L1_attn_qn_w"], f["L1_attn_kn_w"]])[None]
    o["b_out"] = f["L1_attn_b_out"][None]
    o["same_head"] = (head[:, None] == head[None, :]).astype(np.float32)
    o["head_of"] = (head[:, None] == np.arange(P // HD)[None, :]).astype(np.float32)
    o["w_r10"], o["b_r10"] = rows(f["L1_ffn_router_w"].T), f["L1_ffn_router_b"][None]
    o["w_e1"] = np.ascontiguousarray(f["L1_ffn_weights1"].reshape(32, KC, P, 64).transpose(2, 1, 0, 3))
    o["w_e2"] = np.ascontiguousarray(np.concatenate([f["L1_ffn_weights2"], f["L1_ffn_bias2"][:, None, :]], 1).transpose(1, 0, 2))
    o["b_e1"] = f["L1_ffn_bias1"].reshape(1, -1)
    return {k: np.ascontiguousarray(v) for k, v in o.items()}


def kernel(**inputs):
    import concourse.bacc as bacc
    from concourse.bass_utils import run_bass_kernel_spmd

    nc = bacc.Bacc("TRN2", target_bir_lowering=False, num_devices=1)
    arrays = laid_out(inputs)
    aps = {k: nc.dram_tensor(f"in_{k}", v.shape, mybir.dt.from_np(v.dtype), kind="ExternalInput").ap()
           for k, v in arrays.items()}
    out = nc.dram_tensor("out", (B * S, D), F32, kind="ExternalOutput").ap()
    build(nc, aps, out)
    r = run_bass_kernel_spmd(nc, [{f"in_{k}": v for k, v in arrays.items()}], core_ids=[0])
    return r.results[0]["out"].reshape(B, S, D)
```

```python
from contextlib import ExitStack

import numpy as np
import concourse.bass as bass
from concourse import mybir

F32 = mybir.dt.float32
BF16 = mybir.dt.bfloat16
I32 = mybir.dt.int32
U32 = mybir.dt.uint32
ALU = mybir.AluOpType
ACT = mybir.ActivationFunctionType
AX = mybir.AxisListType

P = 128
B, S, D = 8, 512, 256
TT = S // P
NT = B * TT
KC = D // P
HD = 16
NH = D // HD
G4 = 4
NG = NH // G4
VOCAB = 8000
DFF = 4 * D
AWORDS = 52736
LN_EPS = 1e-5

QPART = (0, 0, 1, 1, 0, 2)
KPART = (0, 1, 0, 1, 2, 0)
NPARTS = len(QPART)
SROWS = NPARTS * HD


def build(nc, a, out, stop=99):
    ctx = ExitStack()
    with ctx:
        held = []

        def sem(name):
            held.append(nc.alloc_semaphore(name=name))
            return held[-1]

        arena = ctx.enter_context(nc.sbuf_tensor("arena", [P, AWORDS], F32))
        ps = ctx.enter_context(nc.psum_tensor("ps", [P, 8, 512], F32))
        free = [0]

        def take(n, dt=F32, at=None):
            words = n if dt != BF16 else (n + 1) // 2
            start = free[0] if at is None else at
            if at is None:
                free[0] += words
                assert free[0] <= AWORDS, free[0]
            v = arena[:, start:start + words]
            return v if dt == F32 else v.bitcast(dt)

        def mark():
            return free[0]

        H = take(NT * D).rearrange("p (t d) -> p t d", d=D)
        ident = take(P)
        identb = take(P, BF16)
        mhalf = take(TT)

        ENGINES = 5

        def run(stages):
            bar = sem(f"stage_ends{len(stages)}")

            def program(e, which):
                for n, stage in enumerate(stages):
                    stage[which](e)
                    e.drain().then_inc(bar, 1)
                    e.wait_ge(bar, ENGINES * (n + 1))

            with nc.Block() as block:
                @block.sync
                def _(sp):
                    program(sp, 0)

                @block.gpsimd
                def _(pool):
                    program(pool, 1)

                @block.scalar
                def _(act):
                    program(act, 2)

                @block.vector
                def _(dve):
                    program(dve, 3)

                @block.tensor
                def _(pe):
                    program(pe, 4)
            nc.clear_and_free_semaphores(held)
            held.clear()
            nc.all_engine_barrier()

        def alone(e):
            e.sem_inc(passed[0], 1)

        PERSIST = mark()
        passed = [sem("passed")]

        def batches(e, first, step):
            first(0, 0)
            with e.Fori(0, B // 2 - 1) as pair:
                step(pair * 2, 0, False)
                step(pair * 2 + 1, 1, False)
            step(B - 2, 0, False)
            step(B - 1, 1, True)

        V = take(NT * D).rearrange("p (t d) -> p t d", d=D)
        STAGE1 = mark()
        idx = take(NT, I32)
        W_QK = take(KC * 2 * D).rearrange("p (k m) -> p k m", k=KC)
        W_V = take(KC * D).rearrange("p (k m) -> p k m", k=KC)
        b_qk = take(4)
        pos = take(TT * D).rearrange("p (t d) -> p t d", d=D)
        b_v = take(D)
        b_o = take(D)
        tokf = take(NT)
        negf = take(NT)
        idxs = take(2 * TT, I32).rearrange("p (s t) -> p s t", s=2)
        xg = take(2 * TT * D).rearrange("p (s t d) -> p s t d", s=2, d=D)
        xT = take(2 * KC * S).rearrange("p (s k t) -> p s k t", s=2, k=KC)
        qf = take(2 * S).rearrange("p (s t) -> p s t", s=2)
        qr = take(2 * S).rearrange("p (s t) -> p s t", s=2)
        parts = take(2 * 4 * 3 * S, BF16).rearrange("p (s m c t) -> p s m c t", s=2, m=4, c=3)
        split_dram = nc.dram_tensor("split_dram", (B, 4, P, 3, S), BF16, kind="Internal").ap()

        const_in = sem("const_in")
        tok_in = sem("tok_in")
        idx_steps = sem("idx_steps")
        ident_ready = sem("ident_ready")
        identb_ready = sem("identb_ready")
        idx_slot = sem("idx_slot")
        gathered = [sem(f"gathered{t}") for t in range(2 * TT)]
        x_ready = sem("x_ready")
        x_kept = sem("x_kept")
        x_turned = sem("x_turned")
        xT_ready = sem("xT_ready")
        qk_done = sem("qk_done")
        v_done = sem("v_done")
        qk_read = sem("qk_read")
        v_read = sem("v_read")
        part0 = sem("part0")
        rest0 = sem("rest0")
        part1 = sem("part1")
        part2 = sem("part2")
        parts_out = [sem(f"parts_out{s}") for s in range(2)]
        CONSTS = 8

        def sp_embed(sp):
            sp.dma_start(idx, a["x"]).then_inc(tok_in, 16)
            for dst, name in ((W_QK, "w_qk"), (W_V, "w_v"), (b_qk, "b_qk"), (pos, "pos"), (ident, "ident")):
                sp.dma_start(dst, a[name]).then_inc(const_in, 16)
            sp.dma_start(b_v, a["b_v"].to_broadcast((P, D))).then_inc(const_in, 16)
            sp.dma_start(b_o, a["b_o"].to_broadcast((P, D))).then_inc(const_in, 16)
            with sp.Fori(0, B // 2) as pair:
                for s in range(2):
                    sp.wait_ge(part0, (pair * 2 + s) * 4 + 4)
                    sp.wait_ge(part1, (pair * 2 + s) * 4 + 4)
                    sp.wait_ge(part2, (pair * 2 + s) * 4 + 4)
                    sp.dma_start(split_dram[pair * 2 + s].rearrange("m p c t -> p m c t"), parts[:, s]).then_inc(parts_out[s], 16)
            for s in range(2):
                sp.wait_ge(parts_out[s], 16 * (B // 2))

        def pool_embed(pool):
            pool.wait_ge(idx_steps, 5)
            pool.sem_inc(x_kept, 1)
            with pool.Fori(0, B // 2) as pair:
                for s in range(2):
                    pool.wait_ge(x_turned, pair * 2 + s)
                    pool.wait_ge(x_kept, pair * 2 + s)
                    pool.tensor_copy(idxs[:, s, :], idx[:, bass.ds((pair * 2 + s) * TT, TT)]).then_inc(idx_slot, 1)
                    pool.wait_ge(idx_slot, pair * 2 + s + 1)
                    alone(pool)
                    for t in range(TT):
                        pool.indirect_dma_start(
                            out=xg[:, s, t, :], out_offset=None, in_=a["emb"],
                            in_offset=bass.IndirectOffsetOnAxis(ap=idxs[:, s, t:t + 1].bitcast(U32), axis=0)
                        ).then_inc(gathered[s * TT + t], 16)
                    pool.wait_ge(x_ready, pair * 2 + s + 1)
                    pool.tensor_tensor(H[:, bass.ds((pair * 2 + s) * TT, TT), :], xg[:, s],
                                       b_o.unsqueeze(1).to_broadcast((P, TT, D)), ALU.add).then_inc(x_kept, 1)

        def dve_embed(dve):
            dve.wait_ge(tok_in, 16)
            dve.tensor_copy(tokf, idx).then_inc(idx_steps, 1)
            dve.wait_ge(idx_steps, 1)
            dve.tensor_scalar(negf, tokf, 0.0, float(VOCAB), ALU.is_lt, ALU.mult).then_inc(idx_steps, 1)
            dve.wait_ge(idx_steps, 2)
            dve.tensor_tensor(tokf, tokf, negf, ALU.add).then_inc(idx_steps, 1)
            dve.wait_ge(idx_steps, 3)
            dve.tensor_scalar(negf, tokf, 0.0, float(VOCAB - 1), ALU.max, ALU.min).then_inc(idx_steps, 1)
            dve.wait_ge(idx_steps, 4)
            dve.tensor_copy(idx, negf).then_inc(idx_steps, 1)
            dve.wait_ge(const_in, 16 * 7)
            dve.tensor_copy(identb, ident).then_inc(identb_ready, 1)
            dve.tensor_scalar(b_qk[:, 0:2], b_qk[:, 0:2], HD ** -0.5, None, ALU.mult).then_inc(identb_ready, 1)
            dve.sem_inc(x_turned, 1)

            def add_positions(b, s):
                for t in range(TT):
                    dve.wait_ge(gathered[s * TT + t], (b - s) * 8 + 16)
                dve.tensor_tensor(xg[:, s], xg[:, s], pos, ALU.add).then_inc(x_ready, 1)

            def step(b, s, last):
                if not last:
                    add_positions(b + 1, 1 - s)
                for m in range(4):
                    dve.wait_ge(part0, b * 4 + m + 1)
                    dve.tensor_tensor(qr[:, m % 2], qf[:, m % 2], parts[:, s, m, 0, :], ALU.subtract).then_inc(rest0, 1)
                    dve.wait_ge(part1, b * 4 + m + 1)
                    dve.tensor_tensor(parts[:, s, m, 2, :], qr[:, m % 2], parts[:, s, m, 1, :], ALU.subtract).then_inc(part2, 1)
                for h in range(2):
                    dve.wait_ge(v_done, b * 2 + h + 1)
                    dve.tensor_tensor(V[:, bass.ds(b * TT + 2 * h, 2), :], ps[:, 6 + h, :].rearrange("p (t d) -> p t d", d=D),
                                      b_v.unsqueeze(1).to_broadcast((P, 2, D)), ALU.add).then_inc(v_read, 1)
            batches(dve, add_positions, step)

        def act_embed(act):
            act.wait_ge(identb_ready, 2)

            def keep_turned(b, s, done=None):
                act.wait_ge(x_turned, b + 2)
                if done is not None:
                    act.wait_ge(v_done, done)
                act.activation(xT[:, s], ps[:, 0:2, :], ACT.Copy).then_inc(xT_ready, 1)

            def step(b, s, last):
                act.wait_ge(parts_out[s], (b - s) * 8)
                for m in range(4):
                    scale = HD ** -0.5 if m < 2 else 1.0
                    act.wait_ge(qk_done, b * 4 + m + 1)
                    act.activation(qf[:, m % 2], ps[:, 2 + m, :], ACT.Identity, bias=b_qk[:, m:m + 1], scale=scale).then_inc(qk_read, 1)
                    act.activation(parts[:, s, m, 0, :], ps[:, 2 + m, :], ACT.Identity, bias=b_qk[:, m:m + 1], scale=scale).then_inc(part0, 1)
                    if m == 3 and not last:
                        keep_turned(b + 1, 1 - s, b * 2)
                    act.wait_ge(rest0, b * 4 + m + 1)
                    act.activation(parts[:, s, m, 1, :], qr[:, m % 2], ACT.Copy).then_inc(part1, 1)
            batches(act, keep_turned, step)

        def pe_embed(pe):
            pe.wait_ge(const_in, 16 * 7)

            def turn(b, s):
                pe.wait_ge(x_ready, b + 1)
                pe.wait_ge(xT_ready, b)
                for t in range(TT):
                    for k in range(KC):
                        mm = pe.transpose(ps[:, k, t * P:(t + 1) * P], xg[:, s, t, k * P:(k + 1) * P], ident)
                mm.then_inc(x_turned, 1)

            def step(b, s, last):
                pe.wait_ge(xT_ready, b + 1)
                for m in range(4):
                    pe.wait_ge(part0, b * 4)
                    for k in range(KC):
                        mm = pe.matmul(ps[:, 2 + m, :], W_QK[:, k, m * P:(m + 1) * P], xT[:, s, k, :],
                                       start=(k == 0), stop=(k == KC - 1))
                    mm.then_inc(qk_done, 1)
                if not last:
                    turn(b + 1, 1 - s)
                pe.wait_ge(v_read, b * 2)
                for t in range(TT):
                    for k in range(KC):
                        mm = pe.matmul(ps[:, 6 + t // 2, (t % 2) * D:(t % 2 + 1) * D], xT[:, s, k, t * P:(t + 1) * P], W_V[:, k, :],
                                       start=(k == 0), stop=(k == KC - 1))
                    if t % 2:
                        mm.then_inc(v_done, 1)
            batches(pe, turn, step)

        free[0] = STAGE1
        W_O = take(KC * D).rearrange("p (k d) -> p k d", k=KC)
        RING = 4
        AHEAD = 2
        q6 = take(RING * G4 * S, BF16).rearrange("p (r h t) -> p r h t", r=RING, h=G4)
        k6 = take(RING * G4 * S, BF16).rearrange("p (r h t) -> p r h t", r=RING, h=G4)
        vaug = take(2 * TT * NH * 32).rearrange("p (s t h e) -> p s t h e", s=2, t=TT, h=NH)
        pT = take(2 * G4 * S).rearrange("p (r h t) -> p r h t", r=2, h=G4)
        raw = take(S)
        context = take(2 * TT * D).rearrange("p (s t d) -> p s t d", s=2, d=D)
        contextT = take(D)
        inverse = take(TT * G4).rearrange("p (t h) -> p t h", h=G4)
        nmax = take(16).rearrange("p (t h) -> p t h", h=G4)
        nrest = take(16).rearrange("p (t h) -> p t h", h=G4)
        msplit = take(2 * TT * G4 * 3, BF16).rearrange("p (s t h c) -> p s t h c", s=2, t=TT, h=G4)
        mt = take(2 * S, BF16).rearrange("p (s t) -> p s t", s=2)
        MROWS = 3 * G4
        QROWS = SROWS + 3

        wo_in = sem("wo_in")
        ones_ready = sem("ones_ready")
        k_ones = sem("k_ones")
        qk_in = [sem(f"qk_in{r}") for r in range(RING)]
        m_in = [sem(f"m_in{r}") for r in range(RING)]
        vaug_ready = sem("vaug_ready")
        s1_done = sem("s1_done")
        max_done = sem("max_done")
        max_steps = sem("max_steps")
        mt_done = sem("mt_done")
        mt_ready = sem("mt_ready")
        s2_done = sem("s2_done")
        exp_done = sem("exp_done")
        pv_done = sem("pv_done")
        raw_ready = sem("raw_ready")
        raw_turned = sem("raw_turned")
        inverses = sem("inverses")
        tile_turned = sem("tile_turned")
        tile_ready = sem("tile_ready")
        ctx_ready = sem("ctx_ready")
        o_done = sem("o_done")
        o_read = sem("o_read")
        GROUPS = B * NG
        PAIR = 2 * NG

        def sp_attn(sp):
            sp.dma_start(W_O, a["w_o"]).then_inc(wo_in, 16)

            def load(g, u, b):
                j, r = u % NG, u % RING
                sp.wait_ge(s2_done, (g + 1) * 16)
                for dst, first, which in ((q6, 0, QPART), (k6, 2, KPART)):
                    for n, c in enumerate(which):
                        src = split_dram[b, first + j // 2, (j % 2) * 64:(j % 2 + 1) * 64, c, :]
                        sp.dma_start(dst[n * HD:(n + 1) * HD, r], src.rearrange("(h d) t -> d h t", d=HD)).then_inc(qk_in[r], 16)

            def spread_maxima(g, u):
                sp.wait_ge(mt_ready, g + 1)
                for h in range(G4):
                    sp.dma_start(q6[SROWS:QROWS, u % RING, h, :], mt[3 * h:3 * h + 3, u % 2, :]).then_inc(m_in[u % RING], 16)

            def step(pair, first):
                for u in range(PAIR):
                    g = pair * PAIR + u
                    if not first or u >= 3:
                        spread_maxima(g - 3, (u - 3) % PAIR)
                    load(g, u, pair * 2 + u // NG)
            step(0, True)
            with sp.Fori(1, B // 2) as pair:
                step(pair, False)
            for g in range(GROUPS - 3, GROUPS):
                spread_maxima(g, g % PAIR)

        def pool_attn(pool):
            pool.memset(k6[SROWS:QROWS], 1.0).then_inc(k_ones, 1)
            pool.wait_ge(k_ones, 1)
            with pool.Fori(0, B // 2) as pair:
                for s in range(2):
                    b = pair * 2 + s
                    pool.wait_ge(pv_done, b * 16)
                    pool.tensor_copy(vaug[:, s, :, :, 0:HD], V[:, bass.ds(b * TT, TT), :].rearrange("p t (h d) -> p t h d", d=HD)).then_inc(vaug_ready, 1)

        def pe_attn(pe):
            def maxima(g, u, n, use):
                r, qt, hp = u % RING, n // 2, n % 2
                if n == 0:
                    pe.wait_ge(qk_in[r], use * 12 * 16)
                pe.wait_ge(max_done, g * 8 + n)
                for h in (2 * hp, 2 * hp + 1):
                    mm = pe.matmul(ps[:, h, :], q6[0:SROWS, r, h, qt * P:(qt + 1) * P], k6[0:SROWS, r, h, :], start=True, stop=True)
                mm.then_inc(s1_done, 1)

            def turn_maxima(g, u, residuals):
                pe.wait_ge(max_steps, g * 6 + 6)
                pe.wait_ge(mt_ready, g)
                pe.wait_ge(o_read, residuals)
                out7 = ps[:, 7, 0:256].bitcast(BF16)
                for qt in range(TT):
                    mm = pe.transpose(out7[0:MROWS, qt * P:(qt + 1) * P], msplit[:, u % 2, qt].rearrange("p h c -> p (h c)"), identb)
                mm.then_inc(mt_done, 1)

            def scores(g, u, c, use):
                r, kt, h = u % RING, c // G4, c % G4
                if c == 0:
                    pe.wait_ge(m_in[r], use * G4 * 16)
                pe.wait_ge(exp_done, g * 16 + c)
                pe.matmul(ps[:, 4 + c % 2, :], k6[0:QROWS, r, h, kt * P:(kt + 1) * P], q6[0:QROWS, r, h, :],
                          start=True, stop=True).then_inc(s2_done, 1)

            def values(g, u, kt, batches_in):
                s, j = u // NG % 2, u % NG
                if kt == 0:
                    pe.wait_ge(ctx_ready, g)
                    pe.wait_ge(vaug_ready, batches_in)
                pe.wait_ge(exp_done, g * 16 + 4 * kt + 4 + 1)
                for h in range(G4):
                    mm = pe.matmul(ps[32 * h:32 * h + 32, 6, :], vaug[:, s, kt, G4 * j + h, :], pT[:, kt % 2, h, :],
                                   start=(kt == 0), stop=(kt == TT - 1))
                mm.then_inc(pv_done, 1)

            def turn_context(g):
                pe.wait_ge(raw_ready, g + 1)
                for t in range(TT):
                    mm = pe.transpose(ps[:, 6, t * P:(t + 1) * P], raw[:, t * P:(t + 1) * P], ident)
                mm.then_inc(raw_turned, 1)

            def turn_tile(tile, t, s, turned):
                pe.wait_ge(mt_ready, turned)
                pe.wait_ge(o_read, tile)
                for k in range(KC):
                    mm = pe.transpose(ps[:, 7, 256 + k * P:256 + (k + 1) * P], context[:, s, t, k * P:(k + 1) * P], ident)
                mm.then_inc(tile_turned, 1)

            def project_tile(tile):
                pe.wait_ge(tile_ready, tile + 1)
                for k in range(KC):
                    mm = pe.matmul(ps[:, 7, 256:512], contextT[:, k * P:(k + 1) * P], W_O[:, k, :], start=(k == 0), stop=(k == KC - 1))
                mm.then_inc(o_done, 1)

            pe.sem_inc(s2_done, RING * 16)
            pe.sem_inc(pv_done, 16)
            for n in range(8):
                maxima(0, 0, n, 1)
            turn_maxima(0, 0, 0)
            for n in range(8):
                maxima(1, 1, n, 1)
            pe.wait_ge(wo_in, 16)
            pe.wait_ge(k_ones, 1)
            pe.wait_ge(ones_ready, 1)

            def step(pair, first, last):
                for u in range(PAIR):
                    g = pair * PAIR + u
                    use = pair * 2 + u // RING + 1
                    project = u >= NG or not first
                    before = u > 0 or not first

                    def look(n):
                        if not last or u + AHEAD < PAIR:
                            maxima(g + AHEAD, u + AHEAD, n, pair * 2 + (u + AHEAD) // RING + 1)
                    scores(g, u, 0, use)
                    look(0)
                    scores(g, u, 1, use)
                    if before:
                        values(g - 1, (u - 1) % PAIR, 3, 0)
                    look(1)
                    scores(g, u, 2, use)
                    scores(g, u, 3, use)
                    if before:
                        turn_context(g - 1)
                    if not (last and u == PAIR - 1):
                        turn_maxima(g + 1, u + 1, g - NG if project else 0)
                    for kt in range(3):
                        c = 4 * kt + 4
                        scores(g, u, c, use)
                        look(2 * kt + 2)
                        scores(g, u, c + 1, use)
                        if kt == 2 and project:
                            project_tile(g - NG)
                        values(g, u, kt, pair * 2 + u // NG + 1)
                        look(2 * kt + 3)
                        scores(g, u, c + 2, use)
                        if kt == 1 and project:
                            turn_tile(g - NG, u % NG, (u // NG + 1) % 2, g + (1 if last and u == PAIR - 1 else 2))
                        scores(g, u, c + 3, use)

            step(0, True, False)
            with pe.Fori(1, B // 2 - 1) as pair:
                step(pair, False, False)
            step(B // 2 - 1, False, True)
            values(GROUPS - 1, PAIR - 1, 3, 0)
            turn_context(GROUPS - 1)
            pe.wait_ge(ctx_ready, GROUPS)
            pe.wait_ge(max_done, (GROUPS - 1) * 8 + 8 + 1)
            for t in range(TT):
                for k in range(KC):
                    mm = pe.transpose(ps[:, t, k * P:(k + 1) * P], context[:, 1, t, k * P:(k + 1) * P], ident)
                mm.then_inc(tile_turned, 1)
            pe.wait_ge(tile_ready, B * TT)
            for t in range(TT):
                for k in range(KC):
                    mm = pe.matmul(ps[:, t, 256:512], pT[:, 0, t, k * P:(k + 1) * P], W_O[:, k, :], start=(k == 0), stop=(k == KC - 1))
                mm.then_inc(o_done, 1)

        def act_attn(act):
            def keep_maxima(g, u, sent):
                act.wait_ge(m_in[(u - 2) % RING], sent * G4 * 16)
                act.wait_ge(mt_done, g + 1)
                act.activation(mt[0:MROWS, u % 2, :], ps[0:MROWS, 7, 0:256].bitcast(BF16), ACT.Copy).then_inc(mt_ready, 1)

            def exps(g, u, c):
                kt, h = c // G4, c % G4
                act.wait_ge(s2_done, g * 16 + c + 1 + RING * 16)
                if h == 0:
                    act.wait_ge(pv_done, g * TT + kt + 15)
                act.activation(pT[:, kt % 2, h, :], ps[:, 4 + c % 2, :], ACT.Exp).then_inc(exp_done, 1)

            def keep_context(g):
                act.wait_ge(pv_done, g * TT + TT + 16)
                act.activation(raw, ps[:, 6, :], ACT.Copy).then_inc(raw_ready, 1)

            def keep_tile(tile):
                act.wait_ge(tile_turned, tile + 1)
                act.activation(contextT, ps[:, 7, 256:512], ACT.Copy).then_inc(tile_ready, 1)

            act.sem_inc(exp_done, 1)
            keep_maxima(0, 0, 0)

            def step(pair, first, last):
                for u in range(PAIR):
                    g = pair * PAIR + u
                    for c in range(16):
                        exps(g, u, c)
                        if c == 2 and (u > 0 or not first):
                            keep_context(g - 1)
                        if c == 11 and (u >= NG or not first):
                            keep_tile(g - NG)
                        if c == 5 and not (last and u == PAIR - 1):
                            keep_maxima(g + 1, u + 1, pair * 2 + (u - 1) // RING + 1)

            step(0, True, False)
            with act.Fori(1, B // 2 - 1) as pair:
                step(pair, False, False)
            step(B // 2 - 1, False, True)
            keep_context(GROUPS - 1)
            for t in range(TT):
                act.wait_ge(tile_turned, (B - 1) * TT + t + 1)
                act.activation(pT[:, 0, t, 0:D], ps[:, t, 0:D], ACT.Copy).then_inc(tile_ready, 1)

        def dve_attn(dve):
            def maximum(g, n):
                qt, hp = n // 2, n % 2
                dve.wait_ge(s1_done, g * 8 + n + 1)
                if n == 0:
                    dve.wait_ge(max_steps, g * 6)
                dve.tensor_reduce(nmax[:, qt, 2 * hp:2 * hp + 2], ps[:, 2 * hp:2 * hp + 2, :], AX.X, ALU.max, negate=True).then_inc(max_done, 1)

            def split(g, u):
                m = msplit[:, u % 2]
                dve.wait_ge(max_done, g * 8 + 8 + 1)
                dve.wait_ge(mt_ready, g - 1 if not (isinstance(g, int) and g == 0) else 0)
                dve.tensor_copy(m[:, :, :, 0], nmax).then_inc(max_steps, 1)
                dve.wait_ge(max_steps, g * 6 + 1)
                dve.tensor_tensor(nrest, nmax, m[:, :, :, 0], ALU.subtract).then_inc(max_steps, 1)
                dve.wait_ge(max_steps, g * 6 + 2)
                dve.tensor_copy(m[:, :, :, 1], nrest).then_inc(max_steps, 1)
                dve.wait_ge(max_steps, g * 6 + 3)
                dve.tensor_tensor(m[:, :, :, 2], nrest, m[:, :, :, 1], ALU.subtract).then_inc(max_steps, 3)

            def normed(g, s, j):
                turned = ps[:, 6, :].rearrange("p (t h e) -> p t h e", t=TT, h=G4)
                dve.wait_ge(raw_turned, g + 1)
                dve.reciprocal(inverse, turned[:, :, :, HD]).then_inc(inverses, 1)
                dve.wait_ge(inverses, g + 1)
                width = G4 * HD
                dve.tensor_tensor(context[:, s, :, j * width:(j + 1) * width].rearrange("p t (h d) -> p t h d", h=G4), turned[:, :, :, 0:HD],
                                  inverse.unsqueeze(3).to_broadcast((P, TT, G4, HD)), ALU.mult).then_inc(ctx_ready, 1)

            def residual(tile, bank=7):
                dve.wait_ge(o_done, tile + 1)
                h = H[:, bass.ds(tile, 1), :] if not isinstance(tile, int) else H[:, tile:tile + 1, :]
                dve.tensor_tensor(h, ps[:, bank:bank + 1, 256:512], h, ALU.add).then_inc(o_read, 1)

            dve.memset(vaug[:, :, :, :, HD:].rearrange("p s t h e -> p (s t h) e"), 1.0).then_inc(ones_ready, 1)
            dve.sem_inc(max_done, 1)
            for g in range(AHEAD):
                for n in range(8):
                    maximum(g, n)
                split(g, g)

            def step(pair, first, last):
                for u in range(PAIR):
                    g = pair * PAIR + u
                    there = not last or u + AHEAD < PAIR
                    before = not (first and u == 0)
                    for n in range(8):
                        if there:
                            maximum(g + AHEAD, n)
                        if n == 1 and before:
                            normed(g - 1, (u - 1) // NG % 2, (u - 1) % NG)
                        if n == 6 and (u >= NG or not first):
                            residual(g - NG)
                    if there:
                        split(g + AHEAD, u)

            step(0, True, False)
            with dve.Fori(1, B // 2 - 1) as pair:
                step(pair, False, False)
            step(B // 2 - 1, False, True)
            normed(GROUPS - 1, 1, NG - 1)
            for t in range(TT):
                residual((B - 1) * TT + t, t)

        class Front:

            def __init__(self, name, affine=None, pad=0):
                self.affine = affine
                self.z = take(2 * TT * D).rearrange("p (s t d) -> p s t d", s=2, d=D)
                self.pad = pad
                self.zT = take(2 * KC * (S + pad)).rearrange("p (s k t) -> p s k t", s=2, k=KC)
                self.stats = take(2 * TT * 6).rearrange("p (s t x) -> p s t x", s=2, t=TT)
                self.mv = take(2 * TT * 2).rearrange("p (s t x) -> p s t x", s=2, t=TT)
                self.rstd = take(2 * TT).rearrange("p (s t) -> p s t", s=2)
                self.stat_steps = sem(name + "_stat_steps")
                self.rstd_steps = sem(name + "_rstd_steps")
                self.z_ready = sem(name + "_z_ready")
                self.scaled = sem(name + "_scaled")
                self.turned = sem(name + "_turned")
                self.zT_ready = sem(name + "_zT_ready")

            def dve(self, dve, b, s, wait_slot):
                for t in range(TT):
                    h = H[:, bass.ds(b * TT + t, 1), :].rearrange("p a d -> p (a d)")
                    last = dve.bn_stats(self.stats[:, s, t, :], h)
                last.then_inc(self.stat_steps, 1)
                dve.wait_ge(self.stat_steps, b * 2 + 1)
                alone(dve)
                for t in range(TT):
                    last = dve.bn_aggr(self.mv[:, s, t, :], self.stats[:, s, t, :])
                last.then_inc(self.stat_steps, 1)
                wait_slot()
                dve.wait_ge(self.rstd_steps, b * 2 + 2)
                for t in range(TT):
                    h = H[:, bass.ds(b * TT + t, 1), :].rearrange("p a d -> p (a d)")
                    last = dve.tensor_scalar(self.z[:, s, t, :], h, self.mv[:, s, t, 0:1], self.rstd[:, s, t:t + 1], ALU.subtract, ALU.mult)
                last.then_inc(self.z_ready, 1)

            def pool(self, pool, b, s):
                root_of_variance(pool, self.rstd[:, s], self.mv[:, s, :, 1], self.stat_steps, b * 2 + 2, self.rstd_steps, b * 2)
                if self.affine:
                    gain, shift = self.affine
                    pool.wait_ge(self.z_ready, b + 1)
                    pool.tensor_tensor(self.z[:, s], self.z[:, s], gain.unsqueeze(1).to_broadcast((P, TT, D)), ALU.mult).then_inc(self.scaled, 1)
                    pool.wait_ge(self.scaled, b * 2 + 1)
                    pool.tensor_tensor(self.z[:, s], self.z[:, s], shift.unsqueeze(1).to_broadcast((P, TT, D)), ALU.add).then_inc(self.scaled, 1)

            def pe(self, pe, b, s):
                if self.affine:
                    pe.wait_ge(self.scaled, b * 2 + 2)
                else:
                    pe.wait_ge(self.z_ready, b + 1)
                pe.wait_ge(self.zT_ready, b)
                for t in range(TT):
                    for k in range(KC):
                        mm = pe.transpose(ps[:, k, t * P:(t + 1) * P], self.z[:, s, t, k * P:(k + 1) * P], ident)
                mm.then_inc(self.turned, 1)

            def act(self, act, b, s, wait_slot):
                act.wait_ge(self.turned, b + 1)
                wait_slot()
                act.activation(self.zT[:, s, :, self.pad:], ps[:, 0:KC, :], ACT.Copy).then_inc(self.zT_ready, 1)

        def root_of_variance(pool, rstd, var, ready, count, steps, done):
            pool.wait_ge(ready, count)
            alone(pool)
            pool.tensor_scalar(rstd, var, LN_EPS, None, ALU.add).then_inc(steps, 1)
            pool.wait_ge(steps, done + 1)
            pool.tensor_tensor(rstd, rstd, mhalf, ALU.pow).then_inc(steps, 1)

        def skewed(e, step):
            with e.Fori(0, B // 2 - 2) as pair:
                for s in range(2):
                    step(pair * 2 + s, s, B)
            for b in range(B - 4, B):
                step(b, b % 2, B - 1 - b)

        free[0] = PERSIST
        MF = DFF // P
        W_1 = take(KC * DFF).rearrange("p (k m) -> p k m", k=KC)
        W_2 = take(MF * D).rearrange("p (k d) -> p k d", k=MF)
        b_1 = take(MF)
        norms = take(5 * D).rearrange("p (n d) -> p n d", n=5)
        g_1, beta_1, b_2, g_2, beta_2 = (norms[:, n] for n in range(5))
        f3 = Front("ff", affine=(g_1, beta_1))
        fT = take(2 * MF * S).rearrange("p (s m t) -> p s m t", s=2, m=MF)
        y2 = take(2 * TT * D).rearrange("p (s t d) -> p s t d", s=2, d=D)
        stats2 = take(2 * TT * 6).rearrange("p (s t x) -> p s t x", s=2, t=TT)
        mv2 = take(2 * TT * 2).rearrange("p (s t x) -> p s t x", s=2, t=TT)
        rstd2 = take(2 * TT).rearrange("p (s t) -> p s t", s=2)
        w3_in = sem("w3_in")
        norms_in = sem("norms_in")
        mhalf_ready = sem("mhalf_ready")
        up_done = sem("up_done")
        relu_done = sem("relu_done")
        down_done = sem("down_done")
        y2_sums = sem("y2_sums")
        y2_steps = sem("y2_steps")
        rstd2_steps = sem("rstd2_steps")
        h0_steps = sem("h0_steps")

        def sp_ff(sp):
            sp.dma_start(norms.rearrange("p n d -> p (n d)"), a["norms"].to_broadcast((P, 5 * D))).then_inc(norms_in, 16)
            for dst, name in ((b_1, "b_1"), (W_1, "w_1"), (W_2, "w_2")):
                sp.dma_start(dst, a[name]).then_inc(w3_in, 16)

        def pool_ff(pool):
            pool.memset(mhalf, -0.5).then_inc(mhalf_ready, 1)
            pool.wait_ge(mhalf_ready, 1)
            pool.wait_ge(norms_in, 16)

            def step(b, s, last):
                if not last:
                    f3.pool(pool, b + 1, 1 - s)
                root_of_variance(pool, rstd2[:, s], mv2[:, s, :, 1], y2_steps, b * 3 + 2, rstd2_steps, b * 2)
                pool.wait_ge(y2_steps, b * 3 + 3)
                pool.tensor_tensor(y2[:, s], y2[:, s], g_2.unsqueeze(1).to_broadcast((P, TT, D)), ALU.mult).then_inc(h0_steps, 1)
                pool.wait_ge(h0_steps, b * 2 + 1)
                pool.tensor_tensor(H[:, bass.ds(b * TT, TT), :], y2[:, s], beta_2.unsqueeze(1).to_broadcast((P, TT, D)), ALU.add).then_inc(h0_steps, 1)
            batches(pool, lambda b, s: f3.pool(pool, b, s), step)

        def pe_ff(pe):
            def first(b, s):
                f3.pe(pe, b, s)
                pe.wait_ge(w3_in, 48)

            def step(b, s, last):
                pe.wait_ge(f3.zT_ready, b + 1)
                for m in range(MF):
                    pe.wait_ge(relu_done, b * MF + m - 3 if m >= 4 else b * MF)
                    for k in range(KC):
                        mm = pe.matmul(ps[:, 2 + m % 4, :], W_1[:, k, m * P:(m + 1) * P], f3.zT[:, s, k, :], start=(k == 0), stop=(k == KC - 1))
                    mm.then_inc(up_done, 1)
                pe.wait_ge(relu_done, b * MF + MF)
                pe.wait_ge(y2_sums, b * 2)
                for t in range(TT):
                    if t == 2 and not last:
                        f3.pe(pe, b + 1, 1 - s)
                    for m in range(MF):
                        mm = pe.matmul(ps[:, 6 + t // 2, (t % 2) * D:(t % 2 + 1) * D], fT[:, s, m, t * P:(t + 1) * P], W_2[:, m, :],
                                       start=(m == 0), stop=(m == MF - 1))
                    if t % 2:
                        mm.then_inc(down_done, 1)
            batches(pe, first, step)

        def act_ff(act):
            act.wait_ge(w3_in, 48)
            free_slot = lambda b: (lambda: act.wait_ge(up_done, b * MF))

            def step(b, s, last):
                for m in range(MF):
                    act.wait_ge(up_done, b * MF + m + 1)
                    if m == 0:
                        act.wait_ge(down_done, b * 2)
                    act.activation(fT[:, s, m, :], ps[:, 2 + m % 4, :], ACT.Relu, bias=b_1[:, m:m + 1]).then_inc(relu_done, 1)
                if not last:
                    f3.act(act, b + 1, 1 - s, free_slot(b))
            act.sem_inc(down_done, 2)
            batches(act, lambda b, s: f3.act(act, b, s, lambda: None), step)

        def dve_ff(dve):
            dve.wait_ge(norms_in, 16)

            def step(b, s, last):
                if not last:
                    f3.dve(dve, b + 1, 1 - s, lambda: dve.wait_ge(y2_sums, b * 2))
                dve.wait_ge(h0_steps, b * 2)
                for h in range(2):
                    dve.wait_ge(down_done, b * 2 + h + 1 + 2)
                    dve.tensor_tensor(y2[:, s, 2 * h:2 * h + 2, :], ps[:, 6 + h, :].rearrange("p (t d) -> p t d", d=D),
                                      f3.z[:, s, 2 * h:2 * h + 2, :], ALU.add).then_inc(y2_sums, 1)
                dve.wait_ge(y2_sums, b * 2 + 2)
                dve.tensor_tensor(y2[:, s], y2[:, s], b_2.unsqueeze(1).to_broadcast((P, TT, D)), ALU.add).then_inc(y2_added, 1)
                dve.wait_ge(y2_added, b + 1)
                for t in range(TT):
                    ins = dve.bn_stats(stats2[:, s, t, :], y2[:, s, t, :])
                ins.then_inc(y2_steps, 1)
                dve.wait_ge(y2_steps, b * 3 + 1)
                alone(dve)
                for t in range(TT):
                    ins = dve.bn_aggr(mv2[:, s, t, :], stats2[:, s, t, :])
                ins.then_inc(y2_steps, 1)
                dve.wait_ge(rstd2_steps, b * 2 + 2)
                for t in range(TT):
                    ins = dve.tensor_scalar(y2[:, s, t, :], y2[:, s, t, :], mv2[:, s, t, 0:1], rstd2[:, s, t:t + 1], ALU.subtract, ALU.mult)
                ins.then_inc(y2_steps, 1)
            batches(dve, lambda b, s: f3.dve(dve, b, s, lambda: None), step)
        y2_added = sem("y2_added")

        free[0] = PERSIST
        W_NOW, W_PAST = (take(3 * KC * D).rearrange("p (n k m) -> p n k m", n=3, k=KC) for _ in range(2))
        past = take(3 * KC).rearrange("p (n k) -> p n k", n=3)
        W_WO = take(KC * D).rearrange("p (k d) -> p k d", k=KC)
        vecs = take(5 * KC).rearrange("p (n k) -> p n k", n=5)
        wn = take(KC)
        decay = take(KC * S).rearrange("p (k t) -> p k t", k=KC)
        f4 = Front("wkv", pad=1)

        def rows4(n=S, slots=0):
            if slots:
                return take(slots * KC * n).rearrange("p (s k t) -> p s k t", s=slots, k=KC)
            return take(KC * n).rearrange("p (k t) -> p k t", k=KC)
        k_s, v_s, er_s = rows4(slots=2), rows4(slots=2), rows4(slots=2)
        PPm, AA, BB = rows4(S + 1), rows4(S + 1), rows4(S + 1)
        gap, gap0, gap1, e1b, e2b, e2v = (rows4() for _ in range(6))
        dif, dif0, dif1, e1, e2 = (rows4() for _ in range(5))
        num, nv, den, rden = (rows4() for _ in range(4))
        rT = rows4(slots=2)
        w4_in = sem("w4_in")
        w4_steps = sem("w4_steps")
        edges = sem("edges")
        firsts = sem("firsts")
        mixture = sem("mixture")
        kvr_done = sem("kvr_done")
        kvr_kept = sem("kvr_kept")
        scan_p = sem("scan_p")
        gaps = sem("gaps")
        decays = sem("decays")
        ev_ready = sem("ev_ready")
        scan_ab = sem("scan_ab")
        weights = sem("weights")
        ratio = sem("ratio")
        r_ready = sem("r_ready")
        wo_done = sem("wo_done")
        wo_read = sem("wo_read")

        def sp_wkv(sp):
            for dst, name in ((W_NOW, "w_kvr"), (W_WO, "w_wo"), (vecs, "vecs")):
                sp.dma_start(dst, a[name]).then_inc(w4_in, 16)

        def pool_wkv(pool):
            for s in range(2):
                pool.memset(f4.zT[:, s, :, 0:1], 0.0).then_inc(edges, 1)

            def step(b, s, ahead):
                if ahead >= 2:
                    f4.pool(pool, b + 2, s)
                pool.wait_ge(decays, b * 2 + 2)
                pool.tensor_tensor(e2v, e2b, v_s[:, s], ALU.mult).then_inc(ev_ready, 1)
                pool.wait_ge(weights, b * 2 + 2)
                pool.tensor_tensor(nv, e2, v_s[:, s], ALU.mult).then_inc(sums4, 1)
                pool.wait_ge(ratio, b * 3 + 1)
                pool.tensor_tensor(den, den, e2, ALU.add).then_inc(sums4, 1)
                pool.wait_ge(ratio, b * 3 + 2)
                pool.wait_ge(sums4, b * 3 + 1)
                pool.tensor_tensor(num, num, nv, ALU.add).then_inc(sums4, 1)
            pool.wait_ge(edges, 2)
            f4.pool(pool, 0, 0)
            f4.pool(pool, 1, 1)
            skewed(pool, step)

        def pe_wkv(pe):
            pe.sem_inc(kvr_done, 6)

            def kvr(b, s):
                pe.wait_ge(f4.zT_ready, b + 1)
                for n in range(3):
                    for m in range(KC):
                        pe.wait_ge(kvr_kept, b * 6 if n < 2 else b * 6 + m + 1)
                        for k in range(KC):
                            pe.matmul(ps[:, 2 + (2 * n + m) % 4, :], W_PAST[:, n, k, m * P:(m + 1) * P], f4.zT[:, s, k, 0:S],
                                      start=(k == 0), stop=False)
                            mm = pe.matmul(ps[:, 2 + (2 * n + m) % 4, :], W_NOW[:, n, k, m * P:(m + 1) * P], f4.zT[:, s, k, 1:],
                                           start=False, stop=(k == KC - 1))
                        mm.then_inc(kvr_done, 1)

            def out(b, s):
                pe.wait_ge(r_ready, b + 1)
                pe.wait_ge(wo_read, b * 2)
                for t in range(TT):
                    for k in range(KC):
                        mm = pe.matmul(ps[:, 6 + t // 2, (t % 2) * D:(t % 2 + 1) * D], rT[:, s, k, t * P:(t + 1) * P], W_WO[:, k, :],
                                       start=(k == 0), stop=(k == KC - 1))
                    if t % 2:
                        mm.then_inc(wo_done, 1)

            def step(b, s, ahead):
                if ahead >= 1:
                    kvr(b + 1, 1 - s)
                if ahead >= 2:
                    f4.pe(pe, b + 2, s)
                out(b, s)
            f4.pe(pe, 0, 0)
            pe.wait_ge(mixture, 7)
            pe.wait_ge(edges, 2)
            kvr(0, 0)
            f4.pe(pe, 1, 1)
            skewed(pe, step)

        def act_wkv(act):
            act.wait_ge(w4_in, 48)
            act.activation(wn, vecs[:, 3], ACT.Exp).then_inc(w4_steps, 1)

            def keep(b, s, first=False):
                for n, (dst, f, scale) in enumerate(((k_s, ACT.Copy, 1.0), (v_s, ACT.Copy, 1.0), (er_s, ACT.Exp, -1.0))):
                    if n == 0 and not first:
                        act.wait_ge(r_ready, b - 1)
                    for m in range(KC):
                        act.wait_ge(kvr_done, b * 6 + 2 * n + m + 1 + 6)
                        act.activation(dst[:, s, m, :], ps[:, 2 + (2 * n + m) % 4, :], f, scale=scale).then_inc(kvr_kept, 1)

            def step(b, s, ahead):
                act.wait_ge(gaps, b * 2 + 1)
                act.wait_ge(weights, b * 2)
                act.wait_ge(decays, b * 2)
                act.activation(gap0, gap, ACT.Relu, scale=-1.0).then_inc(clamps, 1)
                act.activation(gap1, gap, ACT.Relu).then_inc(clamps, 1)
                act.wait_ge(gaps, b * 2 + 2)
                act.activation(dif0, dif, ACT.Relu, scale=-1.0).then_inc(clamps, 1)
                act.activation(dif1, dif, ACT.Relu).then_inc(clamps, 1)
                act.wait_ge(r_ready, b)
                for n, (dst, x, done) in enumerate(((e1b, gap0, decays), (e2b, gap1, decays), (e1, dif0, weights), (e2, dif1, weights))):
                    act.wait_ge(clamps, b * 4 + n + 1)
                    act.activation(dst, x, ACT.Exp, scale=-1.0).then_inc(done, 1)
                if ahead >= 1:
                    keep(b + 1, 1 - s)
                if ahead >= 2:
                    f4.act(act, b + 2, s, lambda: act.wait_ge(kvr_done, (b + 2) * 6))
            act.wait_ge(edges, 2)
            f4.act(act, 0, 0, lambda: None)
            keep(0, 0, first=True)
            f4.act(act, 1, 1, lambda: None)
            skewed(act, step)

        def dve_wkv(dve):
            dve.sem_inc(wo_done, 2)
            f4.dve(dve, 0, 0, lambda: None)
            dve.wait_ge(w4_in, 48)
            dve.tensor_scalar(past, vecs[:, 0:3], -1.0, 1.0, ALU.mult, ALU.add).then_inc(mixture, 1)
            dve.wait_ge(mixture, 1)
            for n in range(3):
                for k in range(KC):
                    dve.tensor_scalar(W_PAST[:, n, k], W_NOW[:, n, k], past[:, n, k:k + 1], None, ALU.mult)
                    dve.drain()
                    dve.tensor_scalar(W_NOW[:, n, k], W_NOW[:, n, k], vecs[:, n, k:k + 1], None, ALU.mult).then_inc(mixture, 1)
            for t, x in ((PPm, -1e38), (AA, 0.0), (BB, 0.0)):
                dve.memset(t[:, :, 0:1], x).then_inc(firsts, 1)
            dve.wait_ge(w4_steps, 1)
            dve.tensor_scalar(wn, wn, -1.0, None, ALU.mult).then_inc(w4_steps, 1)
            dve.memset(decay, 0.0).then_inc(w4_steps, 1)
            dve.wait_ge(w4_steps, 3)
            for k in range(KC):
                dve.tensor_scalar(decay[:, k], decay[:, k], wn[:, k:k + 1], None, ALU.add).then_inc(w4_steps, 1)
            dve.wait_ge(w4_steps, 5)
            dve.wait_ge(firsts, 3)
            u_ = vecs[:, 4]

            def exponents(b, s):
                dve.wait_ge(kvr_kept, b * 6 + 2)
                for k in range(KC):
                    dve.tensor_tensor_scan(PPm[:, k, 1:], decay[:, k], k_s[:, s, k], -1e38, ALU.add, ALU.max).then_inc(scan_p, 1)
                dve.wait_ge(scan_p, b * 2 + 2)
                for k in range(KC):
                    ins = dve.scalar_tensor_tensor(out=gap[:, k], in0=PPm[:, k, 0:S], scalar=wn[:, k:k + 1], in1=k_s[:, s, k], op0=ALU.add, op1=ALU.subtract)
                ins.then_inc(gaps, 1)
                for k in range(KC):
                    ins = dve.scalar_tensor_tensor(out=dif[:, k], in0=PPm[:, k, 0:S], scalar=u_[:, k:k + 1], in1=k_s[:, s, k], op0=ALU.subtract, op1=ALU.subtract)
                ins.then_inc(gaps, 1)

            def step(b, s, ahead):
                if ahead >= 2:
                    f4.dve(dve, b + 2, s, lambda: dve.wait_ge(f4.turned, b + 1))
                dve.wait_ge(decays, b * 2 + 2)
                for k in range(KC):
                    dve.tensor_tensor_scan(BB[:, k, 1:], e1b[:, k], e2b[:, k], 0.0, ALU.mult, ALU.add).then_inc(scan_ab, 1)
                dve.wait_ge(weights, b * 2 + 2)
                dve.wait_ge(scan_ab, b * 4 + 2)
                dve.tensor_tensor(den, e1, BB[:, :, 0:S], ALU.mult).then_inc(ratio, 1)
                dve.wait_ge(ev_ready, b + 1)
                for k in range(KC):
                    dve.tensor_tensor_scan(AA[:, k, 1:], e1b[:, k], e2v[:, k], 0.0, ALU.mult, ALU.add).then_inc(scan_ab, 1)
                dve.wait_ge(scan_ab, b * 4 + 4)
                dve.tensor_tensor(num, e1, AA[:, :, 0:S], ALU.mult).then_inc(ratio, 1)
                dve.wait_ge(kvr_kept, b * 6 + 6)
                dve.wait_ge(sums4, b * 3 + 2)
                for k in range(KC):
                    ins = dve.scalar_tensor_tensor(out=den[:, k], in0=er_s[:, s, k], scalar=1.0, in1=den[:, k], op0=ALU.add, op1=ALU.mult)
                ins.then_inc(ratio, 1)
                dve.wait_ge(ratio, b * 3 + 3)
                dve.reciprocal(rden, den).then_inc(gated, 1)
                dve.wait_ge(gated, b + 1)
                dve.wait_ge(sums4, b * 3 + 3)
                dve.wait_ge(wo_done, b * 2)
                dve.tensor_tensor(rT[:, s], num, rden, ALU.mult).then_inc(r_ready, 1)
                if ahead >= 1:
                    exponents(b + 1, 1 - s)
                for h in range(2):
                    dve.wait_ge(wo_done, b * 2 + h + 1 + 2)
                    hh = H[:, bass.ds(b * TT + 2 * h, 2), :]
                    dve.tensor_tensor(hh, ps[:, 6 + h, :].rearrange("p (t d) -> p t d", d=D), hh, ALU.add).then_inc(wo_read, 1)
            f4.dve(dve, 1, 1, lambda: None)
            exponents(0, 0)
            skewed(dve, step)
        gated = sem("gated")
        clamps = sem("clamps")
        sums4 = sem("sums4")

        class Dispatch:

            def __init__(self, name, experts, picks):
                self.E, self.K = experts, picks
                blocks = B * S * picks // P + experts - 1
                self.N = -(-blocks // 8) * 8
                E, K, N = self.E, self.K, self.N
                te = lambda: take(NT * E).rearrange("p (t e) -> p t e", e=E)
                self.logits = te()
                self.rank = te()
                self.chosen = te()
                self.place = te()
                self.total = take(NT * E).rearrange("p (e t) -> p e t", e=E)
                self.run = take(NT * E).rearrange("p (e t) -> p e t", e=E)
                self.nblk = take(E)
                self.start = take(E)
                self.slot = take(NT * K).rearrange("p (t k) -> p t k", k=K)
                self.sloti = take(NT * K, I32).rearrange("p (t k) -> p t k", k=K)
                self.hi = take(NT * K).rearrange("p (t k) -> p t k", k=K)
                self.hii = take(NT * K, I32).rearrange("p (t k) -> p t k", k=K)
                self.lo = take(NT * K).rearrange("p (t k) -> p t k", k=K)
                self.expert = take(N)
                self.experti = take(N, I32)
                self.tokens = take(N, I32)
                self.tokf = take(N)
                self.steps = sem(name + "_steps")
                self.counted = sem(name + "_counted")
                self.hot_ready = sem(name + "_hot_ready")
                self.hot_scaled = sem(name + "_hot_scaled")
                self.listed = sem(name + "_listed")
                self.table = sem(name + "_table")
                self.n = 0

            def temps(self):
                E, K, N = self.E, self.K, self.N
                self.wide = take(max(N * E, NT * E * (E if K > 1 else 1)))
                self.hot_lo = take(4 * K * P, BF16).rearrange("p (s k n) -> p s k n", s=4, k=K)
                self.hot_hi = take(4 * K * N, BF16).rearrange("p (s k n) -> p s k n", s=4, k=K)
                self.hot_t = take(4 * 2 * K * N, BF16).rearrange("p (s k c n) -> p s k c n", s=4, k=K, c=2)

            def link(self, dve, ins):
                self.n += 1
                ins.then_inc(self.steps, 1)
                dve.wait_ge(self.steps, self.n)

            def dve(self, dve):
                E, K, N = self.E, self.K, self.N
                link = lambda ins: self.link(dve, ins)
                dve.wait_ge(self.counted, 1)
                link(dve.tensor_copy(self.total, ps[:, 1, 0:NT * E].rearrange("p (t e) -> p e t", e=E) if NT * E <= 512 else
                                     ps[:, 2:4, :].rearrange("p a (t e) -> p e (a t)", e=E)))
                link(dve.tensor_tensor_scan(self.run.rearrange("p e t -> p (e t)"), later[:, 0:NT * E],
                                            self.total.rearrange("p e t -> p (e t)"), 0.0, ALU.mult, ALU.add))
                wide = self.wide[:, 0:E * NT].rearrange("p (e t) -> p e t", e=E)
                link(dve.tensor_tensor(wide, self.run[:, :, NT - 1:NT].to_broadcast((P, E, NT)),
                                       tiles128.unsqueeze(1).to_broadcast((P, E, NT)), ALU.is_gt))
                link(dve.tensor_reduce(self.nblk, wide, AX.X, ALU.add))
                link(dve.tensor_tensor_scan(self.start, onesr[:, 0:E], self.nblk, 0.0, ALU.mult, ALU.add))
                link(dve.tensor_tensor(self.start, self.start, self.nblk, ALU.subtract))
                wide = self.wide[:, 0:N * E].rearrange("p (n e) -> p n e", e=E)
                link(dve.tensor_tensor(wide, self.start.unsqueeze(1).to_broadcast((P, N, E)),
                                       count[:, 0:N].unsqueeze(2).to_broadcast((P, N, E)), ALU.is_le))
                link(dve.tensor_reduce(self.expert, wide, AX.X, ALU.add))
                link(dve.tensor_scalar(self.expert, self.expert, -1.0, None, ALU.add))
                link(dve.tensor_copy(self.experti, self.expert))
                link(dve.tensor_tensor(self.run, self.run, self.total, ALU.subtract))
                link(dve.tensor_scalar(self.start, self.start, float(P), None, ALU.mult))
                link(dve.tensor_tensor(self.run, self.run, self.start.unsqueeze(2).to_broadcast((P, E, NT)), ALU.add))
                within = ps[:, 0, 0:NT * E].rearrange("p (t e) -> p t e", e=E) if NT * E <= 512 else None
                if within is not None:
                    link(dve.tensor_tensor(self.place, within, self.run.rearrange("p e t -> p t e"), ALU.add))
                else:
                    for h in range(2):
                        link(dve.tensor_tensor(self.place[:, h * NT // 2:(h + 1) * NT // 2, :], ps[:, h, :].rearrange("p (t e) -> p t e", e=E),
                                               self.run.rearrange("p e t -> p t e")[:, h * NT // 2:(h + 1) * NT // 2, :], ALU.add))
                wide = self.wide[:, 0:NT * E].rearrange("p (t e) -> p t e", e=E)
                for k in range(K):
                    if K > 1:
                        link(dve.scalar_tensor_tensor(out=wide, in0=self.rank, scalar=float(k), in1=self.place, op0=ALU.is_equal, op1=ALU.mult))
                    else:
                        link(dve.tensor_tensor(wide, self.chosen, self.place, ALU.mult))
                    link(dve.tensor_reduce(self.slot[:, :, k], wide, AX.X, ALU.add))
                link(dve.tensor_copy(self.sloti, self.slot))
                link(dve.tensor_scalar(self.hii, self.sloti, 7, None, ALU.arith_shift_right))
                link(dve.tensor_copy(self.hi, self.hii))
                link(dve.scalar_tensor_tensor(out=self.lo, in0=self.hi, scalar=-float(P), in1=self.slot, op0=ALU.mult, op1=ALU.add))
                with dve.Fori(0, NT // 4) as quad:
                    for s in range(4):
                        t = quad * 4 + s
                        dve.wait_ge(self.listed, t)
                        dve.tensor_tensor(self.hot_lo[:, s], countb[:, 0:P].unsqueeze(1).to_broadcast((P, K, P)),
                                          self.lo[:, bass.ds(t, 1), :].rearrange("p a k -> p (a k)").unsqueeze(2).to_broadcast((P, K, P)),
                                          ALU.is_equal)
                        dve.tensor_tensor(self.hot_hi[:, s], countb[:, 0:N].unsqueeze(1).to_broadcast((P, K, N)),
                                          self.hi[:, bass.ds(t, 1), :].rearrange("p a k -> p (a k)").unsqueeze(2).to_broadcast((P, K, N)),
                                          ALU.is_equal).then_inc(self.hot_ready, 1)
                dve.wait_ge(self.listed, NT + 3)
                c = [ps[:, 4, 0:N], ps[:, 5, 0:N]]
                link(dve.tensor_copy(self.tokf, c[1]))
                link(dve.scalar_tensor_tensor(out=self.tokf, in0=self.tokf, scalar=float(P), in1=c[0], op0=ALU.mult, op1=ALU.add))
                dve.tensor_copy(self.tokens, self.tokf).then_inc(self.table, 1)

            def act(self, act):
                with act.Fori(0, NT // 4) as quad:
                    for s in range(4):
                        t = quad * 4 + s
                        act.wait_ge(self.hot_ready, t + 1)
                        act.activation(self.hot_t[:, s, :, 0, :], self.hot_hi[:, s], ACT.Copy, scale=row_of)
                        act.activation(self.hot_t[:, s, :, 1, :], self.hot_hi[:, s], ACT.Copy, scale=tile_of[:, bass.ds(t, 1)]).then_inc(self.hot_scaled, 1)

            def pe(self, pe, ready, n):
                E, K, N = self.E, self.K, self.N
                pe.wait_ge(ready, n)
                flat = self.chosen.rearrange("p t e -> p (t e)")
                parts = NT * E // 512
                for h in range(parts):
                    pe.matmul(ps[:, h, :], before, flat[:, h * 512:(h + 1) * 512], start=True, stop=True)
                for h in range(parts):
                    mm = pe.matmul(ps[:, (1 if parts == 1 else 2 + h), :], ones, flat[:, h * 512:(h + 1) * 512], start=True, stop=True)
                mm.then_inc(self.counted, 1)
                for c in range(2):
                    pe.matmul(ps[:, 4 + c, 0:N], zerob, identb_wide[:, 0:N], start=True, stop=False, skip_group_check=True)
                pe.sem_inc(self.listed, 3)
                with pe.Fori(0, NT // 4) as quad:
                    for s in range(4):
                        t = quad * 4 + s
                        pe.wait_ge(self.hot_scaled, t + 1)
                        for k in range(K):
                            for c in range(2):
                                mm = pe.matmul(ps[:, 4 + c, 0:N], self.hot_lo[:, s, k, :], self.hot_t[:, s, k, c, :], start=False, stop=False,
                                               skip_group_check=True)
                        mm.then_inc(self.listed, 1)


        def blocks(e, n, step):
            for i in range(4):
                step(i, i, lambda m: m >= 0)
            with e.Fori(1, n // 4) as quad:
                for s in range(4):
                    step(quad * 4 + s, s, lambda m: True)
            for i in range(n, n + 3):
                step(i, i % 4, lambda m: m < n)

        class Gather:

            def __init__(self, name, d, source):
                self.d, self.source = d, source
                self.x = take(4 * 2 * D).rearrange("p (s n d) -> p s n d", s=4, n=2)
                self.at = take(4 * 2, I32).rearrange("p (s n) -> p s n", s=4)
                self.xT = take(4 * 2 * KC * P).rearrange("p (s n k t) -> p s n k t", s=4, n=2, k=KC)
                self.at_ready = sem(name + "_at_ready")
                self.x_in = [sem(f"{name}_x_in{s}") for s in range(4)]
                self.turned = sem(name + "_x_turned")
                self.ready = sem(name + "_xT_ready")

            def pool(self, pool):
                pool.wait_ge(self.d.table, 1)
                with pool.Fori(0, self.d.N // 8) as quad:
                    for s in range(4):
                        pool.wait_ge(self.x_in[s], quad * 32)
                        pool.tensor_copy(self.at[:, s, :], self.d.tokens[:, bass.ds((quad * 4 + s) * 2, 2)]).then_inc(self.at_ready, 1)
                        pool.wait_ge(self.at_ready, quad * 4 + s + 1)
                        pool.wait_ge(self.turned, quad * 4 + s + 1)
                        alone(pool)
                        for n in range(2):
                            pool.indirect_dma_start(out=self.x[:, s, n, :], out_offset=None, in_=self.source,
                                                    in_offset=bass.IndirectOffsetOnAxis(ap=self.at[:, s, n:n + 1].bitcast(U32), axis=0)
                                                    ).then_inc(self.x_in[s], 16)

            def pe(self, pe, i, s):
                pe.wait_ge(self.x_in[s], (i - s) * 8 + 32)
                pe.wait_ge(self.ready, i + 1)
                for n in range(2):
                    for k in range(KC):
                        mm = pe.transpose(ps[:, s % 2, (n * KC + k) * P:(n * KC + k + 1) * P], self.x[:, s, n, k * P:(k + 1) * P], ident)
                mm.then_inc(self.turned, 1)

            def act(self, act, i, s, used, n):
                act.wait_ge(self.turned, i + 1 + 4)
                act.wait_ge(used, n)
                act.activation(self.xT[:, s].rearrange("p n k t -> p (n k t)"), ps[:, s % 2, :], ACT.Copy).then_inc(self.ready, 1)

        free[0] = PERSIST
        E5, K5, INTER = 16, 4, 128
        GROUPS5, PER5 = 4, 4
        W_GU = take(KC * E5 * 2 * INTER).rearrange("p (k e m) -> p k e m", k=KC, e=E5)
        W_D = take(E5 * D).rearrange("p (e d) -> p e d", e=E5)
        consts = take(1280)
        later, tiles128, onesr, count, tile_of = (consts[:, x:y] for x, y in ((0, 1024), (1024, 1056), (1056, 1088), (1088, 1248), (1248, 1280)))
        before = take(P)
        ones = take(P)
        row_of = take(1)
        countb = take(160, BF16)
        zerob = take(P, BF16)
        identb_wide = countb
        CONST_END = mark()
        d5 = Dispatch("moe", E5, K5)
        weight = take(NT * K5).rearrange("p (t k) -> p t k", k=K5)
        e_bias = take(E5)
        STAGE5 = mark()
        W_R = take(KC * E5).rearrange("p (k e) -> p k e", k=KC)
        W_SG, W_SU, W_SD = (take(KC * D).rearrange("p (k d) -> p k d", k=KC) for _ in range(3))
        f5 = Front("moe")
        z_dram = nc.dram_tensor("z_dram", (B * S, D), F32, kind="Internal").ap()
        sg = take(2 * S).rearrange("p (m t) -> p m t", m=2)
        shT = take(2 * KC * S).rearrange("p (s m t) -> p s m t", s=2, m=KC)
        w5_in = sem("w5_in")
        wx5_in = sem("wx5_in")
        z_out = [sem(f"z_out{s}") for s in range(2)]
        lg_done = sem("lg_done")
        lg_read = sem("lg_read")
        gate_done = sem("gate_done")
        up5_done = sem("up5_done")
        silu_done = sem("silu_done")
        sh_ready = sem("sh_ready")
        sd_done = sem("sd_done")
        sd_read = sem("sd_read")

        def sp_shared(sp):
            for dst, name in ((W_R, "w_r"), (W_SG, "w_sg"), (W_SU, "w_su"), (W_SD, "w_sd"), (before, "before"), (row_of, "row_of")):
                sp.dma_start(dst, a[name]).then_inc(w5_in, 16)
            sp.dma_start(consts, a["consts"].to_broadcast((P, 1280))).then_inc(w5_in, 16)
            sp.dma_start(e_bias, a["e_bias"].to_broadcast((P, E5))).then_inc(w5_in, 16)
            for dst, name in ((W_GU, "w_gu"), (W_D, "w_d")):
                sp.dma_start(dst, a[name]).then_inc(wx5_in, 16)
            with sp.Fori(0, B // 2) as pair:
                for s in range(2):
                    b = pair * 2 + s
                    sp.wait_ge(f5.z_ready, b + 1)
                    sp.dma_start(z_dram[bass.ds(b * S, S), :].rearrange("(t p) d -> p t d", p=P), f5.z[:, s]).then_inc(z_out[s], 16)
            for s in range(2):
                sp.wait_ge(z_out[s], 16 * (B // 2))

        def pool_shared(pool):
            pool.memset(ones, 1.0)

            def step(b, s, last):
                if not last:
                    f5.pool(pool, b + 1, 1 - s)
            batches(pool, lambda b, s: f5.pool(pool, b, s), step)

        def pe_shared(pe):
            pe.wait_ge(w5_in, 16 * 8)
            pe.sem_inc(sd_done, 2)

            def step(b, s, last):
                zT = f5.zT
                pe.wait_ge(f5.zT_ready, b + 1)
                pe.wait_ge(lg_read, b)
                for t in range(TT):
                    for k in range(KC):
                        mm = pe.matmul(ps[:, 5, t * E5:(t + 1) * E5], zT[:, s, k, t * P:(t + 1) * P], W_R[:, k, :], start=(k == 0), stop=(k == KC - 1))
                mm.then_inc(lg_done, 1)
                for m in range(KC):
                    pe.wait_ge(silu_done, b * 2)
                    for k in range(KC):
                        mm = pe.matmul(ps[:, 2 + 2 * m, :], W_SG[:, k, m * P:(m + 1) * P], zT[:, s, k, :], start=(k == 0), stop=(k == KC - 1))
                    mm.then_inc(gate_done, 1)
                    pe.wait_ge(sh_ready, b * 2 + m)
                    for k in range(KC):
                        mm = pe.matmul(ps[:, 3, :], W_SU[:, k, m * P:(m + 1) * P], zT[:, s, k, :], start=(k == 0), stop=(k == KC - 1))
                    mm.then_inc(up5_done, 1)
                if not last:
                    f5.pe(pe, b + 1, 1 - s)
                pe.wait_ge(sh_ready, b * 2 + 2)
                pe.wait_ge(sd_read, b * 2)
                for t in range(TT):
                    for k in range(KC):
                        mm = pe.matmul(ps[:, 6 + t // 2, (t % 2) * D:(t % 2 + 1) * D], shT[:, s, k, t * P:(t + 1) * P], W_SD[:, k, :],
                                       start=(k == 0), stop=(k == KC - 1))
                    if t % 2:
                        mm.then_inc(sd_done, 1)
            batches(pe, lambda b, s: f5.pe(pe, b, s), step)

        def act_shared(act):
            def step(b, s, last):
                for m in range(KC):
                    act.wait_ge(gate_done, b * 2 + m + 1)
                    act.wait_ge(sh_ready, b * 2)
                    act.activation(sg[:, m, :], ps[:, 2 + 2 * m, :], ACT.Silu).then_inc(silu_done, 1)
                if not last:
                    f5.act(act, b + 1, 1 - s, lambda: act.wait_ge(up5_done, b * 2))
            batches(act, lambda b, s: f5.act(act, b, s, lambda: None), step)

        def dve_shared(dve):
            dve.memset(zerob, 0.0)
            dve.wait_ge(w5_in, 16 * 8)
            dve.tensor_copy(countb, count)

            def step(b, s, last):
                if not last:
                    def slot_free():
                        dve.wait_ge(f5.turned, b)
                        dve.wait_ge(z_out[1 - s], b * 8 if s == 0 else (b - 1) * 8 + 16)
                    f5.dve(dve, b + 1, 1 - s, slot_free)
                dve.wait_ge(lg_done, b + 1)
                dve.tensor_copy(d5.logits[:, bass.ds(b * TT, TT), :], ps[:, 5, 0:TT * E5].rearrange("p (t e) -> p t e", e=E5)).then_inc(lg_read, 1)
                for m in range(KC):
                    dve.wait_ge(up5_done, b * 2 + m + 1)
                    dve.wait_ge(silu_done, b * 2 + m + 1)
                    dve.wait_ge(sd_done, b * 2)
                    dve.tensor_tensor(shT[:, s, m, :], sg[:, m, :], ps[:, 3, :], ALU.mult).then_inc(sh_ready, 1)
                for h in range(2):
                    dve.wait_ge(sd_done, b * 2 + h + 1 + 2)
                    hh = H[:, bass.ds(b * TT + 2 * h, 2), :]
                    dve.tensor_tensor(hh, ps[:, 6 + h, :].rearrange("p (t d) -> p t d", d=D), hh, ALU.add).then_inc(sd_read, 1)
            batches(dve, lambda b, s: f5.dve(dve, b, s, lambda: None), step)

        free[0] = STAGE5
        d5.temps()
        sc = take(NT * E5).rearrange("p (t e) -> p t e", e=E5)
        pairs = take(NT * GROUPS5 * 6).rearrange("p (t g n) -> p t g n", g=GROUPS5, n=6)
        gsum = take(NT * GROUPS5).rearrange("p (t g) -> p t g", g=GROUPS5)
        gcmp = take(NT * GROUPS5 * GROUPS5).rearrange("p (t g n) -> p t g n", g=GROUPS5, n=GROUPS5)
        grank = take(NT * GROUPS5).rearrange("p (t g) -> p t g", g=GROUPS5)
        wsum = take(NT)
        scores_ready = sem("scores_ready")
        chosen5 = sem("chosen5")

        def sp_route5(sp):
            sp.wait_ge(wx5_in, 32)

        def pool_route5(pool):
            pass

        def act_route5(act):
            act.activation(d5.logits.rearrange("p t e -> p (t e)"), d5.logits.rearrange("p t e -> p (t e)"), ACT.Sigmoid).then_inc(scores_ready, 1)
            d5.act(act)

        def pe_route5(pe):
            d5.pe(pe, chosen5, 1)

        def ranks(link, dve, values, compared, rank, n):
            for j in range(n):
                v = values[:, :, j:j + 1]
                dve.tensor_tensor(compared[:, :, 0:j + 1, j], v.to_broadcast((P, NT, j + 1)), values[:, :, 0:j + 1], ALU.is_gt)
                if j < n - 1:
                    dve.tensor_tensor(compared[:, :, j + 1:n, j], v.to_broadcast((P, NT, n - 1 - j)), values[:, :, j + 1:n], ALU.is_ge)
            link(dve.drain())
            link(dve.tensor_reduce(rank, compared, AX.X, ALU.add))

        def dve_route5(dve):
            link = lambda ins: d5.link(dve, ins)
            dve.wait_ge(scores_ready, 1)
            link(dve.tensor_tensor(sc, d5.logits, e_bias.unsqueeze(1).to_broadcast((P, NT, E5)), ALU.add))
            g4 = sc.rearrange("p t (g i) -> p (t g) i", i=PER5)
            flat = pairs.rearrange("p t g n -> p (t g) n")
            n = 0
            for i in range(PER5):
                for j in range(i + 1, PER5):
                    ins = dve.tensor_tensor(flat[:, :, n], g4[:, :, i], g4[:, :, j], ALU.add)
                    n += 1
            link(dve.drain())
            link(dve.tensor_reduce(gsum, pairs, AX.X, ALU.max))
            ranks(link, dve, gsum, gcmp, grank, GROUPS5)
            link(dve.tensor_scalar(grank, grank, 2.0, None, ALU.is_lt))
            link(dve.tensor_tensor(sc.rearrange("p t (g i) -> p (t g) i", i=PER5), sc.rearrange("p t (g i) -> p (t g) i", i=PER5),
                                   grank.rearrange("p t g -> p (t g)").unsqueeze(2).to_broadcast((P, NT * GROUPS5, PER5)), ALU.mult))
            ranks(link, dve, sc, d5.wide.rearrange("p (t g n) -> p t g n", g=E5, n=E5), d5.rank, E5)
            dve.tensor_scalar(d5.chosen, d5.rank, float(K5), None, ALU.is_lt).then_inc(chosen5, 1)
            dve.wait_ge(chosen5, 1)
            link(dve.tensor_tensor(sc, d5.logits, d5.chosen, ALU.mult))
            link(dve.tensor_reduce(wsum, sc, AX.X, ALU.add))
            link(dve.tensor_scalar(wsum, wsum, 1e-20, None, ALU.add))
            link(dve.reciprocal(wsum, wsum))
            link(dve.tensor_tensor(sc, sc, wsum.unsqueeze(2).to_broadcast((P, NT, E5)), ALU.mult))
            link(dve.tensor_scalar(sc, sc, 2.5, None, ALU.mult))
            wide = d5.wide[:, 0:NT * E5].rearrange("p (t e) -> p t e", e=E5)
            for k in range(K5):
                link(dve.scalar_tensor_tensor(out=wide, in0=d5.rank, scalar=float(k), in1=sc, op0=ALU.is_equal, op1=ALU.mult))
                link(dve.tensor_reduce(weight[:, :, k], wide, AX.X, ALU.add))
            d5.dve(dve)

        free[0] = STAGE5
        g7 = Gather("moe", d5, z_dram)
        sg7, h7, hT7 = (take(4 * 2 * P).rearrange("p (s n i) -> p s n i", s=4, n=2) for _ in range(3))
        y7 = take(4 * 2 * D).rearrange("p (s n d) -> p s n d", s=4, n=2)
        y_dram = nc.dram_tensor("y_dram", (d5.N * P, D), F32, kind="Internal").ap()
        gu_done = sem("gu_done")
        silu7 = sem("silu7")
        h7_ready = sem("h7_ready")
        h7_turned = sem("h7_turned")
        hT7_ready = sem("hT7_ready")
        dn_done = sem("dn_done")
        y7_ready = sem("y7_ready")
        y7_out = [sem(f"y7_out{s}") for s in range(4)]
        STEPS7 = d5.N // 2

        def store_rows(sp, steps, ready, y, out_sems):
            with sp.Fori(0, steps // 4) as quad:
                for s in range(4):
                    i = quad * 4 + s
                    sp.wait_ge(ready, i + 1 + 2)
                    sp.dma_start(y_dram[bass.ds(i * 2 * P, 2 * P), :].rearrange("(n p) d -> p n d", p=P), y[:, s]).then_inc(out_sems[s], 16)
            for s in range(4):
                sp.wait_ge(out_sems[s], 16 * (steps // 4))

        def sp_experts(sp):
            store_rows(sp, STEPS7, y7_ready, y7, y7_out)

        def pool_experts(pool):
            g7.pool(pool)

        def expert_of(e, d, block, last):
            return e.value_load(d.experti[0:1, bass.ds(block, 1)], min_val=0, max_val=last)

        def pe_experts(pe):
            pe.sem_inc(g7.turned, 4)
            pe.sem_inc(gu_done, 4)

            def step(i, s, there):
                if there(i - 1):
                    up = [expert_of(pe, d5, (i - 1) * 2 + n, E5 - 1) for n in range(2)]
                if there(i - 3):
                    down = [expert_of(pe, d5, (i - 3) * 2 + n, E5 - 1) for n in range(2)]
                if there(i):
                    g7.pe(pe, i, s)
                if there(i - 1):
                    c = (s - 1) % 4
                    pe.wait_ge(g7.ready, i + 2)
                    pe.wait_ge(h7_ready, i)
                    for n in range(2):
                        for k in range(KC):
                            mm = pe.matmul(ps[:, 2 + c % 2, n * 2 * INTER:(n + 1) * 2 * INTER], g7.xT[:, c, n, k, :],
                                           W_GU[:, k, bass.ds(up[n], 1), :].rearrange("p a m -> p (a m)"), start=(k == 0), stop=(k == KC - 1))
                    mm.then_inc(gu_done, 1)
                if there(i - 2):
                    c = (s - 2) % 4
                    pe.wait_ge(h7_ready, i - 1 + 2)
                    pe.wait_ge(hT7_ready, i - 1)
                    for n in range(2):
                        mm = pe.transpose(ps[:, 4 + c % 2, n * P:(n + 1) * P], h7[:, c, n, :], ident)
                    mm.then_inc(h7_turned, 1)
                if there(i - 3):
                    c = (s - 3) % 4
                    pe.wait_ge(hT7_ready, i - 2 + 2)
                    pe.wait_ge(y7_ready, i - 2)
                    for n in range(2):
                        mm = pe.matmul(ps[:, 6 + c % 2, n * D:(n + 1) * D], hT7[:, c, n, :],
                                       W_D[:, bass.ds(down[n], 1), :].rearrange("p a d -> p (a d)"), start=True, stop=True)
                    mm.then_inc(dn_done, 1)
            blocks(pe, STEPS7, step)

        def act_experts(act):
            act.sem_inc(g7.ready, 2)

            def step(i, s, there):
                if there(i):
                    g7.act(act, i, s, gu_done, i + 1)
                if there(i - 1):
                    c = (s - 1) % 4
                    act.wait_ge(gu_done, i + 4)
                    if not isinstance(i, int) or i > 2:
                        act.wait_ge(h7_ready, i - 2)
                    act.activation(sg7[:, c], ps[:, 2 + c % 2, :].rearrange("p (n x) -> p n x", n=2)[:, :, 0:INTER], ACT.Silu).then_inc(silu7, 1)
            blocks(act, STEPS7, step)

        def dve_experts(dve):
            for x in (h7_ready, hT7_ready, y7_ready):
                dve.sem_inc(x, 2)
            dve.sem_inc(h7_turned, 4)

            def step(i, s, there):
                if there(i - 1):
                    c = (s - 1) % 4
                    dve.wait_ge(silu7, i)
                    dve.wait_ge(h7_turned, i)
                    dve.tensor_tensor(h7[:, c], sg7[:, c], ps[:, 2 + c % 2, :].rearrange("p (n x) -> p n x", n=2)[:, :, INTER:],
                                      ALU.mult).then_inc(h7_ready, 1)
                if there(i - 2):
                    c = (s - 2) % 4
                    dve.wait_ge(h7_turned, i - 1 + 4)
                    dve.tensor_copy(hT7[:, c].rearrange("p n t -> p (n t)"), ps[:, 4 + c % 2, 0:2 * P]).then_inc(hT7_ready, 1)
                if there(i - 3):
                    c = (s - 3) % 4
                    dve.wait_ge(dn_done, i - 2)
                    dve.wait_ge(y7_out[c], (i - 3 - c) * 4)
                    dve.tensor_copy(y7[:, c].rearrange("p n d -> p (n d)"), ps[:, 6 + c % 2, :]).then_inc(y7_ready, 1)
            blocks(dve, STEPS7, step)

        def nothing(e):
            pass

        run([(sp_embed, pool_embed, act_embed, dve_embed, pe_embed),
             (sp_attn, pool_attn, act_attn, dve_attn, pe_attn),
             (sp_ff, pool_ff, act_ff, dve_ff, pe_ff),
             (sp_wkv, pool_wkv, act_wkv, dve_wkv, pe_wkv),
             (sp_shared, pool_shared, act_shared, dve_shared, pe_shared),
             (sp_route5, pool_route5, act_route5, dve_route5, pe_route5),
             (sp_experts, pool_experts, act_experts, dve_experts, pe_experts)][:stop])

        passed[0] = sem("passed2")

        free[0] = STAGE5
        back = take(2 * TT * K5 * D).rearrange("p (a s k d) -> p a s k d", a=2, s=TT, k=K5)
        at8 = take(2 * TT * K5, I32).rearrange("p (a s k) -> p a s k", a=2, s=TT)
        at8_ready = sem("at8_ready")
        back_in = [[[sem(f"back_in{a}{s}{k}") for k in range(K5)] for s in range(TT)] for a in range(2)]
        added = sem("added")

        def fetch_rows(pool, b, a):
            pool.wait_ge(added, (b + 1) * K5 * TT)
            pool.tensor_copy(at8[:, a], d5.sloti[:, bass.ds(b * TT, TT), :]).then_inc(at8_ready, 1)
            pool.wait_ge(at8_ready, b + 1)
            alone(pool)
            for k in range(K5):
                for s in range(TT):
                    pool.indirect_dma_start(out=back[:, a, s, k, :], out_offset=None, in_=y_dram,
                                            in_offset=bass.IndirectOffsetOnAxis(ap=at8[:, a, s, k:k + 1].bitcast(U32), axis=0)
                                            ).then_inc(back_in[a][s][k], 16)

        def add_rows(dve, b, k, a):
            for s in range(TT):
                t = b * TT + s
                h = H[:, bass.ds(t, 1), :].rearrange("p a d -> p (a d)")
                dve.wait_ge(back_in[a][s][k], (b - a) * 8 + 16)
                dve.wait_ge(added, (b * K5 + k) * TT + (s - TT + 1 if k else 0) + 2 * K5 * TT)
                dve.scalar_tensor_tensor(out=h, in0=back[:, a, s, k, :], scalar=weight[:, bass.ds(t, 1), k:k + 1].rearrange("p a k -> p (a k)"),
                                         in1=h, op0=ALU.mult, op1=ALU.add).then_inc(added, 1)

        HH = NH // KC
        NORM = P + HH
        W_QKV = take(KC * 3 * D).rearrange("p (k m) -> p k m", k=KC)
        W_OUT = take(KC * D).rearrange("p (k d) -> p k d", k=KC)
        qk_gain = take(2 * D)
        b_out = take(D)
        same_head = take(P)
        head_of = take(HH)
        mhalf8 = take(2 * TT).rearrange("p (t n) -> p t n", n=2)
        f9 = Front("lin")
        qk9 = take(2 * TT * 2 * D).rearrange("p (s t m) -> p s t m", s=2, t=TT)
        v9 = take(2 * TT * KC * (P + 2)).rearrange("p (s t c m) -> p s t c m", s=2, t=TT, c=KC)
        squares = take(2 * D).rearrange("p (n d) -> p n d", n=2)
        ssq = take(2 * TT * 2).rearrange("p (s t n) -> p s t n", s=2, t=TT)
        kv9 = take(2 * KC * NORM).rearrange("p (s c m) -> p s c m", s=2, c=KC)
        qT9 = take(KC * S).rearrange("p (c t) -> p c t", c=KC)
        att9 = take(TT * D).rearrange("p (t d) -> p t d", d=D)
        attT9 = take(KC * S).rearrange("p (c t) -> p c t", c=KC)
        norm9 = take(2 * NH).rearrange("p (s c h) -> p s c h", s=2, c=KC)
        w9_in = sem("w9_in")
        ones9 = sem("ones9")
        qkv_done = sem("qkv_done")
        qkv_kept = sem("qkv_kept")
        v_kept = sem("v_kept")
        squared = sem("squared")
        rms_steps = sem("rms_steps")
        scaled9 = sem("scaled9")
        relu9 = sem("relu9")
        kv_done = sem("kv_done")
        kv_ready = sem("kv_ready")
        q_turned = sem("q_turned")
        qT_ready = sem("qT_ready")
        att_done = sem("att_done")
        norm_steps = sem("norm_steps")
        att_ready = sem("att_ready")
        att_turned = sem("att_turned")
        attT_ready = sem("attT_ready")
        proj_done = sem("proj_done")
        proj_read = sem("proj_read")
        biased9 = sem("biased9")

        def sp_linear(sp):
            for dst, name in ((W_QKV, "w_qkv"), (W_OUT, "w_out"), (same_head, "same_head"), (head_of, "head_of")):
                sp.dma_start(dst, a[name]).then_inc(w9_in, 16)
            sp.dma_start(qk_gain, a["qk_gain"].to_broadcast((P, 2 * D))).then_inc(w9_in, 16)
            sp.dma_start(b_out, a["b_out"].to_broadcast((P, D))).then_inc(w9_in, 16)

        def pool_linear(pool):
            pool.memset(mhalf8, -0.5).then_inc(ones9, 1)
            pool.wait_ge(ones9, 1)
            pool.memset(v9[:, :, :, :, P:P + 1].rearrange("p s t c m -> p (s t c) m"), 1.0).then_inc(ones9, 1)
            pool.wait_ge(w9_in, 96)

            def mean_squares(n, s):
                pool.wait_ge(squared, n * TT * 2 + TT * 2)
                alone(pool)
                pool.tensor_scalar(ssq[:, s], ssq[:, s], 1.0 / D, 1e-6, ALU.mult, ALU.add).then_inc(rms_steps, 1)
                pool.wait_ge(rms_steps, n * 2 + 1)
                pool.tensor_tensor(ssq[:, s], ssq[:, s], mhalf8, ALU.pow).then_inc(rms_steps, 1)

            def step(b, s, ahead):
                if ahead >= 3:
                    fetch_rows(pool, b + 3, 1 - s)
                if ahead >= 1:
                    mean_squares(b + 1, 1 - s)
                if ahead >= 2:
                    f9.pool(pool, b + 2, s)
                pool.wait_ge(proj_read, b * 2 + 2)
                h = H[:, bass.ds(b * TT, TT), :]
                pool.tensor_tensor(h, h, b_out.unsqueeze(1).to_broadcast((P, TT, D)), ALU.add).then_inc(biased9, 1)
            fetch_rows(pool, 0, 0)
            f9.pool(pool, 0, 0)
            fetch_rows(pool, 1, 1)
            f9.pool(pool, 1, 1)
            mean_squares(0, 0)
            fetch_rows(pool, 2, 0)
            skewed(pool, step)

        def pe_linear(pe):
            pe.wait_ge(w9_in, 96)

            def project(n, s, t, first=False):
                bank = 4 - 2 * (t % 2)
                if t == 0:
                    pe.wait_ge(f9.zT_ready, n + 1)
                if not first or t >= 2:
                    pe.wait_ge(qkv_kept, n * TT + t - 1)
                    pe.wait_ge(v_kept, n * TT + t - 1)
                if not first and t < 2:
                    pe.wait_ge(*((attT_ready, n - 1) if t == 0 else (qT_ready, n)))
                zT = f9.zT
                for k in range(KC):
                    pe.matmul(ps[:, bank, :], zT[:, s, k, t * P:(t + 1) * P], W_QKV[:, k, 0:2 * D], start=(k == 0), stop=(k == KC - 1))
                for k in range(KC):
                    mm = pe.matmul(ps[:, bank + 1, 0:D], zT[:, s, k, t * P:(t + 1) * P], W_QKV[:, k, 2 * D:3 * D], start=(k == 0), stop=(k == KC - 1))
                mm.then_inc(qkv_done, 1)

            def attend(b, s, t):
                if t >= 2:
                    pe.wait_ge(att_ready, b * TT + t - 1)
                for c in range(KC):
                    mm = pe.matmul(ps[:, 7 - t % 2, c * 160:c * 160 + NORM], qT9[:, c, t * P:(t + 1) * P], kv9[:, s, c, :], start=True, stop=True)
                mm.then_inc(att_done, 1)

            def step(b, s, ahead):
                pe.wait_ge(relu9, b + 1)
                pe.wait_ge(qkv_kept, b * TT + TT)
                pe.wait_ge(v_kept, b * TT + TT)
                for t in range(TT):
                    for c in range(KC):
                        mm = pe.transpose(ps[:, 2 + c, t * P:(t + 1) * P], qk9[:, s, t, c * P:(c + 1) * P], ident)
                mm.then_inc(q_turned, 1)
                pe.wait_ge(proj_read, b * 2)
                for c in range(KC):
                    for t in range(TT):
                        mm = pe.matmul(ps[:, 6, c * 160:c * 160 + P + 1], qk9[:, s, t, D + c * P:D + (c + 1) * P], v9[:, s, t, c, 0:P + 1],
                                       start=(t == 0), stop=(t == TT - 1))
                mm.then_inc(kv_done, 1)
                if ahead >= 1:
                    f9.pe(pe, b + 1, 1 - s)
                pe.wait_ge(kv_ready, b + 1)
                pe.wait_ge(qT_ready, b + 1)
                attend(b, s, 0)
                attend(b, s, 1)
                if ahead >= 1:
                    project(b + 1, 1 - s, 0)
                    project(b + 1, 1 - s, 1)
                attend(b, s, 2)
                attend(b, s, 3)
                if ahead >= 1:
                    project(b + 1, 1 - s, 2)
                if ahead >= 1:
                    project(b + 1, 1 - s, 3)
                    pe.wait_ge(qkv_kept, b * TT + TT + 3)
                    pe.wait_ge(v_kept, b * TT + TT + 3)
                for t in range(TT):
                    pe.wait_ge(att_ready, b * TT + t + 1)
                    for c in range(KC):
                        mm = pe.transpose(ps[:, 4 + c, t * P:(t + 1) * P], att9[:, t, c * P:(c + 1) * P], ident)
                mm.then_inc(att_turned, 1)
                pe.wait_ge(attT_ready, b + 1)
                for t in range(TT):
                    for c in range(KC):
                        mm = pe.matmul(ps[:, 6 + t // 2, (t % 2) * D:(t % 2 + 1) * D], attT9[:, c, t * P:(t + 1) * P], W_OUT[:, c, :],
                                       start=(c == 0), stop=(c == KC - 1))
                    if t % 2:
                        mm.then_inc(proj_done, 1)
            f9.pe(pe, 0, 0)
            for t in range(TT):
                project(0, 0, t, first=True)
            skewed(pe, step)

        def act_linear(act):
            def keep(n, s, first=False):
                for t in range(TT):
                    i = n * TT + t
                    act.wait_ge(qkv_done, i + 1)
                    if t == 0 and not first:
                        act.wait_ge(scaled9, n - 1)
                    act.activation(v9[:, s, t, :, 0:P], ps[:, 5 - 2 * (t % 2), 0:D].rearrange("p (c m) -> p c m", c=KC), ACT.Copy).then_inc(v_kept, 1)
                    act.wait_ge(qkv_kept, i + 1)
                    act.wait_ge(squared, i * 2)
                    for k in range(2):
                        act.activation(squares[:, k], qk9[:, s, t, k * D:(k + 1) * D], ACT.Square,
                                       accum_out=ssq[:, s, t, k:k + 1]).then_inc(squared, 1)

            def relu(n, s):
                act.wait_ge(scaled9, n + 1)
                act.activation(qk9[:, s], qk9[:, s], ACT.Relu).then_inc(relu9, 1)

            def step(b, s, ahead):
                act.wait_ge(q_turned, b + 1)
                act.wait_ge(proj_done, b * 2)
                act.activation(qT9, ps[:, 2:4, :], ACT.Copy).then_inc(qT_ready, 1)
                if ahead >= 1:
                    f9.act(act, b + 1, 1 - s, lambda: act.wait_ge(qkv_done, b * TT))
                    keep(b + 1, 1 - s)
                act.wait_ge(att_turned, b + 1)
                act.activation(attT9, ps[:, 4:6, :], ACT.Copy).then_inc(attT_ready, 1)
                if ahead >= 1:
                    relu(b + 1, 1 - s)
            act.wait_ge(ones9, 2)
            f9.act(act, 0, 0, lambda: None)
            keep(0, 0, first=True)
            relu(0, 0)
            skewed(act, step)

        def dve_linear(dve):
            dve.wait_ge(w9_in, 96)
            dve.sem_inc(added, 2 * K5 * TT)

            def front(b, s, slot_free):
                dve.wait_ge(added, (b + 3) * K5 * TT)
                alone(dve)
                f9.dve(dve, b, s, slot_free)

            def keep(n, s, t):
                dve.wait_ge(qkv_done, n * TT + t + 1)
                dve.tensor_copy(qk9[:, s, t, :], ps[:, 4 - 2 * (t % 2), :]).then_inc(qkv_kept, 1)

            def scale(n, s):
                dve.wait_ge(rms_steps, n * 2 + 2)
                dve.wait_ge(qkv_kept, n * TT + TT)
                for t in range(TT):
                    for k in range(2):
                        x = qk9[:, s, t, k * D:(k + 1) * D]
                        ins = dve.scalar_tensor_tensor(out=x, in0=x, scalar=ssq[:, s, t, k:k + 1], in1=qk_gain[:, k * D:(k + 1) * D],
                                                       op0=ALU.mult, op1=ALU.mult)
                ins.then_inc(scaled9, 1)

            def normed(b, t):
                i = b * TT + t
                x = ps[:, 7 - t % 2, 0:320].rearrange("p (c m) -> p c m", c=KC)
                dve.wait_ge(att_done, i + 1)
                dve.tensor_scalar(norm9[:, 0], x[:, :, P:NORM], 1e-6, None, ALU.add).then_inc(norm_steps, 1)
                dve.wait_ge(norm_steps, i * 2 + 1)
                dve.reciprocal(norm9[:, 1], norm9[:, 0]).then_inc(norm_steps, 1)
                dve.wait_ge(norm_steps, i * 2 + 2)
                dve.wait_ge(att_turned, b)
                for c in range(KC):
                    ins = dve.tensor_tensor(att9[:, t, c * P:(c + 1) * P].rearrange("p (h d) -> p h d", d=HD),
                                            x[:, c, 0:P].rearrange("p (h d) -> p h d", d=HD),
                                            norm9[:, 1, c, :].unsqueeze(2).to_broadcast((P, HH, HD)), ALU.mult)
                ins.then_inc(att_ready, 1)

            def step(b, s, ahead):
                dve.wait_ge(kv_done, b + 1)
                for c in range(KC):
                    dve.tensor_tensor(kv9[:, s, c, 0:P], ps[:, 6, c * 160:c * 160 + P], same_head, ALU.mult)
                    ins = dve.tensor_scalar(kv9[:, s, c, P:NORM], head_of, ps[:, 6, c * 160 + P:c * 160 + P + 1], None, ALU.mult)
                ins.then_inc(kv_ready, 1)
                def look(t):
                    if ahead >= 2:
                        add_rows(dve, b + 2, t, s)
                    if ahead >= 1:
                        keep(b + 1, 1 - s, t)
                normed(b, 0)
                normed(b, 1)
                look(0)
                look(1)
                normed(b, 2)
                normed(b, 3)
                look(2)
                look(3)
                if ahead >= 1:
                    scale(b + 1, 1 - s)
                for h in range(2):
                    dve.wait_ge(proj_done, b * 2 + h + 1)
                    hh = H[:, bass.ds(b * TT + 2 * h, 2), :]
                    dve.tensor_tensor(hh, ps[:, 6 + h, :].rearrange("p (t d) -> p t d", d=D), hh, ALU.add).then_inc(proj_read, 1)
                if ahead >= 2:
                    front(b + 2, s, lambda: dve.wait_ge(f9.turned, b + 1))
            for n in range(2):
                for k in range(K5):
                    add_rows(dve, n, k, n)
                front(n, n, lambda: None)
            for t in range(TT):
                keep(0, 0, t)
            scale(0, 0)
            skewed(dve, step)

        free[0] = CONST_END
        E10, HID = 32, 64
        W_E1 = take(KC * E10 * HID).rearrange("p (k e m) -> p k e m", k=KC, e=E10)
        W_E2 = take(E10 * D).rearrange("p (e d) -> p e d", e=E10)
        b_e1 = take(E10 * HID).rearrange("p (e m) -> p e m", e=E10)
        d10 = Dispatch("top", E10, 1)
        STAGE10 = mark()
        W_R10 = take(KC * E10).rearrange("p (k e) -> p k e", k=KC)
        b_r10 = take(E10)
        f10 = Front("top")
        w10_in = sem("w10_in")
        wx10_in = sem("wx10_in")
        z10_out = [sem(f"z10_out{s}") for s in range(2)]
        lg10_done = sem("lg10_done")
        lg10_read = sem("lg10_read")

        def sp_router10(sp):
            sp.dma_start(W_R10, a["w_r10"]).then_inc(w10_in, 16)
            sp.dma_start(b_r10, a["b_r10"].to_broadcast((P, E10))).then_inc(w10_in, 16)
            sp.dma_start(W_E1, a["w_e1"]).then_inc(wx10_in, 16)
            sp.dma_start(W_E2[0:HID + 1], a["w_e2"]).then_inc(wx10_in, 16)
            sp.dma_start(b_e1.rearrange("p e m -> p (e m)"), a["b_e1"].to_broadcast((P, E10 * HID))).then_inc(wx10_in, 16)
            with sp.Fori(0, B // 2) as pair:
                for s in range(2):
                    b = pair * 2 + s
                    sp.wait_ge(f10.z_ready, b + 1)
                    sp.dma_start(z_dram[bass.ds(b * S, S), :].rearrange("(t p) d -> p t d", p=P), f10.z[:, s]).then_inc(z10_out[s], 16)
            for s in range(2):
                sp.wait_ge(z10_out[s], 16 * (B // 2))

        def pool_router10(pool):
            def step(b, s, last):
                if not last:
                    f10.pool(pool, b + 1, 1 - s)
            batches(pool, lambda b, s: f10.pool(pool, b, s), step)

        def pe_router10(pe):
            pe.wait_ge(w10_in, 32)

            def step(b, s, last):
                pe.wait_ge(f10.zT_ready, b + 1)
                pe.wait_ge(lg10_read, b)
                for t in range(TT):
                    for k in range(KC):
                        mm = pe.matmul(ps[:, 5, t * E10:(t + 1) * E10], f10.zT[:, s, k, t * P:(t + 1) * P], W_R10[:, k, :],
                                       start=(k == 0), stop=(k == KC - 1))
                mm.then_inc(lg10_done, 1)
                if not last:
                    f10.pe(pe, b + 1, 1 - s)
            batches(pe, lambda b, s: f10.pe(pe, b, s), step)

        def act_router10(act):
            def step(b, s, last):
                if not last:
                    f10.act(act, b + 1, 1 - s, lambda: act.wait_ge(lg10_done, b))
            batches(act, lambda b, s: f10.act(act, b, s, lambda: None), step)

        def dve_router10(dve):
            dve.wait_ge(w10_in, 32)

            def step(b, s, last):
                if not last:
                    def slot_free():
                        dve.wait_ge(f10.turned, b)
                        dve.wait_ge(z10_out[1 - s], b * 8 if s == 0 else (b - 1) * 8 + 16)
                    f10.dve(dve, b + 1, 1 - s, slot_free)
                dve.wait_ge(lg10_done, b + 1)
                dve.tensor_tensor(d10.logits[:, bass.ds(b * TT, TT), :], ps[:, 5, 0:TT * E10].rearrange("p (t e) -> p t e", e=E10),
                                  b_r10.unsqueeze(1).to_broadcast((P, TT, E10)), ALU.add).then_inc(lg10_read, 1)
            batches(dve, lambda b, s: f10.dve(dve, b, s, lambda: None), step)

        free[0] = STAGE10
        d10.temps()
        best = take(NT)
        rev = take(E10)
        chosen10 = sem("chosen10")

        def sp_route10(sp):
            sp.wait_ge(wx10_in, 48)

        def act_route10(act):
            d10.act(act)

        def pe_route10(pe):
            d10.pe(pe, chosen10, 1)

        def dve_route10(dve):
            link = lambda ins: d10.link(dve, ins)
            wide = d10.wide[:, 0:NT * E10].rearrange("p (t e) -> p t e", e=E10)
            link(dve.tensor_reduce(best, d10.logits, AX.X, ALU.max))
            link(dve.tensor_tensor(wide, d10.logits, best.unsqueeze(2).to_broadcast((P, NT, E10)), ALU.is_equal))
            link(dve.tensor_scalar(rev, count[:, 0:E10], -1.0, float(E10), ALU.mult, ALU.add))
            link(dve.tensor_tensor(wide, wide, rev.unsqueeze(1).to_broadcast((P, NT, E10)), ALU.mult))
            link(dve.tensor_reduce(best, wide, AX.X, ALU.max))
            dve.tensor_tensor(d10.chosen, rev.unsqueeze(1).to_broadcast((P, NT, E10)), best.unsqueeze(2).to_broadcast((P, NT, E10)),
                              ALU.is_equal).then_inc(chosen10, 1)
            d10.dve(dve)

        free[0] = STAGE10
        g12 = Gather("top", d10, z_dram)
        h12 = take(4 * 2 * HID).rearrange("p (s n i) -> p s n i", s=4, n=2)
        hT12 = take(4 * 2 * P).rearrange("p (s n t) -> p s n t", s=4, n=2)
        y12 = take(4 * 2 * D).rearrange("p (s n d) -> p s n d", s=4, n=2)
        e1_done = sem("e1_done")
        h12_ready = sem("h12_ready")
        h12_turned = sem("h12_turned")
        hT12_ready = sem("hT12_ready")
        e2_done = sem("e2_done")
        y12_ready = sem("y12_ready")
        y12_out = [sem(f"y12_out{s}") for s in range(4)]
        ones12 = sem("ones12")
        STEPS12 = d10.N // 2

        def sp_experts12(sp):
            store_rows(sp, STEPS12, y12_ready, y12, y12_out)

        def pool_experts12(pool):
            pool.memset(hT12[HID:HID + 1], 1.0).then_inc(ones12, 1)
            pool.wait_ge(ones12, 1)
            g12.pool(pool)

        def pe_experts12(pe):
            pe.sem_inc(g12.turned, 4)
            pe.sem_inc(e1_done, 4)
            pe.sem_inc(e2_done, 4)
            pe.wait_ge(ones12, 1)

            def step(i, s, there):
                if there(i - 1):
                    up = [expert_of(pe, d10, (i - 1) * 2 + n, E10 - 1) for n in range(2)]
                if there(i - 3):
                    down = [expert_of(pe, d10, (i - 3) * 2 + n, E10 - 1) for n in range(2)]
                if there(i):
                    g12.pe(pe, i, s)
                if there(i - 1):
                    c = (s - 1) % 4
                    pe.wait_ge(g12.ready, i + 2)
                    pe.wait_ge(h12_ready, i)
                    for n in range(2):
                        for k in range(KC):
                            mm = pe.matmul(ps[:, 2 + c % 2, n * HID:(n + 1) * HID], g12.xT[:, c, n, k, :],
                                           W_E1[:, k, bass.ds(up[n], 1), :].rearrange("p a m -> p (a m)"), start=(k == 0), stop=(k == KC - 1))
                    mm.then_inc(e1_done, 1)
                if there(i - 2):
                    c = (s - 2) % 4
                    pe.wait_ge(h12_ready, i - 1 + 2)
                    pe.wait_ge(hT12_ready, i - 1)
                    alone(pe)
                    for n in range(2):
                        mm = pe.transpose(ps[0:HID, 4 + c % 2, n * P:(n + 1) * P], h12[:, c, n, :], ident)
                    mm.then_inc(h12_turned, 1)
                if there(i - 3):
                    c = (s - 3) % 4
                    pe.wait_ge(hT12_ready, i - 2 + 2)
                    pe.wait_ge(y12_ready, i - 2)
                    for n in range(2):
                        mm = pe.matmul(ps[:, 6 + c % 2, n * D:(n + 1) * D], hT12[0:HID + 1, c, n, :],
                                       W_E2[0:HID + 1, bass.ds(down[n], 1), :].rearrange("p a d -> p (a d)"), start=True, stop=True)
                    mm.then_inc(e2_done, 1)
            blocks(pe, STEPS12, step)

        def act_experts12(act):
            act.sem_inc(g12.ready, 2)
            act.sem_inc(hT12_ready, 2)

            def step(i, s, there):
                if there(i):
                    g12.act(act, i, s, e1_done, i + 1)
                if there(i - 2):
                    c = (s - 2) % 4
                    act.wait_ge(h12_turned, i - 1 + 4)
                    act.wait_ge(e2_done, i - 1)
                    act.activation(hT12[0:HID, c].rearrange("p n t -> p (n t)"), ps[0:HID, 4 + c % 2, 0:2 * P], ACT.Relu).then_inc(hT12_ready, 1)
            blocks(act, STEPS12, step)

        def dve_experts12(dve):
            for x in (h12_ready, y12_ready):
                dve.sem_inc(x, 2)
            dve.sem_inc(h12_turned, 4)

            def step(i, s, there):
                if there(i - 1):
                    c = (s - 1) % 4
                    bias = [expert_of(dve, d10, (i - 1) * 2 + n, E10 - 1) for n in range(2)]
                    dve.wait_ge(e1_done, i + 4)
                    dve.wait_ge(h12_turned, i)
                    for n in range(2):
                        ins = dve.tensor_tensor(h12[:, c, n, :], ps[:, 2 + c % 2, n * HID:(n + 1) * HID],
                                                b_e1[:, bass.ds(bias[n], 1), :].rearrange("p a m -> p (a m)"), ALU.add)
                    ins.then_inc(h12_ready, 1)
                if there(i - 3):
                    c = (s - 3) % 4
                    dve.wait_ge(e2_done, i - 2 + 4)
                    dve.wait_ge(y12_out[c], (i - 3 - c) * 4)
                    dve.tensor_scalar(y12[:, c].rearrange("p n d -> p (n d)"), ps[:, 6 + c % 2, :], 0.0, None, ALU.max).then_inc(y12_ready, 1)
            blocks(dve, STEPS12, step)

        free[0] = STAGE10
        SLOTS13 = 8
        back13, sum13 = (take(SLOTS13 * D).rearrange("p (s d) -> p s d", s=SLOTS13) for _ in range(2))
        at13 = take(SLOTS13, I32)
        at13_ready = sem("at13_ready")
        back13_in = [sem(f"back13_in{s}") for s in range(SLOTS13)]
        sum13_ready = sem("sum13_ready")
        stored = [sem(f"stored{s}") for s in range(SLOTS13 // 2)]

        def pool_output(pool):
            with pool.Fori(0, NT // SLOTS13) as turn:
                for s in range(SLOTS13):
                    pool.wait_ge(back13_in[s], turn * 16)
                pool.tensor_copy(at13, d10.sloti[:, bass.ds(turn * SLOTS13, SLOTS13), :].rearrange("p a k -> p (a k)")).then_inc(at13_ready, 1)
                pool.wait_ge(at13_ready, turn + 1)
                for s in range(SLOTS13):
                    pool.wait_ge(sum13_ready, turn * SLOTS13 + s + 1)
                    alone(pool)
                    pool.indirect_dma_start(out=back13[:, s, :], out_offset=None, in_=y_dram,
                                            in_offset=bass.IndirectOffsetOnAxis(ap=at13[:, s:s + 1].bitcast(U32), axis=0)
                                            ).then_inc(back13_in[s], 16)

        def dve_output(dve):
            dve.sem_inc(sum13_ready, SLOTS13)
            with dve.Fori(0, NT // SLOTS13) as turn:
                for s in range(SLOTS13):
                    dve.wait_ge(back13_in[s], turn * 16 + 16)
                    dve.wait_ge(stored[s // 2], turn * 16)
                    dve.tensor_tensor(sum13[:, s, :], back13[:, s, :], H[:, bass.ds(turn * SLOTS13 + s, 1), :].rearrange("p a d -> p (a d)"),
                                      ALU.add).then_inc(sum13_ready, 1)

        def sp_output(sp):
            with sp.Fori(0, NT // SLOTS13) as turn:
                for s in range(0, SLOTS13, 2):
                    t = turn * SLOTS13 + s
                    sp.wait_ge(sum13_ready, t + 2 + SLOTS13)
                    sp.dma_start(out[bass.ds(t * P, 2 * P), :].rearrange("(n p) d -> p n d", p=P), sum13[:, s:s + 2, :]).then_inc(stored[s // 2], 16)
            for x in stored:
                sp.wait_ge(x, 16 * (NT // SLOTS13))

        stages = [(sp_linear, pool_linear, act_linear, dve_linear, pe_linear),
                  (sp_router10, pool_router10, act_router10, dve_router10, pe_router10),
                  (sp_route10, nothing, act_route10, dve_route10, pe_route10),
                  (sp_experts12, pool_experts12, act_experts12, dve_experts12, pe_experts12),
                  (sp_output, pool_output, nothing, dve_output, nothing)][:max(0, stop - 7)]
        if a.get("dbg"):
            dbg_out = sem("dbg_out")

            def sp_dbg(sp):
                sp.dma_start(a["dbg"]["H"].rearrange("(t p) d -> p t d", p=P), H).then_inc(dbg_out, 16)
                sp.wait_ge(dbg_out, 16)
            stages.append((sp_dbg, nothing, nothing, nothing, nothing))
        run(stages)


def laid_out(x):
    f = {k: np.asarray(v) for k, v in x.items()}

    def rows(w):
        return np.ascontiguousarray(w.reshape(w.shape[0] // P, P, -1).transpose(1, 0, 2))

    def cols(v):
        return np.ascontiguousarray(v.reshape(-1, P).T)

    at = np.arange(S, dtype=np.float32)[:, None]
    even = np.arange(0, D, 2, dtype=np.float32)[None, :]
    angle = at / np.power(np.float32(10000.0), np.float32(2.0) * even / np.float32(D))
    pe = np.zeros((S, D), np.float32)
    pe[:, 0::2], pe[:, 1::2] = np.sin(angle), np.cos(angle)

    w_in, b_in = f["L0_tok_in_proj_w"], f["L0_tok_in_proj_b"]
    o = {
        "x": np.ascontiguousarray(f["x"].reshape(NT, P).T),
        "emb": f["L0_tok_emb"],
        "pos": rows(pe),
        "ident": np.eye(P, dtype=np.float32),
        "w_qk": rows(w_in[:2 * D].T),
        "w_v": rows(w_in[2 * D:].T),
        "b_qk": cols(b_in[:2 * D]),
        "b_v": b_in[None, 2 * D:],
        "b_o": f["L0_tok_out_proj_b"][None],
    }
    o["w_o"] = rows(f["L0_tok_out_proj_w"].T)
    o["w_1"], o["w_2"], o["b_1"] = rows(f["L0_tok_w1"].T), rows(f["L0_tok_w2"].T), cols(f["L0_tok_b1"])
    o["norms"] = np.concatenate([f["L0_tok_" + n] for n in ("g1", "beta1", "b2", "g2", "beta2")])[None]
    o["w_kvr"] = np.stack([rows(f["L0_attn_W" + n].T) for n in "kvr"], 1)
    o["w_wo"] = rows(f["L0_attn_Wo"].T)
    o["vecs"] = np.stack([cols(f["L0_attn_" + n].reshape(-1)) for n in ("time_mix_k", "time_mix_v", "time_mix_r", "w", "u")], 1)
    gu = np.concatenate([f["L0_ffn_gate_w"], f["L0_ffn_up_w"]], 1)
    o["w_gu"] = np.ascontiguousarray(gu.reshape(16, 256, KC, P).transpose(3, 2, 0, 1))
    o["w_d"] = np.ascontiguousarray(f["L0_ffn_down_w"].transpose(2, 0, 1))
    o["w_r"] = rows(f["L0_ffn_router_weight"].T)
    o["e_bias"] = f["L0_ffn_e_bias"][None]
    for n, w in (("w_sg", "gate"), ("w_su", "up"), ("w_sd", "down")):
        o[n] = rows(f[f"L0_ffn_sh_{w}_w"].T)
    tile = np.arange(NT, dtype=np.float32)
    o["consts"] = np.concatenate([np.tile((tile > 0).astype(np.float32), 32), P * tile, np.ones(32, np.float32),
                                  np.arange(160, dtype=np.float32), tile])[None]
    o["before"] = np.triu(np.ones((P, P), np.float32), 1)
    o["row_of"] = np.arange(P, dtype=np.float32)[:, None]
    head = np.arange(P) // HD
    o["w_qkv"], o["w_out"] = rows(f["L1_attn_W_qkv"]), rows(f["L1_attn_W_out"])
    o["qk_gain"] = np.concatenate([f["L1_attn_qn_w"], f["L1_attn_kn_w"]])[None]
    o["b_out"] = f["L1_attn_b_out"][None]
    o["same_head"] = (head[:, None] == head[None, :]).astype(np.float32)
    o["head_of"] = (head[:, None] == np.arange(P // HD)[None, :]).astype(np.float32)
    o["w_r10"], o["b_r10"] = rows(f["L1_ffn_router_w"].T), f["L1_ffn_router_b"][None]
    o["w_e1"] = np.ascontiguousarray(f["L1_ffn_weights1"].reshape(32, KC, P, 64).transpose(2, 1, 0, 3))
    o["w_e2"] = np.ascontiguousarray(np.concatenate([f["L1_ffn_weights2"], f["L1_ffn_bias2"][:, None, :]], 1).transpose(1, 0, 2))
    o["b_e1"] = f["L1_ffn_bias1"].reshape(1, -1)
    return {k: np.ascontiguousarray(v) for k, v in o.items()}


def kernel(**inputs):
    import concourse.bacc as bacc
    from concourse.bass_utils import run_bass_kernel_spmd

    nc = bacc.Bacc("TRN2", target_bir_lowering=False, num_devices=1)
    arrays = laid_out(inputs)
    aps = {k: nc.dram_tensor(f"in_{k}", v.shape, mybir.dt.from_np(v.dtype), kind="ExternalInput").ap()
           for k, v in arrays.items()}
    out = nc.dram_tensor("out", (B * S, D), F32, kind="ExternalOutput").ap()
    build(nc, aps, out)
    r = run_bass_kernel_spmd(nc, [{f"in_{k}": v for k, v in arrays.items()}], core_ids=[0])
    return r.results[0]["out"].reshape(B, S, D)
```
